# Optimizing a Trainium2 kernel written in Bass

```python
import numpy as np
import jax
import jax.numpy as jnp

def _softmax(x, axis=-1):
    return jax.nn.softmax(x, axis=axis)

def _gelu(x):
    return jax.nn.gelu(x, approximate=True)

def _silu(x):
    return jax.nn.silu(x)

def _sigmoid(x):
    return jax.nn.sigmoid(x)

def _layernorm(x, axis=-1, eps=1e-05):
    m = jnp.mean(x, axis=axis, keepdims=True)
    v = jnp.var(x, axis=axis, keepdims=True)
    return (x - m) / jnp.sqrt(v + eps)

def _scatter_add(tgt, idx, src, axis=0):
    return tgt.at[idx].add(src)

def _segment_sum(src, seg, n):
    return jax.ops.segment_sum(src, seg, n)
kernel_name = 'mk_gnn_resnorm_d4_gnn_r32_b4bd69'

def setup_inputs(seed: int=0):
    np.random.seed(seed)
    _w = jnp.asarray

    def _rec_inputs():
        import jax
        import jax.numpy as jnp
        _gk = jax.random.key(seed)
        x = -0.000202 + 1 * jax.random.normal(jax.random.fold_in(_gk, 1), (50000, 128), jnp.float32)
        src = jax.random.randint(jax.random.fold_in(_gk, 2), (50000,), 0, 50000, jnp.int32)
        dst = jax.random.randint(jax.random.fold_in(_gk, 3), (50000,), 0, 50000, jnp.int32)
        _o = jnp.argsort(dst, stable=True)
        src = src[_o]
        dst = dst[_o]
        edge_attr_128 = 7.68618e-05 + 1.00005 * jax.random.normal(jax.random.fold_in(_gk, 11), (50000, 128), jnp.float32)
        edge_weight1 = -0.00126848 + 0.999356 * jax.random.normal(jax.random.fold_in(_gk, 13), (50000, 1), jnp.float32)
        return (x, src, dst, edge_attr_128, edge_weight1)
    x, src, dst, edge_attr_128, edge_weight1 = _rec_inputs()

    def _L0_gnn_setup():
        import jax, jax.numpy as jnp
        import numpy as np
        LN_EPS = 1e-05
        key = jax.random.key(seed)
        k1, k2, k3 = jax.random.split(key, 3)
        N, E, D_IN, D_OUT = (50000, 15625, 128, 128)
        x = jax.random.normal(k1, (N, D_IN), dtype=jnp.float32)
        edge_index = jax.random.randint(k2, (2, E), 0, N, dtype=jnp.int64)
        W = jax.random.normal(k3, (D_IN, D_OUT), dtype=jnp.float32) * (1.0 / np.sqrt(D_IN))
        b = jnp.zeros((D_OUT,), dtype=jnp.float32)
        ln_gamma = jnp.ones((D_OUT,), dtype=jnp.float32)
        ln_beta = jnp.zeros((D_OUT,), dtype=jnp.float32)
        return {'x': x, 'edge_index': edge_index, 'W': W, 'b': b, 'ln_gamma': ln_gamma, 'ln_beta': ln_beta}
    _L0_gnn_all = _L0_gnn_setup()
    _L0_gnn_in = {k: v for k, v in _L0_gnn_all.items() if k in ('W', 'b', 'ln_gamma', 'ln_beta')}
    del _L0_gnn_all

    def _L1_gnn_setup():
        import jax, jax.numpy as jnp
        import numpy as np
        HID, HEADS, LAYERS, EDIM = (128, 2, 3, 1)
        HEAD_DIM = HID
        N_NODES, N_EDGES = (50000, 15625)
        LN_EPS = 1e-05

        def _layer_norm(x, g, b):
            mu = x.mean(-1, keepdims=True)
            var = ((x - mu) ** 2).mean(-1, keepdims=True)
            return (x - mu) * jax.lax.rsqrt(var + LN_EPS) * g + b

        def _transformer_conv(x, src, tgt, edge_attr, Wq, bq, Wk, bk, Wv, bv, We, Wskip, bskip):
            N = x.shape[0]
            E = src.shape[0]
            q = (x @ Wq + bq).reshape(N, HEADS, HEAD_DIM)
            k = (x @ Wk + bk).reshape(N, HEADS, HEAD_DIM)
            v = (x @ Wv + bv).reshape(N, HEADS, HEAD_DIM)
            e = (edge_attr @ We).reshape(E, HEADS, HEAD_DIM)
            k_j = k[src] + e
            q_i = q[tgt]
            alpha = (q_i * k_j).sum(-1) / jnp.sqrt(jnp.asarray(HEAD_DIM, x.dtype))
            m = jax.ops.segment_max(alpha, tgt, num_segments=N)
            a = jnp.exp(alpha - m[tgt])
            denom = jax.ops.segment_sum(a, tgt, num_segments=N)
            a = a / jnp.where(denom[tgt] > 0, denom[tgt], 1.0)
            msg = (v[src] + e) * a[..., None]
            out = jax.ops.segment_sum(msg, tgt, num_segments=N)
            out = out.mean(axis=1)
            return out + x @ Wskip + bskip
        key = jax.random.key(seed)
        ks = jax.random.split(key, 12)
        HC = HEADS * HEAD_DIM
        s = 1.0 / np.sqrt(HID)
        inp = {'x': jax.random.normal(ks[0], (N_NODES, HID), jnp.float32), 'edge_index': jax.random.randint(ks[1], (2, N_EDGES), 0, N_NODES, jnp.int64), 'edge_attr': jax.random.normal(ks[2], (N_EDGES, EDIM), jnp.float32), 'ln_in_g': jnp.ones((HID,), jnp.float32), 'ln_in_b': jnp.zeros((HID,), jnp.float32), 'Wq': jax.random.normal(ks[3], (LAYERS, HID, HC), jnp.float32) * s, 'bq': jnp.zeros((LAYERS, HC), jnp.float32), 'Wk': jax.random.normal(ks[4], (LAYERS, HID, HC), jnp.float32) * s, 'bk': jnp.zeros((LAYERS, HC), jnp.float32), 'Wv': jax.random.normal(ks[5], (LAYERS, HID, HC), jnp.float32) * s, 'bv': jnp.zeros((LAYERS, HC), jnp.float32), 'We': jax.random.normal(ks[6], (LAYERS, EDIM, HC), jnp.float32), 'Wskip': jax.random.normal(ks[7], (LAYERS, HID, HID), jnp.float32) * s, 'bskip': jnp.zeros((LAYERS, HID), jnp.float32), 'ln_g': jnp.ones((LAYERS, HID), jnp.float32), 'ln_b': jnp.zeros((LAYERS, HID), jnp.float32)}
        return inp
    _L1_gnn_all = _L1_gnn_setup()
    _L1_gnn_in = {k: v for k, v in _L1_gnn_all.items() if k in ('ln_in_g', 'ln_in_b', 'Wq', 'bq', 'Wk', 'bk', 'Wv', 'bv', 'We', 'Wskip', 'bskip', 'ln_g', 'ln_b')}
    del _L1_gnn_all

    def _L2_gnn_setup():
        import jax, jax.numpy as jnp
        import numpy as np
        N_NODES = 3125
        N_EDGES = 50000
        F_IN = 128
        HID = 128
        BN_EPS = 1e-05
        NORM_EPS = 1e-12
        key = jax.random.key(seed)
        ks = jax.random.split(key, 5)
        x = jax.random.normal(ks[0], (N_NODES, F_IN), dtype=jnp.float32)
        edge_index = jax.random.randint(ks[1], (2, N_EDGES), 0, N_NODES, dtype=jnp.int64)
        adj_norm_sp = jnp.zeros((1,), dtype=jnp.float32)
        s = 1.0 / np.sqrt(F_IN)
        W_l = jax.random.uniform(ks[2], (HID, F_IN), jnp.float32, -s, s)
        b_l = jnp.zeros((HID,), dtype=jnp.float32)
        W_r = jax.random.uniform(ks[3], (HID, F_IN), jnp.float32, -s, s)
        gamma = jnp.ones((HID,), dtype=jnp.float32)
        beta = jnp.zeros((HID,), dtype=jnp.float32)
        return {'x': x, 'edge_index': edge_index, 'adj_norm_sp': adj_norm_sp, 'W_l': W_l, 'b_l': b_l, 'W_r': W_r, 'gamma': gamma, 'beta': beta}
    _L2_gnn_all = _L2_gnn_setup()
    _L2_gnn_in = {k: v for k, v in _L2_gnn_all.items() if k in ('adj_norm_sp', 'W_l', 'b_l', 'W_r', 'gamma', 'beta')}
    del _L2_gnn_all

    def _L3_gnn_setup():
        import jax, jax.numpy as jnp
        import numpy as np
        HIDDEN = 128
        HEADS = 8
        HEAD_DIM = HIDDEN // HEADS
        N_NODES = 50000
        N_EDGES = 15625
        key = jax.random.key(seed)
        ks = jax.random.split(key, 12)
        s = 1.0 / np.sqrt(HIDDEN)
        inp = {'edge_state': jax.random.normal(ks[0], (N_NODES, HIDDEN), jnp.float32), 'lg_edge_index': jax.random.randint(ks[1], (2, N_EDGES), 0, N_NODES, jnp.int64), 'angle_emb': jax.random.normal(ks[2], (N_EDGES, HIDDEN), jnp.float32), 'Wq': jax.random.normal(ks[3], (HIDDEN, HIDDEN), jnp.float32) * s, 'bq': jnp.zeros((HIDDEN,), jnp.float32), 'Wk': jax.random.normal(ks[4], (HIDDEN, HIDDEN), jnp.float32) * s, 'bk': jnp.zeros((HIDDEN,), jnp.float32), 'Wv': jax.random.normal(ks[5], (HIDDEN, HIDDEN), jnp.float32) * s, 'bv': jnp.zeros((HIDDEN,), jnp.float32), 'We': jax.random.normal(ks[6], (HIDDEN, HIDDEN), jnp.float32) * s, 'Wskip': jax.random.normal(ks[7], (HIDDEN, HIDDEN), jnp.float32) * s, 'bskip': jnp.zeros((HIDDEN,), jnp.float32), 'Wbeta': jax.random.normal(ks[8], (3 * HIDDEN, 1), jnp.float32) * s, 'ln_gamma': jnp.ones((HIDDEN,), jnp.float32), 'ln_beta': jnp.zeros((HIDDEN,), jnp.float32)}
        return inp
    _L3_gnn_all = _L3_gnn_setup()
    _L3_gnn_in = {k: v for k, v in _L3_gnn_all.items() if k in ('Wq', 'bq', 'Wk', 'bk', 'Wv', 'bv', 'We', 'Wskip', 'bskip', 'Wbeta', 'ln_gamma', 'ln_beta')}
    del _L3_gnn_all
    return {'x': x, 'src': src, 'dst': dst, 'edge_attr_128': edge_attr_128, 'edge_weight1': edge_weight1, 'L0_gnn_W': _L0_gnn_in['W'], 'L0_gnn_b': _L0_gnn_in['b'], 'L0_gnn_ln_gamma': _L0_gnn_in['ln_gamma'], 'L0_gnn_ln_beta': _L0_gnn_in['ln_beta'], 'L1_gnn_ln_in_g': _L1_gnn_in['ln_in_g'], 'L1_gnn_ln_in_b': _L1_gnn_in['ln_in_b'], 'L1_gnn_Wq': _L1_gnn_in['Wq'], 'L1_gnn_bq': _L1_gnn_in['bq'], 'L1_gnn_Wk': _L1_gnn_in['Wk'], 'L1_gnn_bk': _L1_gnn_in['bk'], 'L1_gnn_Wv': _L1_gnn_in['Wv'], 'L1_gnn_bv': _L1_gnn_in['bv'], 'L1_gnn_We': _L1_gnn_in['We'], 'L1_gnn_Wskip': _L1_gnn_in['Wskip'], 'L1_gnn_bskip': _L1_gnn_in['bskip'], 'L1_gnn_ln_g': _L1_gnn_in['ln_g'], 'L1_gnn_ln_b': _L1_gnn_in['ln_b'], 'L2_gnn_adj_norm_sp': _L2_gnn_in['adj_norm_sp'], 'L2_gnn_W_l': _L2_gnn_in['W_l'], 'L2_gnn_b_l': _L2_gnn_in['b_l'], 'L2_gnn_W_r': _L2_gnn_in['W_r'], 'L2_gnn_gamma': _L2_gnn_in['gamma'], 'L2_gnn_beta': _L2_gnn_in['beta'], 'L3_gnn_Wq': _L3_gnn_in['Wq'], 'L3_gnn_bq': _L3_gnn_in['bq'], 'L3_gnn_Wk': _L3_gnn_in['Wk'], 'L3_gnn_bk': _L3_gnn_in['bk'], 'L3_gnn_Wv': _L3_gnn_in['Wv'], 'L3_gnn_bv': _L3_gnn_in['bv'], 'L3_gnn_We': _L3_gnn_in['We'], 'L3_gnn_Wskip': _L3_gnn_in['Wskip'], 'L3_gnn_bskip': _L3_gnn_in['bskip'], 'L3_gnn_Wbeta': _L3_gnn_in['Wbeta'], 'L3_gnn_ln_gamma': _L3_gnn_in['ln_gamma'], 'L3_gnn_ln_beta': _L3_gnn_in['ln_beta']}

def reference(x, src, dst, edge_attr_128, edge_weight1, L0_gnn_W, L0_gnn_b, L0_gnn_ln_gamma, L0_gnn_ln_beta, L1_gnn_ln_in_g, L1_gnn_ln_in_b, L1_gnn_Wq, L1_gnn_bq, L1_gnn_Wk, L1_gnn_bk, L1_gnn_Wv, L1_gnn_bv, L1_gnn_We, L1_gnn_Wskip, L1_gnn_bskip, L1_gnn_ln_g, L1_gnn_ln_b, L2_gnn_adj_norm_sp, L2_gnn_W_l, L2_gnn_b_l, L2_gnn_W_r, L2_gnn_gamma, L2_gnn_beta, L3_gnn_Wq, L3_gnn_bq, L3_gnn_Wk, L3_gnn_bk, L3_gnn_Wv, L3_gnn_bv, L3_gnn_We, L3_gnn_Wskip, L3_gnn_bskip, L3_gnn_Wbeta, L3_gnn_ln_gamma, L3_gnn_ln_beta):
    import jax
    import jax.numpy as jnp

    def _L0_gnn_ref(x, edge_index, W, b, ln_gamma, ln_beta):
        import jax, jax.numpy as jnp
        import numpy as np
        LN_EPS = 1e-05
        N = x.shape[0]
        h = x @ W
        loops = jnp.arange(N, dtype=edge_index.dtype)
        src = jnp.concatenate([edge_index[0], loops])
        dst = jnp.concatenate([edge_index[1], loops])
        deg = jax.ops.segment_sum(jnp.ones(src.shape, dtype=h.dtype), dst, num_segments=N)
        dinv = jnp.where(deg > 0, jax.lax.rsqrt(deg), 0.0)
        norm = dinv[src] * dinv[dst]
        msgs = h[src] * norm[:, None]
        out = jax.ops.segment_sum(msgs, dst, num_segments=N) + b
        mu = out.mean(axis=-1, keepdims=True)
        var = out.var(axis=-1, keepdims=True)
        out = (out - mu) * jax.lax.rsqrt(var + LN_EPS) * ln_gamma + ln_beta
        return jax.nn.relu(out)

    def _L1_gnn_ref(x, edge_index, edge_attr, ln_in_g, ln_in_b, Wq, bq, Wk, bk, Wv, bv, We, Wskip, bskip, ln_g, ln_b):
        import jax, jax.numpy as jnp
        import numpy as np
        HID, HEADS, LAYERS, EDIM = (128, 2, 3, 1)
        HEAD_DIM = HID
        N_NODES, N_EDGES = (50000, 15625)
        LN_EPS = 1e-05

        def _layer_norm(x, g, b):
            mu = x.mean(-1, keepdims=True)
            var = ((x - mu) ** 2).mean(-1, keepdims=True)
            return (x - mu) * jax.lax.rsqrt(var + LN_EPS) * g + b

        def _transformer_conv(x, src, tgt, edge_attr, Wq, bq, Wk, bk, Wv, bv, We, Wskip, bskip):
            N = x.shape[0]
            E = src.shape[0]
            q = (x @ Wq + bq).reshape(N, HEADS, HEAD_DIM)
            k = (x @ Wk + bk).reshape(N, HEADS, HEAD_DIM)
            v = (x @ Wv + bv).reshape(N, HEADS, HEAD_DIM)
            e = (edge_attr @ We).reshape(E, HEADS, HEAD_DIM)
            k_j = k[src] + e
            q_i = q[tgt]
            alpha = (q_i * k_j).sum(-1) / jnp.sqrt(jnp.asarray(HEAD_DIM, x.dtype))
            m = jax.ops.segment_max(alpha, tgt, num_segments=N)
            a = jnp.exp(alpha - m[tgt])
            denom = jax.ops.segment_sum(a, tgt, num_segments=N)
            a = a / jnp.where(denom[tgt] > 0, denom[tgt], 1.0)
            msg = (v[src] + e) * a[..., None]
            out = jax.ops.segment_sum(msg, tgt, num_segments=N)
            out = out.mean(axis=1)
            return out + x @ Wskip + bskip
        src, tgt = (edge_index[0], edge_index[1])
        x = _layer_norm(x, ln_in_g, ln_in_b)
        for l in range(LAYERS):
            h = _transformer_conv(x, src, tgt, edge_attr, Wq[l], bq[l], Wk[l], bk[l], Wv[l], bv[l], We[l], Wskip[l], bskip[l])
            h = jax.nn.elu(h)
            x = _layer_norm(x + h, ln_g[l], ln_b[l])
        return x

    def _L2_gnn_ref(x, edge_index, adj_norm_sp, W_l, b_l, W_r, gamma, beta):
        import jax, jax.numpy as jnp
        import numpy as np
        N_NODES = 3125
        N_EDGES = 50000
        F_IN = 128
        HID = 128
        BN_EPS = 1e-05
        NORM_EPS = 1e-12
        src, dst = (edge_index[0], edge_index[1])
        n = x.shape[0]
        agg = jax.ops.segment_sum(x[src], dst, num_segments=n)
        cnt = jax.ops.segment_sum(jnp.ones_like(dst, dtype=x.dtype), dst, num_segments=n)
        agg = agg / jnp.maximum(cnt, 1.0)[:, None]
        out = agg @ W_l.T + b_l + x @ W_r.T
        out = out / jnp.maximum(jnp.linalg.norm(out, axis=-1, keepdims=True), NORM_EPS)
        out = jax.nn.relu(out)
        mean = jnp.mean(out, axis=0)
        var = jnp.var(out, axis=0)
        out = (out - mean) * jax.lax.rsqrt(var + BN_EPS) * gamma + beta
        return out

    def _L3_gnn_ref(edge_state, lg_edge_index, angle_emb, Wq, bq, Wk, bk, Wv, bv, We, Wskip, bskip, Wbeta, ln_gamma, ln_beta):
        import jax, jax.numpy as jnp
        import numpy as np
        HIDDEN = 128
        HEADS = 8
        HEAD_DIM = HIDDEN // HEADS
        N_NODES = 50000
        N_EDGES = 15625
        N = edge_state.shape[0]
        H, D = (HEADS, HEAD_DIM)
        src = lg_edge_index[0]
        dst = lg_edge_index[1]
        q = (edge_state @ Wq + bq).reshape(N, H, D)
        k = (edge_state @ Wk + bk).reshape(N, H, D)
        v = (edge_state @ Wv + bv).reshape(N, H, D)
        e = (angle_emb @ We).reshape(-1, H, D)
        k_e = k[src] + e
        v_e = v[src] + e
        alpha = jnp.einsum('ehd,ehd->eh', q[dst], k_e) / jnp.sqrt(jnp.float32(D))
        m = jax.ops.segment_max(alpha, dst, num_segments=N)
        a = jnp.exp(alpha - m[dst])
        z = jax.ops.segment_sum(a, dst, num_segments=N)
        attn = a / z[dst]
        out = jax.ops.segment_sum(attn[:, :, None] * v_e, dst, num_segments=N)
        out = out.reshape(N, H * D)
        x_r = edge_state @ Wskip + bskip
        beta = jax.nn.sigmoid(jnp.concatenate([out, x_r, out - x_r], axis=-1) @ Wbeta)
        out = beta * x_r + (1.0 - beta) * out
        mu = jnp.mean(out, axis=-1, keepdims=True)
        var = jnp.mean(jnp.square(out - mu), axis=-1, keepdims=True)
        out = (out - mu) / jnp.sqrt(var + 1e-05) * ln_gamma + ln_beta
        return edge_state + jax.nn.relu(out)
    edge_index = jnp.stack([src, dst])
    x = _layernorm(x + _L0_gnn_ref(x, edge_index, L0_gnn_W, L0_gnn_b, L0_gnn_ln_gamma, L0_gnn_ln_beta), axis=-1)
    x = _layernorm(x + _L1_gnn_ref(x, edge_index, edge_weight1, L1_gnn_ln_in_g, L1_gnn_ln_in_b, L1_gnn_Wq, L1_gnn_bq, L1_gnn_Wk, L1_gnn_bk, L1_gnn_Wv, L1_gnn_bv, L1_gnn_We, L1_gnn_Wskip, L1_gnn_bskip, L1_gnn_ln_g, L1_gnn_ln_b), axis=-1)
    x = _layernorm(x + _L2_gnn_ref(x, edge_index, L2_gnn_adj_norm_sp, L2_gnn_W_l, L2_gnn_b_l, L2_gnn_W_r, L2_gnn_gamma, L2_gnn_beta), axis=-1)
    x = _layernorm(x + _L3_gnn_ref(x, edge_index, edge_attr_128, L3_gnn_Wq, L3_gnn_bq, L3_gnn_Wk, L3_gnn_bk, L3_gnn_Wv, L3_gnn_bv, L3_gnn_We, L3_gnn_Wskip, L3_gnn_bskip, L3_gnn_Wbeta, L3_gnn_ln_gamma, L3_gnn_ln_beta), axis=-1)
    return x

_drawn_inputs = setup_inputs


def setup_inputs(seed=0):
    import zlib

    import numpy as np

    out = dict(_drawn_inputs(seed))
    spreads = {'L0_gnn_b': (0.0, 0.1),
     'L0_gnn_ln_gamma': (1.0, 0.2),
     'L0_gnn_ln_beta': (0.0, 0.1),
     'L1_gnn_ln_in_g': (1.0, 0.2),
     'L1_gnn_ln_in_b': (0.0, 0.1),
     'L1_gnn_bq': (0.0, 0.434),
     'L1_gnn_bk': (0.0, 0.8),
     'L1_gnn_bv': (0.0, 0.1),
     'L1_gnn_bskip': (0.0, 0.1),
     'L1_gnn_ln_g': (1.0, 0.2),
     'L1_gnn_ln_b': (0.0, 0.1),
     'L2_gnn_b_l': (0.0, 0.1),
     'L2_gnn_gamma': (1.0, 0.2),
     'L2_gnn_beta': (0.0, 0.1),
     'L3_gnn_bq': (0.0, 0.8),
     'L3_gnn_bk': (0.0, 0.8),
     'L3_gnn_bv': (0.0, 0.594),
     'L3_gnn_bskip': (0.0, 0.1),
     'L3_gnn_ln_gamma': (1.0, 0.2),
     'L3_gnn_ln_beta': (0.0, 0.1)}
    factors = {}
    for name, (base, spread) in spreads.items():
        noise = np.random.default_rng([zlib.crc32(name.encode()), seed]).standard_normal(out[name].shape)
        drawn = base * np.exp(spread * noise) if base else spread * noise
        out[name] = jnp.asarray(drawn.astype(out[name].dtype))
    for name, factor in factors.items():
        out[name] = (out[name] * factor).astype(out[name].dtype)
    return out
```

```python
from contextlib import ExitStack

import concourse.bass as bass
import concourse.mybir as mybir
import numpy as np

F32 = mybir.dt.float32
BF16 = mybir.dt.bfloat16
I32 = mybir.dt.int32
ALU = mybir.AluOpType
ACT = mybir.ActivationFunctionType
AX = mybir.AxisListType

P = 128
D = 128
J = 7
U = 4
LAG = 2
JN = 14
UN = 2
GROUPS = [(0, 4), (4, 8), (8, 12), (12, 14)]
NG = len(GROUPS)
FAR = float(1 << 20)
LOW = -1.0e30
EPS = 1.0e-5

SRC, DST, PUT, SAME, END, WGT = range(6)
FIELDS = 6


def padded(n):
    return -(-n // (P * J * U)) * P * J * U


def turns(eng, n, body):
    body(0)
    if n > 2:
        with eng.Fori(1, n - 1) as t:
            body(t)
    if n > 1:
        body(n - 1)


def wait(eng, sem, value, passed=None):
    if isinstance(value, int) and value <= 0:
        return
    eng.wait_ge(sem, value)
    if passed is not None and not isinstance(value, int):
        eng.sem_inc(passed, 1)


class Chain:

    def __init__(self, eng, sem, per=0):
        self.eng, self.sem, self.per, self.base, self.n = eng, sem, per, 0, 0

    def at(self, chunk):
        self.base, self.n = chunk * self.per, 0

    def __call__(self, ins):
        self.n += 1
        ins.then_inc(self.sem, 1)
        self.eng.wait_ge(self.sem, self.base + self.n)

    def end(self):
        assert self.n == self.per, (self.n, self.per)


class Net:
    def __init__(self, nc, args, outs):
        self.nc = nc
        self.a = args
        self.out = outs
        self.NR = args["x"].shape[0]
        self.COLS = self.NR // P
        self.NB = self.COLS // J
        self.T = self.NB // U
        self.TN = self.COLS // (JN * UN)
        self.names = 0
        self.sems = []

    def semaphore(self, what):
        handle = self.nc.alloc_semaphore(self.name(what))
        self.sems.append(handle)
        return handle

    def end_phase(self):
        self.nc.clear_and_free_semaphores(self.sems)
        self.nc.all_engine_barrier()
        self.sems = []

    def name(self, what):
        self.names += 1
        return f"{what}_{self.names}"


def rows(table, j=JN):
    return table.rearrange("(p b j) d -> p b (j d)", p=P, j=j)


def wide(col, n):
    return col.to_broadcast([P, n])


def setup(k):
    nc, A = k.nc, k.a
    NB, COLS, T = k.NB, k.COLS, k.T
    with ExitStack() as c:
        sb = lambda n, s, d=F32: c.enter_context(nc.sbuf_tensor(k.name(n), s, d))
        sem = lambda n: k.semaphore(n)
        dst_i = sb("dst_i", [P, COLS], I32)
        nxt_i = sb("nxt_i", [P, COLS], I32)
        prv_i = sb("prv_i", [P, COLS], I32)
        src_i = sb("src_i", [P, COLS], I32)
        w_in = sb("w_in", [P, COLS])
        dst = sb("dst", [P, COLS])
        nxt = sb("nxt", [P, COLS])
        prv = sb("prv", [P, COLS])
        last = sb("last", [P, COLS])
        tmp = sb("tmp", [P, COLS])
        tmp_i = sb("tmp_i", [P, COLS], I32)
        hi = sb("hi", [P, COLS])
        lo = sb("lo", [P, COLS])
        rec = sb("rec", [P, NB, FIELDS, J], I32)
        zero = sb("zero", [P, JN * D])
        iota_i = sb("iota_i", [P, max(COLS, P)], I32)
        iota = sb("iota", [P, max(COLS, P)])
        upper = sb("upper", [P, P])
        lower = sb("lower", [P, P])
        any_end = sb("any_end", [P, 1])
        small = sb("small", [P, 4])
        hi1 = sb("hi1", [P, U, J, P], BF16)
        lo1 = sb("lo1", [P, U, J, COLS], BF16)
        hist = c.enter_context(nc.psum_tensor(k.name("hist"), [P, 512], F32))
        row_ps = c.enter_context(nc.psum_tensor(k.name("row_ps"), [P, 512], F32))
        loaded, zeroed, consts, made, stored = [sem(n) for n in ("loaded", "zeroed", "consts", "made", "stored")]
        zstored, hots, counted, rowed, done = [sem(n) for n in ("zstored", "hots", "counted", "rowed", "done")]
        split, pooled, degree, rooted = sem("split"), sem("pooled"), sem("degree"), sem("rooted")
        flat = lambda ap: ap.rearrange("(p c) -> p c", p=P)
        recf = rec[:].bitcast(F32)
        field = lambda r, f: r[:, :, f, :]
        col = lambda t: t[:].rearrange("p (b j) -> p b j", j=J)
        n_ext = k.NR
        with nc.Block() as b:

            @b.sync
            def _(sp):
                sp.dma_start(dst_i[:], flat(A["dst"][1 : 1 + n_ext])).then_inc(loaded, 16)
                sp.dma_start(nxt_i[:], flat(A["dst"][2 : 2 + n_ext])).then_inc(loaded, 16)
                sp.dma_start(prv_i[:], flat(A["dst"][0:n_ext])).then_inc(loaded, 16)
                sp.dma_start(src_i[:], flat(A["src"])).then_inc(loaded, 16)
                sp.dma_start(w_in[:], A["weight"].rearrange("(p c) o -> p (c o)", p=P)).then_inc(loaded, 16)
                sp.wait_ge(zeroed, 1)
                for i in range(COLS // JN):
                    sp.dma_start(rows(k.msg)[:, i, :], zero[:]).then_inc(zstored, 16)
                sp.wait_ge(made, 1)
                sp.dma_start(k.meta.rearrange("p b f j -> p (b f j)"),
                             rec[:].rearrange("p b f j -> p (b f j)")).then_inc(stored, 16)
                sp.wait_ge(stored, 16)
                sp.wait_ge(zstored, 16 * (COLS // JN))

            @b.gpsimd
            def _(pool):
                pool.memset(zero[:], 0.0).then_inc(zeroed, 1)
                pool.memset(k.ident[:], 0.0).then_inc(pooled, 1)
                pool.memset(k.ones[:], 1.0).then_inc(pooled, 1)
                pool.memset(k.root[:], -0.5).then_inc(pooled, 1)
                pool.memset(upper[:], 1.0).then_inc(pooled, 1)
                pool.memset(lower[:], 1.0).then_inc(pooled, 1)
                pool.wait_ge(pooled, 5)
                pool.affine_select(out=k.ident[:], in_=k.ident[:], compare_op=ALU.not_equal, fill=1.0, base=0,
                                   pattern=[[-1, P]], channel_multiplier=1).then_inc(consts, 1)
                pool.affine_select(out=upper[:], in_=upper[:], compare_op=ALU.is_gt, fill=0.0, base=0,
                                   pattern=[[1, P]], channel_multiplier=-1).then_inc(consts, 1)
                pool.affine_select(out=lower[:], in_=lower[:], compare_op=ALU.is_gt, fill=0.0, base=0,
                                   pattern=[[-1, P]], channel_multiplier=1).then_inc(consts, 1)
                pool.iota(iota_i[:], pattern=[[1, max(COLS, P)]], base=0, channel_multiplier=0).then_inc(consts, 1)
                pool.wait_ge(degree, 1)
                pool.tensor_tensor(k.dinv[:], k.dinv[:], wide(k.root[:], COLS), ALU.pow).then_inc(rooted, 1)
                pool.wait_ge(rooted, 1)

            @b.vector
            def _(dve):
                step = Chain(dve, done)
                dve.wait_ge(loaded, 80)
                step(dve.tensor_copy(dst[:], dst_i[:]))
                step(dve.tensor_copy(nxt[:], nxt_i[:]))
                step(dve.tensor_copy(prv[:], prv_i[:]))
                step(dve.tensor_tensor(last[:], dst[:], nxt[:], ALU.not_equal))
                step(dve.tensor_tensor(tmp[:], dst[:], last[:], ALU.mult))
                step(dve.tensor_scalar(hi[:], last[:], -FAR, FAR, ALU.mult, ALU.add))
                step(dve.tensor_tensor(tmp[:], tmp[:], hi[:], ALU.add))
                step(dve.tensor_copy(field(rec, PUT), col(tmp)))
                step(dve.tensor_copy(field(rec, SRC), col(src_i)))
                step(dve.tensor_copy(field(rec, DST), col(dst_i)))
                step(dve.tensor_copy(field(recf, WGT), col(w_in)))
                step(dve.tensor_tensor(tmp[:], dst[:], prv[:], ALU.is_equal))
                step(dve.memset(tmp[:, 0:1], 0.0))
                step(dve.tensor_copy(field(recf, SAME), col(tmp)))
                step(dve.tensor_scalar(tmp[:], dst[:], dst[:, 0:1], None, ALU.is_equal))
                step(dve.tensor_tensor(tmp[:], tmp[:], last[:], ALU.mult))
                step(dve.tensor_copy(field(recf, END), col(tmp)))
                step(dve.tensor_reduce(any_end[:], tmp[:], AX.X, ALU.add))
                dve.nop().then_inc(made, 1)
                step(dve.tensor_scalar(tmp_i[:], dst[:], 1.0 / COLS, None, ALU.mult))
                step(dve.tensor_copy(hi[:], tmp_i[:]))
                step(dve.scalar_tensor_tensor(lo[:], hi[:], -float(COLS), dst[:], ALU.mult, ALU.add))
                step(dve.tensor_scalar(tmp[:], lo[:], 0.0, None, ALU.is_lt))
                step(dve.tensor_tensor(hi[:], hi[:], tmp[:], ALU.subtract))
                step(dve.scalar_tensor_tensor(lo[:], tmp[:], float(COLS), lo[:], ALU.mult, ALU.add))
                step(dve.tensor_scalar(tmp[:], lo[:], float(COLS), None, ALU.is_ge))
                step(dve.tensor_tensor(hi[:], hi[:], tmp[:], ALU.add))
                step(dve.scalar_tensor_tensor(lo[:], tmp[:], -float(COLS), lo[:], ALU.mult, ALU.add))
                dve.wait_ge(consts, 4)
                step(dve.tensor_copy(iota[:], iota_i[:]))
                dve.nop().then_inc(split, 1)
                dve.wait_ge(rowed, 1)
                step(dve.tensor_scalar(k.join_t[:], row_ps[:, 0:P], dst[:, COLS - 1 : COLS], None, ALU.is_equal))
                step(dve.tensor_tensor(k.join_t[:], k.join_t[:], upper[:], ALU.mult))
                step(dve.tensor_scalar(k.join[:], row_ps[:, P : 2 * P], dst[:, 0:1], None, ALU.is_equal))
                step(dve.tensor_tensor(k.join[:], k.join[:], lower[:], ALU.mult))
                step(dve.tensor_scalar(k.no_join[:], k.join[:], -LOW, LOW, ALU.mult, ALU.add))
                step(dve.tensor_reduce(small[:, 0:1], k.join[:], AX.X, ALU.max))
                step(dve.tensor_tensor(small[:, 0:1], small[:, 0:1], any_end[:], ALU.mult))
                step(dve.tensor_tensor(small[:, 1:2], small[:, 0:1], dst[:, 0:1], ALU.mult))
                step(dve.tensor_scalar(small[:, 2:3], small[:, 0:1], -FAR, FAR, ALU.mult, ALU.add))
                step(dve.tensor_tensor(small[:, 1:2], small[:, 1:2], small[:, 2:3], ALU.add))
                step(dve.tensor_copy(k.join_row[:], small[:, 1:2]))
                hi3, lo3 = col(hi), col(lo)

                def body(t):
                    for u in range(U):
                        blk = t * U + u
                        wait(dve, counted, blk - U + 1)
                        for j in range(J):
                            dve.tensor_scalar(hi1[:, u, j, :], iota[:, 0:P], hi3[:, blk, j : j + 1], None, ALU.is_equal)
                            ins = dve.tensor_scalar(lo1[:, u, j, :], iota[:, 0:COLS], lo3[:, blk, j : j + 1], None, ALU.is_equal)
                        ins.then_inc(hots, 1)

                turns(dve, T, body)
                dve.wait_ge(counted, NB)
                h = hist[:, 0:COLS]
                step(dve.tensor_scalar(k.dinv[:], h, 1.0, None, ALU.add))
                dve.nop().then_inc(degree, 1)
                step(dve.tensor_scalar(tmp[:], h, 1.0, None, ALU.max))
                step(dve.reciprocal(k.rcnt[:], tmp[:]))

            @b.tensor
            def _(pe):
                pe.wait_ge(consts, 1)
                pe.wait_ge(split, 1)
                pe.transpose(row_ps[:, 0:P], wide(dst[:, 0:1], P), k.ident[:])
                pe.transpose(row_ps[:, P : 2 * P], wide(dst[:, COLS - 1 : COLS], P), k.ident[:]).then_inc(rowed, 1)

                def chunk(blk, u, first, final):
                    pe.wait_ge(hots, blk + 1)
                    for j in range(J):
                        ins = pe.matmul(hist[:, 0:COLS], hi1[:, u, j, :], lo1[:, u, j, :],
                                        start=first and j == 0, stop=final and j == J - 1)
                    ins.then_inc(counted, 1)

                def body(t):
                    for u in range(U):
                        blk = t * U + u
                        chunk(blk, u, isinstance(blk, int) and blk == 0, isinstance(blk, int) and blk == NB - 1)

                turns(pe, T, body)


def scale_pass(k):
    nc = k.nc
    with ExitStack() as c:
        xin = c.enter_context(nc.sbuf_tensor(k.name("xin"), [P, UN, JN, D], F32))
        xs = c.enter_context(nc.sbuf_tensor(k.name("xs"), [P, UN, JN, D], F32))
        loaded = [k.semaphore(f"loaded{u}") for u in range(UN)]
        stored = [k.semaphore(f"stored{u}") for u in range(UN)]
        scaled, passed = k.semaphore("scaled"), k.semaphore("passed")
        src, dst = rows(k.a["x"]), rows(k.tab[0])
        dinv = k.dinv[:].rearrange("p (b j) -> p b j", j=JN)
        with nc.Block() as b:

            @b.sync
            def _(sp):
                def body(t):
                    for u in range(UN):
                        wait(sp, scaled, t * UN + u - 1, passed)
                        sp.dma_start(xin[:, u].rearrange("p j d -> p (j d)"), src[:, t * UN + u, :]).then_inc(loaded[u], 16)

                turns(sp, k.TN, body)

            @b.vector
            def _(dve):
                def body(t):
                    for u in range(UN):
                        dve.wait_ge(loaded[u], (t + 1) * 16)
                        wait(dve, stored[u], t * 16)
                        dve.tensor_tensor(xs[:, u], xin[:, u], dinv[:, t * UN + u, :].unsqueeze(2).to_broadcast([P, JN, D]),
                                          ALU.mult).then_inc(scaled, 1)

                turns(dve, k.TN, body)

            @b.scalar
            def _(act):
                def body(t):
                    for u in range(UN):
                        act.wait_ge(scaled, t * UN + u + 1)
                        act.dma_start(dst[:, t * UN + u, :], xs[:, u].rearrange("p j d -> p (j d)")).then_inc(stored[u], 16)

                turns(act, k.TN, body)
                for u in range(UN):
                    act.wait_ge(stored[u], k.TN * 16)


def load_records(sp, k, u, t, rec, rec_in):
    sp.dma_start(rec[:, u].rearrange("p f j -> p (f j)"),
                 k.meta[:, t * U + u].rearrange("p f j -> p (f j)")).then_inc(rec_in[u], 16)


def sum_edges(k, table):
    nc = k.nc
    with ExitStack() as c:
        sb = lambda n, s, d=F32: c.enter_context(nc.sbuf_tensor(k.name(n), s, d))
        sem = lambda n: k.semaphore(n)
        rec = sb("rec", [P, U, FIELDS, J], I32)
        got = sb("got", [P, U, J, D])
        run = sb("run", [P, U, J, D])
        head = sb("head", [P, D])
        fix = sb("fix", [P, D])
        part = c.enter_context(nc.psum_tensor(k.name("part"), [P, 512], F32))
        rec_in = [sem(f"rec_in{u}") for u in range(U)]
        got_in = [sem(f"got_in{u}") for u in range(U)]
        put_out = [sem(f"put_out{u}") for u in range(U)]
        summed, ready, begun = sem("summed"), sem("ready"), sem("begun")
        joined, fixed, fix_out = sem("joined"), sem("fixed"), sem("fix_out")
        passed = sem("passed")
        recf = rec[:].bitcast(F32)
        T = k.T
        PER = 2 * J
        with nc.Block() as b:

            @b.sync
            def _(sp):
                def body(t):
                    for u in range(U):
                        wait(sp, put_out[u], t * 16 * J, passed)
                        wait(sp, summed, (t * U + u - U + 1) * PER, passed)
                        load_records(sp, k, u, t, rec, rec_in)

                turns(sp, T, body)

            @b.gpsimd
            def _(pool):
                def gather(t, u):
                    wait(pool, rec_in[u], (t + 1) * 16, passed)
                    for j in range(J):
                        pool.indirect_dma_start(got[:, u, j, :], None, table,
                                                bass.IndirectOffsetOnAxis(ap=rec[:, u, SRC, j : j + 1], axis=0)).then_inc(got_in[u], 16)

                def scatter(t, u):
                    wait(pool, summed, (t * U + u + 1) * PER, passed)
                    for j in range(J):
                        pool.indirect_dma_start(k.msg, bass.IndirectOffsetOnAxis(ap=rec[:, u, PUT, j : j + 1], axis=0),
                                                run[:, u, j, :], None, bounds_check=k.NR - 1, oob_is_err=False).then_inc(put_out[u], 16)

                def body(t):
                    for u in range(U):
                        if not (isinstance(t, int) and t == T - 1 and u + LAG >= U):
                            gather(t + (u + LAG) // U, (u + LAG) % U)
                        scatter(t, u)

                for u in range(LAG):
                    gather(0, u)
                turns(pool, T, body)
                for u in range(U):
                    pool.wait_ge(put_out[u], T * 16 * J)
                pool.wait_ge(fixed, 1)
                pool.indirect_dma_start(k.msg, bass.IndirectOffsetOnAxis(ap=k.join_row[:], axis=0), fix[:], None,
                                        bounds_check=k.NR - 1, oob_is_err=False).then_inc(fix_out, 16)
                pool.wait_ge(fix_out, 16)

            @b.vector
            def _(dve):
                step = Chain(dve, summed, PER)
                begin = Chain(dve, begun)
                begin(dve.memset(run[:, U - 1, J - 1, :], 0.0))
                begin(dve.memset(head[:], 0.0))

                def body(t):
                    for u in range(U):
                        step.at(t * U + u)
                        dve.wait_ge(got_in[u], (t + 1) * 16 * J)
                        wait(dve, put_out[u], t * 16 * J)
                        for j in range(J):
                            prev = run[:, u, j - 1, :] if j else run[:, (u - 1) % U, J - 1, :]
                            step(dve.scalar_tensor_tensor(run[:, u, j, :], prev, recf[:, u, SAME, j : j + 1], got[:, u, j, :],
                                                          ALU.mult, ALU.add))
                            step(dve.scalar_tensor_tensor(head[:], run[:, u, j, :], recf[:, u, END, j : j + 1], head[:],
                                                          ALU.mult, ALU.add))
                        step.end()

                turns(dve, T, body)
                dve.nop().then_inc(ready, 1)
                dve.wait_ge(joined, 1)
                dve.tensor_tensor(fix[:], part[:, 0:D], head[:], ALU.add).then_inc(fixed, 1)

            @b.tensor
            def _(pe):
                pe.wait_ge(ready, 1)
                pe.matmul(part[:, 0:D], k.join_t[:], run[:, U - 1, J - 1, :], start=True, stop=True).then_inc(joined, 1)


class Coef:

    def __init__(self, sb, H):
        self.H = H
        self.A = sb("cA", [P, H, J + 1])
        self.neg = sb("cneg", [P, H, J + 1])
        self.m = sb("cm", [P, H, J + 1])
        self.ex = sb("cex", [P, 2, H, J])
        self.f = sb("cf", [P, H, J + 1])
        self.a = sb("ca", [P, H, J + 1])
        self.z = sb("cz", [P, H, J + 1])
        self.rz = sb("crz", [P, H, J])
        self.b = sb("cb", [P, H, J])
        self.g = sb("cg", [P, H, J])
        self.pick = sb("cpick", [P, 2, H, J])
        self.got = sb("cgot", [P, 2 * H])
        self.head = sb("chead", [P, 2 * H])

    def begin(self, step, dve):
        step(dve.memset(self.neg[:], LOW))
        step(dve.memset(self.f[:], 0.0))
        step(dve.memset(self.A[:], 0.0))
        step(dve.memset(self.a[:], 1.0))
        step(dve.memset(self.head[:], 0.0))

    BEFORE, AFTER = 5, 11

    def before_exp(self, step, dve, same):
        H = self.H
        samw = same.unsqueeze(1).to_broadcast([P, H, J])
        flat = lambda t: t[:].rearrange("p h j -> p (h j)")
        step(dve.tensor_scalar(self.neg[:, :, 1:], samw, -LOW, LOW, ALU.mult, ALU.add))
        step(dve.tensor_tensor_scan(flat(self.m), flat(self.neg), flat(self.A), 0.0, ALU.add, ALU.max))
        step(dve.tensor_tensor(self.ex[:, 0], self.m[:, :, 0:J], self.m[:, :, 1:], ALU.subtract))
        step(dve.tensor_scalar(self.ex[:, 0], self.ex[:, 0], 0.0, None, ALU.min))
        step(dve.tensor_tensor(self.ex[:, 1], self.A[:, :, 1:], self.m[:, :, 1:], ALU.subtract))

    def after_exp(self, step, dve, same, end):
        H = self.H
        wide3 = lambda s: s.unsqueeze(1).to_broadcast([P, H, J])
        flat = lambda t: t[:].rearrange("p h j -> p (h j)")
        step(dve.tensor_tensor(self.f[:, :, 1:], self.ex[:, 0], wide3(same), ALU.mult))
        step(dve.tensor_copy(self.a[:, :, 1:], self.ex[:, 1]))
        step(dve.tensor_tensor_scan(flat(self.z), flat(self.f), flat(self.a), 0.0, ALU.mult, ALU.add))
        step(dve.reciprocal(self.rz[:], self.z[:, :, 1:]))
        step(dve.tensor_tensor(self.b[:], self.a[:, :, 1:], self.rz[:], ALU.mult))
        step(dve.tensor_tensor(self.g[:], self.f[:, :, 1:], self.z[:, :, 0:J], ALU.mult))
        step(dve.tensor_tensor(self.g[:], self.g[:], self.rz[:], ALU.mult))
        step(dve.tensor_tensor(self.pick[:, 0], self.m[:, :, 1:], wide3(end), ALU.mult))
        step(dve.tensor_tensor(self.pick[:, 1], self.z[:, :, 1:], wide3(end), ALU.mult))
        step(dve.tensor_reduce(self.got[:], self.pick[:].rearrange("p s h j -> p (s h) j"), AX.X, ALU.add))
        step(dve.tensor_tensor(self.head[:], self.head[:], self.got[:], ALU.add))

    CARRY = 2

    def carry(self, step, dve):
        step(dve.tensor_copy(self.A[:, :, 0:1], self.m[:, :, J : J + 1]))
        step(dve.tensor_copy(self.a[:, :, 0:1], self.z[:, :, J : J + 1]))


def merge_softmax(k, sb, sem, ps, co, tail, head, out, W):
    nc, H = k.nc, co.H
    e = sb("me", [P, P])
    w = sb("mw", [P, P])
    wt = sb("mwt", [P, P])
    t = sb("mt", [P, P])
    s = sb("ms", [P, 8])
    rowed, exped, exp_in, turned, weighed, untangled, summed, out_of, done = [
        sem(n) for n in ("rowed", "exped", "exp_in", "turned", "weighed", "untangled", "msummed", "out_of", "mdone")]
    tm = lambda h: co.m[:, h, J : J + 1]
    tz = lambda h: co.z[:, h, J : J + 1]
    with nc.Block() as b:

        @b.tensor
        def _(pe):
            for h in range(H):
                if h:
                    pe.wait_ge(out_of, h)
                pe.transpose(ps[0][:, 0:P], wide(tm(h), P), k.ident[:])
                pe.transpose(ps[0][:, P : 2 * P], wide(tz(h), P), k.ident[:]).then_inc(rowed, 1)
                pe.wait_ge(weighed, h + 1)
                pe.transpose(ps[1][:, 0:P], w[:], k.ident[:]).then_inc(turned, 1)
                pe.wait_ge(untangled, h + 1)
                pe.matmul(ps[2][:, 0:W], wt[:], tail[:, h, :], start=True, stop=True).then_inc(summed, 1)

        @b.scalar
        def _(act):
            for h in range(H):
                act.wait_ge(exp_in, h + 1)
                act.activation(s[:, 3:4], s[:, 2:3], ACT.Exp)
                act.activation(e[:], e[:], ACT.Exp).then_inc(exped, 1)

        @b.vector
        def _(dve):
            step = Chain(dve, done)
            for h in range(H):
                dve.wait_ge(rowed, h + 1)
                mrow, zrow = ps[0][:, 0:P], ps[0][:, P : 2 * P]
                step(dve.tensor_tensor(t[:], mrow, k.no_join[:], ALU.add))
                step(dve.tensor_reduce(s[:, 0:1], t[:], AX.X, ALU.max))
                step(dve.tensor_tensor(s[:, 1:2], s[:, 0:1], co.head[:, h : h + 1], ALU.max))
                step(dve.tensor_scalar(e[:], mrow, s[:, 1:2], 0.0, ALU.subtract, ALU.min))
                step(dve.tensor_tensor(s[:, 2:3], co.head[:, h : h + 1], s[:, 1:2], ALU.subtract))
                dve.nop().then_inc(exp_in, 1)
                dve.wait_ge(exped, h + 1)
                step(dve.tensor_tensor(w[:], e[:], k.join[:], ALU.mult))
                step(dve.tensor_tensor(w[:], w[:], zrow, ALU.mult))
                step(dve.tensor_reduce(s[:, 4:5], w[:], AX.X, ALU.add))
                step(dve.tensor_tensor(s[:, 5:6], s[:, 3:4], co.head[:, H + h : H + h + 1], ALU.mult))
                step(dve.tensor_tensor(s[:, 4:5], s[:, 4:5], s[:, 5:6], ALU.add))
                step(dve.tensor_scalar(s[:, 4:5], s[:, 4:5], 1.0e-30, None, ALU.max))
                step(dve.reciprocal(s[:, 6:7], s[:, 4:5]))
                step(dve.tensor_tensor(s[:, 7:8], s[:, 5:6], s[:, 6:7], ALU.mult))
                step(dve.tensor_scalar(w[:], w[:], s[:, 6:7], None, ALU.mult))
                dve.nop().then_inc(weighed, 1)
                dve.wait_ge(turned, h + 1)
                step(dve.tensor_copy(wt[:], ps[1][:, 0:P]))
                dve.nop().then_inc(untangled, 1)
                dve.wait_ge(summed, h + 1)
                step(dve.scalar_tensor_tensor(out[:, h, :], head[:, h, :], s[:, 7:8], ps[2][:, 0:W], ALU.mult, ALU.add))
                dve.nop().then_inc(out_of, 1)


X2 = D + 2
FEAT = (slice(0, D), slice(2, X2))
PAIR = (slice(D, X2), slice(0, 2))
SEEN = (slice(2, 2 + X2), slice(0, X2))


def fold_conv(k, l):
    nc, A = k.nc, k.a
    with ExitStack() as c:
        sb = lambda n, s, d=F32: c.enter_context(nc.sbuf_tensor(k.name(n), s, d))
        sem = lambda n: k.semaphore(n)
        wq = sb("wq", [P, 2, D])
        wk = sb("wk", [P, 2, D])
        wv = sb("wv", [P, 2, D])
        vb = sb("vb", [4, D])
        bq = sb("bq", [P, 2])
        wqt = sb("wqt", [P, 2, D])
        right = sb("right", [P, 2, X2])
        pt = [c.enter_context(nc.psum_tensor(k.name(f"pt{i}"), [P, 512], F32)) for i in range(2)]
        pm = [c.enter_context(nc.psum_tensor(k.name(f"pm{i}"), [P, 512], F32)) for i in range(2)]
        loaded, turned, copied, folded, done = [sem(n) for n in ("loaded", "turned", "copied", "folded", "done")]
        heads = lambda ap: ap.rearrange("i (h d) -> i h d", h=2)
        cols = lambda ap: ap.rearrange("(h d) -> d h", h=2)
        with nc.Block() as b:

            @b.sync
            def _(sp):
                with nc.allow_non_contiguous_dma(reason="two columns of biases"):
                    sp.dma_start(wq[:], heads(A["L1_gnn_Wq"][l])).then_inc(loaded, 16)
                    sp.dma_start(wk[:], heads(A["L1_gnn_Wk"][l])).then_inc(loaded, 16)
                    sp.dma_start(wv[:], heads(A["L1_gnn_Wv"][l])).then_inc(loaded, 16)
                    sp.dma_start(k.w_skip[:], A["L1_gnn_Wskip"][l]).then_inc(loaded, 16)
                    for h in range(2):
                        hd = slice(h * D, (h + 1) * D)
                        sp.dma_start(right[:, h, PAIR[h].start : PAIR[h].start + 1], A["L1_gnn_bk"][l, hd].unsqueeze(1)).then_inc(loaded, 16)
                        sp.dma_start(right[:, h, PAIR[h].start + 1 : PAIR[h].stop], A["L1_gnn_We"][l, 0, hd].unsqueeze(1)).then_inc(loaded, 16)
                        sp.dma_start(bq[:, h : h + 1], A["L1_gnn_bq"][l, hd].unsqueeze(1)).then_inc(loaded, 16)
                        sp.dma_start(vb[2 * h : 2 * h + 1, :], A["L1_gnn_bv"][l, hd].unsqueeze(0)).then_inc(loaded, 16)
                        sp.dma_start(vb[2 * h + 1 : 2 * h + 2, :], A["L1_gnn_We"][l, 0:1, hd]).then_inc(loaded, 16)
                    sp.dma_start(k.b_skip[0:1, :], A["L1_gnn_bskip"][l].unsqueeze(0)).then_inc(loaded, 16)
                    sp.dma_start(k.ln_g[:], A["L1_gnn_ln_g"][l].partition_broadcast(P)).then_inc(loaded, 16)
                    sp.dma_start(k.ln_b[:], A["L1_gnn_ln_b"][l].partition_broadcast(P)).then_inc(loaded, 16)
                sp.wait_ge(loaded, 16 * 17)

            @b.tensor
            def _(pe):
                pe.wait_ge(loaded, 16 * 17)
                for h in range(2):
                    pe.transpose(pt[0][:, h * D : (h + 1) * D], wq[:, h, :], k.ident[:])
                    pe.transpose(pt[1][:, h * D : (h + 1) * D], wk[:, h, :], k.ident[:]).then_inc(turned, 1)
                pe.wait_ge(copied, 2)
                for h in range(2):
                    pe.matmul(pm[0][:, h * X2 : (h + 1) * X2], wqt[:, h, :], right[:, h, :], start=True, stop=True)
                    pe.matmul(pm[1][0:1, h * X2 : (h + 1) * X2], bq[:, h : h + 1], right[:, h, :], start=True,
                              stop=True).then_inc(folded, 1)

            @b.vector
            def _(dve):
                step = Chain(dve, done)
                dve.wait_ge(loaded, 16 * 17)
                dve.wait_ge(turned, 2)
                step(dve.tensor_copy(wqt[:], pt[0][:, 0 : 2 * D].rearrange("p (h d) -> p h d", h=2)))
                dve.nop().then_inc(copied, 1)
                for h in range(2):
                    step(dve.tensor_copy(right[:, h, FEAT[h]], pt[1][:, h * D : (h + 1) * D]))
                dve.nop().then_inc(copied, 1)
                step(dve.tensor_scalar(k.w_val[:], wv[:], 0.5, None, ALU.mult))
                step(dve.tensor_scalar(k.b_val[:], vb[:], 0.5, None, ALU.mult))
                dve.wait_ge(folded, 2)
                step(dve.tensor_copy(k.w_qk[:].rearrange("p h d -> p (h d)"), pm[0][:, 0 : 2 * X2]))
                step(dve.tensor_copy(k.b_qk[:].rearrange("p h d -> p (h d)"), pm[1][0:1, 0 : 2 * X2]))


def conv_edges(k, table):
    nc, T = k.nc, k.T
    H = 2
    with ExitStack() as c:
        sb = lambda n, s, d=F32: c.enter_context(nc.sbuf_tensor(k.name(n), s, d))
        sem = lambda n: k.semaphore(n)
        psum = lambda n: c.enter_context(nc.psum_tensor(k.name(n), [P, 512], F32))
        rec = sb("rec", [P, U, FIELDS, J], I32)
        xs = sb("xs", [P, U, J, D + 4])
        xd = sb("xd", [P, U, J, D])
        xdt = sb("xdt", [P, 2, D])
        junk = sb("junk", [P, 2, H, X2])
        st = sb("st", [P, U, J, H, X2])
        at = sb("at", [P, 2, H * D])
        bt = sb("bt", [4, 2, P])
        head = sb("head", [P, H, X2])
        fix = sb("fix", [P, H, X2])
        mo = sb("mo", [P, U, J, D])
        fo = sb("fo", [P, D])
        co = Coef(sb, H)
        p_t = [psum(f"p_t{i}") for i in range(2)]
        p_y = [psum(f"p_y{i}") for i in range(2)]
        p_a = [psum(f"p_a{i}") for i in range(2)]
        p_m = [psum(f"p_m{i}") for i in range(2)]
        rec_in = [sem(f"rec_in{u}") for u in range(U)]
        got_in = [sem(f"got_in{u}") for u in range(U)]
        put_out = [sem(f"put_out{u}") for u in range(U)]
        xd_turned, xd_copied, y_made, scored = [sem(n) for n in ("xd_turned", "xd_copied", "y_made", "scored")]
        exp_in, exped, shares, weighted, st_done = [sem(n) for n in ("exp_in", "exped", "shares", "weighted", "st_done")]
        st_turned, st_copied, m_made, m_out = [sem(n) for n in ("st_turned", "st_copied", "m_made", "m_out")]
        dve_done, begun = sem("dve_done"), sem("begun")
        passed = sem("passed")
        recf = rec[:].bitcast(F32)
        PER = 2 + co.BEFORE + co.AFTER + co.CARRY + J * 3
        scale = float(D) ** -0.5

        def value_turn(pe, a, i):
            for h in range(H):
                pe.transpose(p_a[i][:, h * D : (h + 1) * D], a[:, h, FEAT[h]], k.ident[:])
            pair = a.rearrange("p h x -> p (h x)")[:, D : D + 4]
            return pe.transpose(p_a[i][0:4, 2 * D : 3 * D], pair, k.ident[:])

        def value_copy(act, i):
            act.activation(bt[:, i, :], p_a[i][0:4, 2 * D : 3 * D], ACT.Copy)
            return act.activation(at[:, i, :], p_a[i][:, 0 : 2 * D], ACT.Copy)

        def value_product(pe, i):
            pe.matmul(p_m[i][:, 0:D], at[:, i, 0:D], k.w_val[:, 0, :], start=True, stop=False)
            pe.matmul(p_m[i][:, 0:D], at[:, i, D : 2 * D], k.w_val[:, 1, :], start=False, stop=False)
            return pe.matmul(p_m[i][:, 0:D], bt[:, i, :], k.b_val[:], start=False, stop=True)

        with nc.Block() as b:

            @b.sync
            def _(sp):
                def body(t):
                    for u in range(U):
                        wait(sp, put_out[u], t * 16 * J, passed)
                        wait(sp, dve_done, (t * U + u - U + 1) * PER, passed)
                        load_records(sp, k, u, t, rec, rec_in)

                turns(sp, T, body)

            @b.gpsimd
            def _(pool):
                def gather(t, u):
                    wait(pool, rec_in[u], (t + 1) * 16, passed)
                    for j in range(J):
                        pool.indirect_dma_start(xs[:, u, j, 2 : 2 + D], None, table,
                                                bass.IndirectOffsetOnAxis(ap=rec[:, u, SRC, j : j + 1], axis=0)).then_inc(got_in[u], 16)
                        pool.indirect_dma_start(xd[:, u, j, :], None, table,
                                                bass.IndirectOffsetOnAxis(ap=rec[:, u, DST, j : j + 1], axis=0)).then_inc(got_in[u], 16)

                def scatter(t, u):
                    wait(pool, m_out, (t * U + u + 1) * J, passed)
                    for j in range(J):
                        pool.indirect_dma_start(k.msg, bass.IndirectOffsetOnAxis(ap=rec[:, u, PUT, j : j + 1], axis=0),
                                                mo[:, u, j, :], None, bounds_check=k.NR - 1, oob_is_err=False).then_inc(put_out[u], 16)

                def body(t):
                    for u in range(U):
                        if not (isinstance(t, int) and t == T - 1 and u + LAG >= U):
                            gather(t + (u + LAG) // U, (u + LAG) % U)
                        scatter(t, u)

                for u in range(LAG):
                    gather(0, u)
                turns(pool, T, body)
                for u in range(U):
                    pool.wait_ge(put_out[u], T * 16 * J)

            @b.tensor
            def _(pe):
                def body(t):
                    for u in range(U):
                        blk = t * U + u
                        n0 = blk * J
                        pe.wait_ge(got_in[u], (t + 1) * 32 * J)

                        def turn_xd(j):
                            wait(pe, xd_copied, n0 + j - 1)
                            pe.transpose(p_t[(u * J + j) % 2][:, 0:D], xd[:, u, j, :], k.ident[:]).then_inc(xd_turned, 1)

                        turn_xd(0)
                        for j in range(J):
                            if j + 1 < J:
                                turn_xd(j + 1)
                            pe.wait_ge(xd_copied, n0 + j + 1)
                            wait(pe, scored, n0 + j - 1)
                            pe.matmul(p_y[(u * J + j) % 2][:, 0 : H * X2], xdt[:, (u * J + j) % 2, :], k.w_qk[:].rearrange("p h d -> p (h d)"),
                                      start=True, stop=False)
                            pe.matmul(p_y[(u * J + j) % 2][:, 0 : H * X2], k.ones[0:1, :], k.b_qk[:].rearrange("p h d -> p (h d)"),
                                      start=False, stop=True).then_inc(y_made, 1)

                        def turn_st(j):
                            pe.wait_ge(st_done, n0 + j + 1)
                            wait(pe, st_copied, n0 + j - 1)
                            value_turn(pe, st[:, u, j], (u * J + j) % 2).then_inc(st_turned, 1)

                        turn_st(0)
                        for j in range(J):
                            if j + 1 < J:
                                turn_st(j + 1)
                            pe.wait_ge(st_copied, n0 + j + 1)
                            wait(pe, m_out, n0 + j - 1)
                            value_product(pe, (u * J + j) % 2).then_inc(m_made, 1)

                turns(pe, T, body)

            @b.scalar
            def _(act):
                def body(t):
                    for u in range(U):
                        blk = t * U + u
                        n0 = blk * J
                        for j in range(J):
                            act.wait_ge(xd_turned, n0 + j + 1)
                            wait(act, y_made, n0 + j - 1)
                            act.activation(xdt[:, (u * J + j) % 2, :], p_t[(u * J + j) % 2][:, 0:D], ACT.Copy).then_inc(xd_copied, 1)
                        act.wait_ge(exp_in, blk + 1)
                        act.activation(co.ex[:], co.ex[:], ACT.Exp).then_inc(exped, 1)
                        act.wait_ge(shares, blk + 1)
                        wait(act, st_turned, (blk - U + 1) * J)
                        for j in range(J):
                            act.activation(st[:, u, j, 0, :], xs[:, u, j, SEEN[0]], ACT.Copy, scale=co.b[:, 0, j : j + 1])
                            act.activation(st[:, u, j, 1, :], xs[:, u, j, SEEN[1]], ACT.Copy,
                                           scale=co.b[:, 1, j : j + 1]).then_inc(weighted, 1)
                        wait(act, put_out[u], t * 16 * J)

                        def evac(j):
                            act.wait_ge(m_made, n0 + j + 1)
                            act.activation(mo[:, u, j, :], p_m[(u * J + j) % 2][:, 0:D], ACT.Copy).then_inc(m_out, 1)

                        for j in range(J):
                            act.wait_ge(st_turned, n0 + j + 1)
                            wait(act, m_made, n0 + j - 1)
                            value_copy(act, (u * J + j) % 2).then_inc(st_copied, 1)
                            if j:
                                evac(j - 1)
                        evac(J - 1)

                turns(act, T, body)

            @b.vector
            def _(dve):
                begin = Chain(dve, begun)
                co.begin(begin, dve)
                begin(dve.memset(head[:], 0.0))
                begin(dve.memset(st[:, U - 1, J - 1], 0.0))
                for at_ in (0, D + 2):
                    begin(dve.memset(xs[:, :, :, at_ : at_ + 1], 1.0))
                step = Chain(dve, dve_done, PER)

                def body(t):
                    for u in range(U):
                        blk = t * U + u
                        step.at(blk)
                        n0 = blk * J
                        same, end = recf[:, u, SAME, :], recf[:, u, END, :]
                        dve.wait_ge(got_in[u], (t + 1) * 32 * J)
                        wait(dve, weighted, (blk - U + 1) * J)
                        for at_ in (1, D + 3):
                            step(dve.tensor_copy(xs[:, u, :, at_ : at_ + 1], recf[:, u, WGT, :].unsqueeze(2)))
                        for j in range(J):
                            dve.wait_ge(y_made, n0 + j + 1)
                            wait(dve, scored, n0 + j - 1)
                            dve.tensor_tensor_reduce(junk[:, (u * J + j) % 2, 0], p_y[(u * J + j) % 2][:, 0:X2], xs[:, u, j, SEEN[0]], scale, 0.0, ALU.mult,
                                                     ALU.add, co.A[:, 0, 1 + j : 2 + j])
                            ins = dve.tensor_tensor_reduce(junk[:, (u * J + j) % 2, 1], p_y[(u * J + j) % 2][:, X2 : 2 * X2], xs[:, u, j, SEEN[1]], scale, 0.0,
                                                           ALU.mult, ALU.add, co.A[:, 1, 1 + j : 2 + j])
                            ins.then_inc(scored, 1)
                        dve.wait_ge(scored, n0 + J)
                        co.before_exp(step, dve, same)
                        dve.nop().then_inc(exp_in, 1)
                        dve.wait_ge(exped, blk + 1)
                        co.after_exp(step, dve, same, end)
                        dve.nop().then_inc(shares, 1)
                        co.carry(step, dve)
                        for j in range(J):
                            dve.wait_ge(weighted, n0 + j + 1)
                            prev = st[:, u, j - 1] if j else st[:, (u - 1) % U, J - 1]
                            for h in range(H):
                                step(dve.scalar_tensor_tensor(st[:, u, j, h, :], prev[:, h, :], co.g[:, h, j : j + 1],
                                                              st[:, u, j, h, :], ALU.mult, ALU.add))
                            dve.nop().then_inc(st_done, 1)
                            step(dve.scalar_tensor_tensor(head[:], st[:, u, j], end[:, j : j + 1], head[:], ALU.mult, ALU.add))
                        step.end()

                turns(dve, T, body)

        merge_softmax(k, sb, sem, [p_t[0], p_t[1], p_y[0]], co, st[:, U - 1, J - 1], head, fix, X2)
        f_turned, f_copied, f_made, f_out, f_put = [sem(n) for n in ("f_turned", "f_copied", "f_made", "f_out", "f_put")]
        with nc.Block() as b:

            @b.tensor
            def _(pe):
                value_turn(pe, fix[:], 0).then_inc(f_turned, 1)
                pe.wait_ge(f_copied, 1)
                value_product(pe, 0).then_inc(f_made, 1)

            @b.scalar
            def _(act):
                act.wait_ge(f_turned, 1)
                value_copy(act, 0).then_inc(f_copied, 1)
                act.wait_ge(f_made, 1)
                act.activation(fo[:], p_m[0][:, 0:D], ACT.Copy).then_inc(f_out, 1)

            @b.gpsimd
            def _(pool):
                pool.wait_ge(f_out, 1)
                pool.indirect_dma_start(k.msg, bass.IndirectOffsetOnAxis(ap=k.join_row[:], axis=0), fo[:], None,
                                        bounds_check=k.NR - 1, oob_is_err=False).then_inc(f_put, 16)
                pool.wait_ge(f_put, 16)


def angle_edges(k, table):
    nc, T, A = k.nc, k.T, k.a
    H, W = 8, 16
    with ExitStack() as c:
        sb = lambda n, s, d=F32: c.enter_context(nc.sbuf_tensor(k.name(n), s, d))
        sem = lambda n: k.semaphore(n)
        psum = lambda n: c.enter_context(nc.psum_tensor(k.name(n), [P, 512], F32))
        rec = sb("rec", [P, U, FIELDS, J], I32)
        x3 = sb("x3", [P, 3, U, J, D])
        x3t = sb("x3t", [P, 2, 3 * D])
        q = sb("q", [P, 2, D])
        prod = sb("prod", [P, D])
        st = sb("st", [P, U, J, D])
        kept = sb("kept", [P, D])
        carry = sb("carry", [P, D])
        head = sb("head", [P, H, W])
        fix = sb("fix", [P, H, W])
        w_kv = sb("w_kv", [P, 2, D])
        w_q = sb("w_q", [P, D])
        w_ee = sb("w_ee", [P, D])
        b_q = sb("b_q", [P, D])
        b_kv = sb("b_kv", [1, 2 * D])
        co = Coef(sb, H)
        p_t = [psum(f"p_t{i}") for i in range(2)]
        p_q = [psum(f"p_q{i}") for i in range(2)]
        p_v = [psum(f"p_v{i}") for i in range(2)]
        rec_in = [sem(f"rec_in{u}") for u in range(U)]
        edge_in = [sem(f"edge_in{u}") for u in range(U)]
        got_in = [sem(f"got_in{u}") for u in range(U)]
        put_out = [sem(f"put_out{u}") for u in range(U)]
        w_in, turned, copied, made, v_out = [sem(n) for n in ("w_in", "turned", "copied", "made", "v_out")]
        exp_in, exped, st_done, scored = [sem(n) for n in ("exp_in", "exped", "st_done", "scored")]
        dve_done, begun, f_put = sem("dve_done"), sem("begun"), sem("f_put")
        passed = sem("passed")
        recf = rec[:].bitcast(F32)
        PER = J * 3 + co.BEFORE + co.AFTER + co.CARRY + 1 + J * 3
        scale = float(W) ** -0.5
        edge = rows(A["edge"], J)
        heads = lambda ap: ap.rearrange("p (h w) -> p h w", h=H)
        with nc.Block() as b:

            @b.sync
            def _(sp):
                sp.dma_start(w_kv[:, 0, :], A["L3_gnn_Wk"]).then_inc(w_in, 16)
                sp.dma_start(w_kv[:, 1, :], A["L3_gnn_Wv"]).then_inc(w_in, 16)
                sp.dma_start(w_q[:], A["L3_gnn_Wq"]).then_inc(w_in, 16)
                sp.dma_start(w_ee[:], A["L3_gnn_We"]).then_inc(w_in, 16)
                sp.dma_start(b_q[:], A["L3_gnn_bq"].partition_broadcast(P)).then_inc(w_in, 16)
                sp.dma_start(b_kv[:, 0:D], A["L3_gnn_bk"].unsqueeze(0)).then_inc(w_in, 16)
                sp.dma_start(b_kv[:, D : 2 * D], A["L3_gnn_bv"].unsqueeze(0)).then_inc(w_in, 16)

                def body(t):
                    for u in range(U):
                        wait(sp, put_out[u], t * 16 * J, passed)
                        wait(sp, dve_done, (t * U + u - U + 1) * PER, passed)
                        load_records(sp, k, u, t, rec, rec_in)
                        sp.dma_start(x3[:, 2, u].rearrange("p j d -> p (j d)"), edge[:, t * U + u, :]).then_inc(edge_in[u], 16)

                turns(sp, T, body)

            @b.gpsimd
            def _(pool):
                def gather(t, u):
                    wait(pool, rec_in[u], (t + 1) * 16, passed)
                    for j in range(J):
                        for s, f in ((0, SRC), (1, DST)):
                            pool.indirect_dma_start(x3[:, s, u, j, :], None, table,
                                                    bass.IndirectOffsetOnAxis(ap=rec[:, u, f, j : j + 1], axis=0)).then_inc(got_in[u], 16)

                def scatter(t, u):
                    wait(pool, st_done, t * U + u + 1, passed)
                    for j in range(J):
                        pool.indirect_dma_start(k.msg, bass.IndirectOffsetOnAxis(ap=rec[:, u, PUT, j : j + 1], axis=0),
                                                st[:, u, j, :], None, bounds_check=k.NR - 1, oob_is_err=False).then_inc(put_out[u], 16)

                def body(t):
                    for u in range(U):
                        if not (isinstance(t, int) and t == T - 1 and u + LAG >= U):
                            gather(t + (u + LAG) // U, (u + LAG) % U)
                        scatter(t, u)

                for u in range(LAG):
                    gather(0, u)
                turns(pool, T, body)
                for u in range(U):
                    pool.wait_ge(put_out[u], T * 16 * J)

            @b.tensor
            def _(pe):
                pe.wait_ge(w_in, 16 * 7)

                def body(t):
                    for u in range(U):
                        n0 = (t * U + u) * J
                        pe.wait_ge(got_in[u], (t + 1) * 32 * J)
                        pe.wait_ge(edge_in[u], (t + 1) * 16)

                        def turn(j):
                            wait(pe, copied, n0 + j - 1)
                            for s in range(3):
                                ins = pe.transpose(p_t[(u * J + j) % 2][:, s * D : (s + 1) * D], x3[:, s, u, j, :], k.ident[:])
                            ins.then_inc(turned, 1)

                        turn(0)
                        for j in range(J):
                            if j + 1 < J:
                                turn(j + 1)
                            pe.wait_ge(copied, n0 + j + 1)
                            wait(pe, v_out, n0 + j - 1)
                            wait(pe, scored, n0 + j - 1)
                            tj = x3t[:, (u * J + j) % 2, :]
                            pe.matmul(p_q[(u * J + j) % 2][:, 0:D], tj[:, D : 2 * D], w_q[:], start=True, stop=True)
                            for s, o in enumerate((p_q[(u * J + j) % 2][:, D : 2 * D], p_v[(u * J + j) % 2][:, 0:D])):
                                pe.matmul(o, tj[:, 0:D], w_kv[:, s, :], start=True, stop=False)
                                pe.matmul(o, tj[:, 2 * D : 3 * D], w_ee[:], start=False, stop=False)
                                ins = pe.matmul(o, k.ones[0:1, :], b_kv[:, s * D : (s + 1) * D], start=False, stop=True)
                            ins.then_inc(made, 1)

                turns(pe, T, body)

            @b.scalar
            def _(act):
                def body(t):
                    for u in range(U):
                        blk = t * U + u
                        n0 = blk * J

                        def values(j):
                            act.wait_ge(made, n0 + j + 1)
                            act.activation(st[:, u, j, :], p_v[(u * J + j) % 2][:, 0:D], ACT.Copy).then_inc(v_out, 1)

                        for j in range(J):
                            act.wait_ge(turned, n0 + j + 1)
                            wait(act, made, n0 + j - 1)
                            act.activation(x3t[:, (u * J + j) % 2, :], p_t[(u * J + j) % 2][:, 0 : 3 * D], ACT.Copy).then_inc(copied, 1)
                            if j == 0:
                                wait(act, put_out[u], t * 16 * J)
                            else:
                                values(j - 1)
                        values(J - 1)
                        act.wait_ge(exp_in, blk + 1)
                        act.activation(co.ex[:], co.ex[:], ACT.Exp).then_inc(exped, 1)

                turns(act, T, body)

            @b.vector
            def _(dve):
                begin = Chain(dve, begun)
                co.begin(begin, dve)
                begin(dve.memset(head[:], 0.0))
                begin(dve.memset(st[:, U - 1, J - 1], 0.0))
                begin(dve.memset(kept[:], 0.0))
                dve.wait_ge(w_in, 16 * 7)
                step = Chain(dve, dve_done, PER)

                def body(t):
                    for u in range(U):
                        blk = t * U + u
                        step.at(blk)
                        n0 = blk * J
                        same, end = recf[:, u, SAME, :], recf[:, u, END, :]
                        dve.wait_ge(rec_in[u], (t + 1) * 16)
                        for j in range(J):
                            dve.wait_ge(made, n0 + j + 1)
                            step(dve.tensor_tensor(q[:, (u * J + j) % 2, :], p_q[(u * J + j) % 2][:, 0:D], b_q[:], ALU.add))
                            step(dve.scalar_tensor_tensor(prod[:], q[:, (u * J + j) % 2, :], scale, p_q[(u * J + j) % 2][:, D : 2 * D], ALU.mult, ALU.mult))
                            dve.nop().then_inc(scored, 1)
                            step(dve.tensor_reduce(co.A[:, :, 1 + j : 2 + j], heads(prod[:]), AX.X, ALU.add))
                        co.before_exp(step, dve, same)
                        dve.nop().then_inc(exp_in, 1)
                        dve.wait_ge(exped, blk + 1)
                        co.after_exp(step, dve, same, end)
                        co.carry(step, dve)
                        dve.wait_ge(v_out, n0 + J)
                        step(dve.tensor_tensor(st[:, u].rearrange("p j (h w) -> p j h w", h=H),
                                               st[:, u].rearrange("p j (h w) -> p j h w", h=H),
                                               co.b[:].rearrange("p h j -> p j h").unsqueeze(3).to_broadcast([P, J, H, W]), ALU.mult))
                        for j in range(J):
                            prev = st[:, u, j - 1, :] if j else carry[:]
                            step(dve.tensor_tensor(heads(kept[:]), heads(prev), co.g[:, :, j : j + 1].to_broadcast([P, H, W]), ALU.mult))
                            step(dve.tensor_tensor(st[:, u, j, :], st[:, u, j, :], kept[:], ALU.add))
                            step(dve.scalar_tensor_tensor(head[:].rearrange("p h w -> p (h w)"), st[:, u, j, :], end[:, j : j + 1],
                                                          head[:].rearrange("p h w -> p (h w)"), ALU.mult, ALU.add))
                        dve.tensor_copy(carry[:], st[:, u, J - 1, :]).then_inc(st_done, 1)
                        dve.wait_ge(st_done, blk + 1)
                        step.end()

                dve.memset(carry[:], 0.0).then_inc(begun, 1)
                dve.wait_ge(begun, begin.n + 1)
                turns(dve, T, body)

        merge_softmax(k, sb, sem, [p_t[0], p_t[1], p_q[0]], co, heads(carry[:]), head, fix, W)
        with nc.Block() as b:

            @b.gpsimd
            def _(pool):
                pool.indirect_dma_start(k.msg, bass.IndirectOffsetOnAxis(ap=k.join_row[:], axis=0),
                                        fix[:].rearrange("p h w -> p (h w)"), None,
                                        bounds_check=k.NR - 1, oob_is_err=False).then_inc(f_put, 16)
                pool.wait_ge(f_put, 16)


class Nodes:

    def __init__(self, k, c, n_in, n_out, n_tmp, n_src):
        nc = self.nc = k.nc
        self.k = k
        sb = lambda n, s, d=F32: c.enter_context(nc.sbuf_tensor(k.name(n), s, d))
        sem = lambda n: k.semaphore(n)
        psum = lambda n: c.enter_context(nc.psum_tensor(k.name(n), [P, 512], F32))
        self.x = [sb(f"in{i}", [P, UN, JN, D]) for i in range(n_in)]
        self.o = [sb(f"out{i}", [P, UN, JN, D]) for i in range(n_out)]
        self.t = [sb(f"tmp{i}", [P, JN, D]) for i in range(n_tmp)]
        self.sq = sb("sq", [P, JN, D])
        self.s = sb("stat", [P, 4, JN])
        self.xt = sb("xt", [P, 2, max(n_src, 1), 4 * D])
        self.p_t = [[psum(f"p_t{i}{s}") for s in range(max(n_src, 1))] for i in range(2)]
        self.p_m = [psum(f"p_m{i}") for i in range(2)]
        self.loaded = [sem(f"loaded{u}") for u in range(UN)]
        self.stored = [sem(f"stored{u}") for u in range(UN)]
        self.prepped, self.turned, self.copied = sem("prepped"), sem("turned"), sem("copied")
        self.made, self.taken, self.asked = sem("made"), sem("taken"), sem("asked")
        self.radicand, self.rooted, self.passed = sem("radicand"), sem("rooted"), sem("passed")
        self.answered, self.finished, self.done = sem("answered"), sem("finished"), sem("done")

    def norm(self, step, dve, v, o, gain=None, shift=None):
        s = self.s
        row = lambda i: s[:, i, :].unsqueeze(2).to_broadcast([P, JN, D])
        step(dve.tensor_reduce(s[:, 0, :], v, AX.X, ALU.add))
        step(dve.tensor_scalar(s[:, 0, :], s[:, 0, :], -1.0 / D, None, ALU.mult))
        step(dve.tensor_tensor(v, v, row(0), ALU.add))
        self.ask(dve)
        step(dve.tensor_reduce(s[:, 1, :], self.sq[:], AX.X, ALU.add))
        step(dve.tensor_scalar(s[:, 1, :], s[:, 1, :], 1.0 / D, EPS, ALU.mult, ALU.add))
        self.root(dve)
        step(dve.tensor_tensor(o, v, row(1), ALU.mult))
        if gain is not None:
            step(dve.tensor_tensor(o, o, gain[:].unsqueeze(1).to_broadcast([P, JN, D]), ALU.mult))
            step(dve.tensor_tensor(o, o, shift[:].unsqueeze(1).to_broadcast([P, JN, D]), ALU.add))

    def root(self, dve):
        self.n_root += 1
        dve.nop().then_inc(self.radicand, 1)
        dve.wait_ge(self.rooted, self.root_base + self.n_root)

    def ask(self, dve):
        self.n_ask += 1
        dve.nop().then_inc(self.asked, 1)
        dve.wait_ge(self.answered, self.ask_base + self.n_ask)

    def run(self, ins, outs, srcs, weights, bias, math, per, asks, n_root, prep=None, prep_per=0, stats=None, begin=None):
        k, nc, TN = self.k, self.nc, self.k.TN
        n_ask = len(asks(0))
        n_src = len(srcs(0)) if srcs else 0

        def is_last(t, u):
            return isinstance(t, int) and t == TN - 1 and u == UN - 1

        with nc.Block() as b:

            @b.sync
            def _(sp):
                def body(t):
                    for u in range(UN):
                        wait(sp, self.finished, t * UN + u - 1, self.passed)
                        for i, table in enumerate(ins):
                            sp.dma_start(self.x[i][:, u].rearrange("p j d -> p (j d)"),
                                         rows(table)[:, t * UN + u, :]).then_inc(self.loaded[u], 16)

                turns(sp, TN, body)

            @b.gpsimd
            def _(pool):
                def body(t):
                    for u in range(UN):
                        for i in range(n_root):
                            wait(pool, self.radicand, (t * UN + u) * n_root + i + 1, self.passed)
                            root = self.s[:, 1, :]
                            pool.tensor_tensor(root, root, wide(k.root[:], JN), ALU.pow).then_inc(self.rooted, 1)
                        wait(pool, self.finished, t * UN + u + 1, self.passed)
                        for i, table in enumerate(outs):
                            pool.dma_start(rows(table)[:, t * UN + u, :],
                                           self.o[i][:, u].rearrange("p j d -> p (j d)")).then_inc(self.stored[u], 16)

                turns(pool, TN, body)
                for u in range(UN):
                    pool.wait_ge(self.stored[u], TN * 16 * len(outs))

            @b.tensor
            def _(pe):
                def body(t):
                    for u in range(UN):
                        blk = t * UN + u
                        g0 = blk * NG
                        if n_src:
                            pe.wait_ge(self.loaded[u], (t + 1) * 16 * len(ins))
                            if prep:
                                pe.wait_ge(self.prepped, blk + 1)

                            def turn(g):
                                a, z = GROUPS[g]
                                wait(pe, self.copied, g0 + g - 1)
                                for s, x in enumerate(srcs(u)):
                                    for r in range(a, z):
                                        ins_ = pe.transpose(self.p_t[g % 2][s][:, (r - a) * D : (r - a + 1) * D], x[:, r, :], k.ident[:])
                                ins_.then_inc(self.turned, 1)

                            turn(0)
                            for g, (a, z) in enumerate(GROUPS):
                                if g + 1 < NG:
                                    turn(g + 1)
                                pe.wait_ge(self.copied, g0 + g + 1)
                                wait(pe, self.taken, g0 + g - 1)
                                for r in range(z - a):
                                    o = self.p_m[g % 2][:, r * D : (r + 1) * D]
                                    for s in range(n_src):
                                        pe.matmul(o, self.xt[:, g % 2, s, r * D : (r + 1) * D], weights[s][:], start=s == 0, stop=False)
                                    ins_ = pe.matmul(o, k.ones[0:1, :], bias[0:1, :], start=False, stop=True)
                                ins_.then_inc(self.made, 1)
                        if stats and not (isinstance(blk, int) and blk == 0):
                            stats(pe, blk - 1, (u - 1) % UN)

                turns(pe, TN, body)
                if stats:
                    stats(pe, TN * UN - 1, UN - 1)

            @b.scalar
            def _(act):
                def evacuate(blk):
                    for g, (a, z) in enumerate(GROUPS):
                        act.wait_ge(self.turned, blk * NG + g + 1)
                        wait(act, self.made, blk * NG + g - 1)
                        for s in range(n_src):
                            ins_ = act.activation(self.xt[:, g % 2, s, 0 : (z - a) * D], self.p_t[g % 2][s][:, 0 : (z - a) * D], ACT.Copy)
                        ins_.then_inc(self.copied, 1)

                def body(t):
                    for u in range(UN):
                        blk = t * UN + u
                        if n_src and not is_last(t, u):
                            evacuate(blk + 1)
                        for i, (o, v, f, scale) in enumerate(asks(u)):
                            act.wait_ge(self.asked, blk * n_ask + i + 1)
                            act.activation(o, v, f, scale=scale).then_inc(self.answered, 1)

                if n_src:
                    evacuate(0)
                turns(act, TN, body)

            @b.vector
            def _(dve):
                if begin:
                    begin(dve)
                step = Chain(dve, self.done, per + prep_per)

                def prepare(t, u):
                    dve.wait_ge(self.loaded[u], (t + 1) * 16 * len(ins))
                    if prep:
                        prep(step, dve, t * UN + u, u)
                        dve.nop().then_inc(self.prepped, 1)

                def body(t):
                    for u in range(UN):
                        blk = t * UN + u
                        step.at(blk)
                        if is_last(t, u):
                            for _ in range(prep_per):
                                step(dve.nop())
                        else:
                            prepare(t + (u + 1) // UN, (u + 1) % UN)
                        wait(dve, self.stored[u], t * 16 * len(outs))
                        self.ask_base, self.n_ask = blk * n_ask, 0
                        self.root_base, self.n_root = blk * n_root, 0
                        math(step, dve, blk, u)
                        dve.nop().then_inc(self.finished, 1)
                        step.end()
                        assert (self.n_ask, self.n_root) == (n_ask, n_root)

                first = Chain(dve, self.done0, 0) if prep else None
                if prep:
                    dve.wait_ge(self.loaded[0], 16 * len(ins))
                    prep(first, dve, 0, 0)
                    dve.nop().then_inc(self.prepped, 1)
                else:
                    dve.wait_ge(self.loaded[0], 16 * len(ins))
                turns(dve, TN, body)

    def take(self, step, dve, blk, z, other=None):
        for g, (a, e) in enumerate(GROUPS):
            dve.wait_ge(self.made, blk * NG + g + 1)
            ps = self.p_m[g % 2][:, 0 : (e - a) * D].rearrange("p (j d) -> p j d", d=D)
            if other is None:
                step(dve.tensor_copy(z[:, a:e, :], ps))
            else:
                step(dve.tensor_tensor(z[:, a:e, :], ps, other[:, a:e, :], ALU.add))
            dve.nop().then_inc(self.taken, 1)


def load_rows(k, pairs):
    nc = k.nc
    with ExitStack() as c:
        loaded = k.semaphore("loaded")
        with nc.Block() as b:

            @b.sync
            def _(sp):
                for tile, ap in pairs:
                    sp.dma_start(tile, ap).then_inc(loaded, 16)
                sp.wait_ge(loaded, 16 * len(pairs))


def gcn_nodes(k):
    nc, A = k.nc, k.a
    bc = lambda n: A[n].partition_broadcast(P)
    with ExitStack() as c:
        sb = lambda n, s: c.enter_context(nc.sbuf_tensor(k.name(n), s, F32))
        g2, b2 = sb("g2", [P, D]), sb("b2", [P, D])
        load_rows(k, [(k.w_skip[:], A["L0_gnn_W"]), (k.b_skip[0:1, :], A["L0_gnn_b"].unsqueeze(0)),
                      (k.ln_g[:], bc("L0_gnn_ln_gamma")), (k.ln_b[:], bc("L0_gnn_ln_beta")),
                      (g2[:], bc("L1_gnn_ln_in_g")), (b2[:], bc("L1_gnn_ln_in_b"))])
        n = Nodes(k, c, 3, 2, 2, 1)
        n.done0 = k.semaphore("done0")
        srcu = [sb(f"src{u}", [P, JN, D]) for u in range(UN)]
        z = n.t[0]
        dinv = k.dinv[:].rearrange("p (b j) -> p b j", j=JN)

        def prep(step, dve, blk, u):
            step(dve.tensor_tensor(srcu[u][:], n.x[0][:, u], n.x[1][:, u], ALU.add))
            step(dve.tensor_tensor(srcu[u][:], srcu[u][:], dinv[:, blk, :].unsqueeze(2).to_broadcast([P, JN, D]), ALU.mult))

        def math(step, dve, blk, u):
            n.take(step, dve, blk, z)
            n.norm(step, dve, z[:], z[:], k.ln_g, k.ln_b)
            step(dve.scalar_tensor_tensor(z[:], z[:], 0.0, n.x[2][:, u], ALU.max, ALU.add))
            n.norm(step, dve, z[:], n.o[0][:, u])
            step(dve.tensor_copy(z[:], n.o[0][:, u]))
            n.norm(step, dve, z[:], n.o[1][:, u], g2, b2)

        sq = (n.sq[:], z[:], ACT.Square, 1.0)
        n.run([k.msg, k.tab[0], A["x"]], [k.res, k.tab[1]], lambda u: [srcu[u]], [k.w_skip], k.b_skip,
              math, NG + 8 + 1 + 6 + 1 + 8, lambda u: [sq, sq, sq], 3, prep, 2)


def conv_nodes(k, src, dst, last):
    nc = k.nc
    with ExitStack() as c:
        n = Nodes(k, c, 3 if last else 2, 1, 3, 1)
        z, e, y = n.t

        def math(step, dve, blk, u):
            n.take(step, dve, blk, z, n.x[1][:, u])
            step(dve.tensor_scalar(e[:], z[:], 0.0, None, ALU.min))
            n.ask(dve)
            step(dve.scalar_tensor_tensor(z[:], z[:], 0.0, e[:], ALU.max, ALU.add))
            step(dve.scalar_tensor_tensor(y[:], z[:], -1.0, n.x[0][:, u], ALU.add, ALU.add))
            n.norm(step, dve, y[:], n.o[0][:, u], k.ln_g, k.ln_b)
            if last:
                step(dve.tensor_tensor(y[:], n.o[0][:, u], n.x[2][:, u], ALU.add))
                n.norm(step, dve, y[:], n.o[0][:, u])

        sq = (n.sq[:], y[:], ACT.Square, 1.0)
        n.run([src, k.msg] + ([k.res] if last else []), [dst], lambda u: [n.x[0][:, u]], [k.w_skip], k.b_skip,
              math, NG + 3 + 8 + (7 if last else 0), lambda u: [(e[:], e[:], ACT.Exp, 1.0), sq] + ([sq] if last else []),
              2 if last else 1)


def sage_nodes(k):
    nc, A = k.nc, k.a
    with ExitStack() as c:
        sb = lambda n, s, d=F32: c.enter_context(nc.sbuf_tensor(k.name(n), s, d))
        sem = lambda n: k.semaphore(n)
        w = sb("w", [P, 2, D])
        wt = sb("wt", [P, 2, D])
        gb = sb("gb", [1, 2, D])
        real_i = sb("real_i", [P, k.COLS], I32)
        real = sb("real", [P, k.COLS])
        load_rows(k, [(w[:, 0, :], A["L2_gnn_W_l"]), (w[:, 1, :], A["L2_gnn_W_r"]), (k.b_skip[0:1, :], A["L2_gnn_b_l"].unsqueeze(0)),
                      (gb[:, 0, :], A["L2_gnn_gamma"].unsqueeze(0)), (gb[:, 1, :], A["L2_gnn_beta"].unsqueeze(0))])
        with ExitStack() as c2:
            turned, row_no, done = [k.semaphore(s) for s in ("turned", "row_no", "done")]
            pw = c2.enter_context(nc.psum_tensor(k.name("pw"), [P, 512], F32))
            with nc.Block() as b:

                @b.tensor
                def _(pe):
                    pe.transpose(pw[:, 0:D], w[:, 0, :], k.ident[:])
                    pe.transpose(pw[:, D : 2 * D], w[:, 1, :], k.ident[:]).then_inc(turned, 1)

                @b.gpsimd
                def _(pool):
                    pool.iota(real_i[:], pattern=[[1, k.COLS]], base=0, channel_multiplier=k.COLS).then_inc(row_no, 1)

                @b.vector
                def _(dve):
                    step = Chain(dve, done)
                    dve.wait_ge(turned, 1)
                    step(dve.tensor_copy(wt[:].rearrange("p s d -> p (s d)"), pw[:, 0 : 2 * D]))
                    dve.wait_ge(row_no, 1)
                    step(dve.tensor_copy(real[:], real_i[:]))
                    step(dve.tensor_scalar(real[:], real[:], float(k.N), None, ALU.is_lt))

        n = Nodes(k, c, 2, 1, 1, 2)
        n.done0 = sem("done0")
        p_s = [c.enter_context(nc.psum_tensor(k.name(f"p_s{i}"), [P, 512], F32)) for i in range(2)]
        row = sb("row", [1, 6, 2 * D])
        srcu = [sb(f"src{u}", [P, JN, D]) for u in range(UN)]
        o2 = sb("o2", [P, UN, JN, D])
        counted = sem("counted")
        z = n.t[0]
        s = n.s
        part = lambda t: t[:].rearrange("p (b j) -> p b j", j=JN)
        wide3 = lambda a: a.unsqueeze(2).to_broadcast([P, JN, D])

        def prep(step, dve, blk, u):
            step(dve.tensor_tensor(srcu[u][:], n.x[0][:, u], wide3(part(k.rcnt)[:, blk, :]), ALU.mult))

        def math(step, dve, blk, u):
            n.take(step, dve, blk, z)
            n.ask(dve)
            step(dve.tensor_reduce(s[:, 1, :], n.sq[:], AX.X, ALU.add))
            step(dve.tensor_scalar(s[:, 1, :], s[:, 1, :], 1.0e-24, None, ALU.max))
            n.root(dve)
            step(dve.tensor_tensor(s[:, 1, :], s[:, 1, :], part(real)[:, blk, :], ALU.mult))
            wait(dve, counted, blk - UN + 1)
            step(dve.scalar_tensor_tensor(n.o[0][:, u], z[:], 0.0, wide3(s[:, 1, :]), ALU.max, ALU.mult))
            n.ask(dve)

        def stats(pe, blk, u):
            pe.wait_ge(n.answered, (blk + 1) * 2)
            first = isinstance(blk, int) and blk == 0
            final = isinstance(blk, int) and blk == k.TN * UN - 1
            for r in range(0, JN, 2):
                for i, src in enumerate((n.o[0], o2)):
                    ins = pe.matmul(p_s[i][0:1, 0 : 2 * D], k.ones[:, 0:1], src[:, u, r : r + 2, :].rearrange("p j d -> p (j d)"),
                                    start=first and r == 0, stop=final and r == JN - 2)
            ins.then_inc(counted, 1)

        n.run([k.msg, k.tab[0]], [k.tab[1]], lambda u: [srcu[u], n.x[1][:, u]], [wt[:, 0, :], wt[:, 1, :]], k.b_skip,
              math, NG + 4, lambda u: [(n.sq[:], z[:], ACT.Square, 1.0), (o2[:, u], n.o[0][:, u], ACT.Square, 1.0)],
              1, prep, 1, stats)
        ready, spread, done, radicand, rooted = [sem(x) for x in ("ready", "spread", "bdone", "bradicand", "brooted")]
        with nc.Block() as b:

            @b.gpsimd
            def _(pool):
                pool.wait_ge(radicand, 1)
                pool.tensor_tensor(row[:, 2, 0:D], row[:, 2, 0:D], k.root[0:1, :].to_broadcast([1, D]), ALU.pow).then_inc(rooted, 1)

            @b.vector
            def _(dve):
                step = Chain(dve, done)
                f = lambda i: row[:, i, 0:D]
                step(dve.tensor_copy(row[:, 0, :], p_s[0][0:1, 0 : 2 * D]))
                step(dve.tensor_copy(row[:, 1, :], p_s[1][0:1, 0 : 2 * D]))
                for i in range(2):
                    step(dve.tensor_tensor(f(i), f(i), row[:, i, D : 2 * D], ALU.add))
                    step(dve.tensor_scalar(f(i), f(i), 1.0 / k.N, None, ALU.mult))
                step(dve.tensor_tensor(f(2), f(0), f(0), ALU.mult))
                step(dve.tensor_tensor(f(2), f(1), f(2), ALU.subtract))
                step(dve.tensor_scalar(f(2), f(2), 0.0, EPS, ALU.max, ALU.add))
                dve.nop().then_inc(radicand, 1)
                dve.wait_ge(rooted, 1)
                step(dve.tensor_tensor(row[:, 3, 0:D], f(2), gb[:, 0, :], ALU.mult))
                step(dve.tensor_tensor(f(4), f(0), row[:, 3, 0:D], ALU.mult))
                step(dve.tensor_tensor(row[:, 3, D : 2 * D], gb[:, 1, :], f(4), ALU.subtract))
                dve.nop().then_inc(ready, 1)
                dve.wait_ge(spread, 1)
                step(dve.tensor_copy(k.bn[:].rearrange("p s d -> p (s d)"), n.p_m[0][:, 0 : 2 * D]))

            @b.tensor
            def _(pe):
                pe.wait_ge(ready, 1)
                pe.matmul(n.p_m[0][:, 0 : 2 * D], k.ones[0:1, :], row[:, 3, :], start=True, stop=True).then_inc(spread, 1)


def batch_norm_nodes(k):
    with ExitStack() as c:
        n = Nodes(k, c, 2, 1, 1, 0)
        z = n.t[0]
        every = lambda i: k.bn[:, i : i + 1, :].to_broadcast([P, JN, D])

        def math(step, dve, blk, u):
            step(dve.tensor_tensor(z[:], n.x[0][:, u], every(0), ALU.mult))
            step(dve.tensor_tensor(z[:], z[:], every(1), ALU.add))
            step(dve.tensor_tensor(z[:], z[:], n.x[1][:, u], ALU.add))
            n.norm(step, dve, z[:], n.o[0][:, u])

        n.run([k.tab[1], k.tab[0]], [k.res], None, [], None, math, 3 + 6, lambda u: [(n.sq[:], z[:], ACT.Square, 1.0)], 1)


def angle_nodes(k):
    nc, A = k.nc, k.a
    with ExitStack() as c:
        sb = lambda n, s, d=F32: c.enter_context(nc.sbuf_tensor(k.name(n), s, d))
        wb = sb("wb", [P, 3, D])
        bc = lambda n: A[n].partition_broadcast(P)
        load_rows(k, [(k.w_skip[:], A["L3_gnn_Wskip"]), (k.b_skip[0:1, :], A["L3_gnn_bskip"].unsqueeze(0)),
                      (k.ln_g[:], bc("L3_gnn_ln_gamma")), (k.ln_b[:], bc("L3_gnn_ln_beta"))]
                  + [(wb[:, i, :], A["L3_gnn_Wbeta"][i * D : (i + 1) * D, :].rearrange("d o -> (d o)").partition_broadcast(P)) for i in range(3)])
        n = Nodes(k, c, 2, 1, 3, 1)
        z, e, y = n.t
        s = n.s
        begun = k.semaphore("begun")
        row = lambda i: s[:, i, :].unsqueeze(2).to_broadcast([P, JN, D])
        every = lambda i: wb[:, i : i + 1, :].to_broadcast([P, JN, D])

        def begin(dve):
            step = Chain(dve, begun)
            step(dve.tensor_tensor(wb[:, 0, :], wb[:, 0, :], wb[:, 2, :], ALU.add))
            step(dve.tensor_tensor(wb[:, 1, :], wb[:, 1, :], wb[:, 2, :], ALU.subtract))

        def math(step, dve, blk, u):
            x, m = n.x[0][:, u], n.x[1][:, u]
            n.take(step, dve, blk, z)
            step(dve.tensor_tensor(e[:], m, every(0), ALU.mult))
            step(dve.tensor_tensor(y[:], z[:], every(1), ALU.mult))
            step(dve.tensor_tensor(e[:], e[:], y[:], ALU.add))
            step(dve.tensor_reduce(s[:, 2, :], e[:], AX.X, ALU.add))
            step(dve.tensor_scalar(s[:, 2, :], s[:, 2, :], -80.0, None, ALU.max))
            n.ask(dve)
            step(dve.tensor_scalar(s[:, 2, :], s[:, 2, :], 1.0, None, ALU.add))
            step(dve.reciprocal(s[:, 3, :], s[:, 2, :]))
            step(dve.tensor_tensor(z[:], z[:], m, ALU.subtract))
            step(dve.tensor_tensor(z[:], z[:], row(3), ALU.mult))
            step(dve.tensor_tensor(y[:], z[:], m, ALU.add))
            n.norm(step, dve, y[:], y[:], k.ln_g, k.ln_b)
            step(dve.scalar_tensor_tensor(y[:], y[:], 0.0, x, ALU.max, ALU.add))
            step(dve.tensor_tensor(y[:], y[:], x, ALU.add))
            n.norm(step, dve, y[:], n.o[0][:, u])

        sq = (n.sq[:], y[:], ACT.Square, 1.0)
        n.run([k.res, k.msg], [k.out], lambda u: [n.x[0][:, u]], [k.w_skip], k.b_skip, math, NG + 10 + 8 + 2 + 6,
              lambda u: [(s[:, 2, :], s[:, 2, :], ACT.Exp, -1.0), sq, sq], 2, begin=begin)


def build(nc, args, out, n_nodes):
    args["n_nodes"] = n_nodes
    k = Net(nc, args, out)
    k.N = n_nodes
    dram = lambda n, s, d=F32: nc.dram_tensor(n, s, d, kind="Internal").ap()
    k.msg = dram("msg", [k.NR, D])
    k.tab = [dram("tab0", [k.NR, D]), dram("tab1", [k.NR, D])]
    k.res = dram("res", [k.NR, D])
    k.meta = dram("meta", [P, k.NB, FIELDS, J], I32)
    with ExitStack() as c:
        sb = lambda n, s, d=F32: c.enter_context(nc.sbuf_tensor(k.name(n), s, d))
        k.ident, k.ones = sb("ident", [P, P]), sb("ones", [P, P])
        k.dinv, k.rcnt = sb("dinv", [P, k.COLS]), sb("rcnt", [P, k.COLS])
        k.join, k.join_t, k.no_join = sb("join", [P, P]), sb("join_t", [P, P]), sb("no_join", [P, P])
        k.root = sb("root", [P, 1])
        k.join_row = sb("join_row", [P, 1], I32)
        k.w_skip, k.b_skip = sb("w_skip", [P, D]), sb("b_skip", [1, D])
        k.ln_g, k.ln_b = sb("ln_g", [P, D]), sb("ln_b", [P, D])
        k.w_qk, k.b_qk = sb("w_qk", [P, 2, X2]), sb("b_qk", [1, 2, X2])
        k.w_val, k.b_val = sb("w_val", [P, 2, D]), sb("b_val", [4, D])
        k.bn = sb("bn", [P, 2, D])
        setup(k)
        k.end_phase()
        scale_pass(k)
        k.end_phase()
        sum_edges(k, k.tab[0])
        k.end_phase()
        gcn_nodes(k)
        k.end_phase()
        src, dst = k.tab[1], k.tab[0]
        for l in range(args["L1_gnn_Wq"].shape[0]):
            last = l == args["L1_gnn_Wq"].shape[0] - 1
            fold_conv(k, l)
            k.end_phase()
            conv_edges(k, src)
            k.end_phase()
            conv_nodes(k, src, dst, last)
            k.end_phase()
            src, dst = dst, src
        sum_edges(k, k.tab[0])
        k.end_phase()
        sage_nodes(k)
        k.end_phase()
        batch_norm_nodes(k)
        k.end_phase()
        angle_edges(k, k.res)
        k.end_phase()
        angle_nodes(k)
        k.end_phase()


_ORDER = {"x": "x", "src": "src", "dst": "dst", "edge_attr_128": "edge", "edge_weight1": "weight"}


def kernel(**inputs):
    import concourse.bacc as _bacc
    from concourse.bass_utils import run_bass_kernel_spmd as _run

    nc = _bacc.Bacc("TRN2", target_bir_lowering=False, num_devices=1)
    n = inputs["x"].shape[0]
    nr = padded(n)

    def fill(a, rows_, value):
        return np.concatenate([a, np.full((rows_,) + a.shape[1:], value, a.dtype)])

    arrays, args = {}, {}
    for name, a in inputs.items():
        if name == "L2_gnn_adj_norm_sp":
            continue
        a = np.ascontiguousarray(a)
        if name in ("x", "edge_attr_128", "edge_weight1", "src"):
            a = fill(a, nr - n, 0)
        elif name == "dst":
            a = np.concatenate([np.full((1,), -1, a.dtype), a, np.full((nr - n,), n, a.dtype), np.full((1,), -1, a.dtype)])
        arrays[f"in_{name}"] = a
        args[_ORDER.get(name, name)] = nc.dram_tensor(f"in_{name}", a.shape, mybir.dt.from_np(a.dtype), kind="ExternalInput").ap()
    out = nc.dram_tensor("out_0", (nr, D), F32, kind="ExternalOutput").ap()
    build(nc, args, out, n)
    r = _run(nc, [arrays], core_ids=[0])
    return r.results[0]["out_0"][0:n]
```

```python
from contextlib import ExitStack

import concourse.bass as bass
import concourse.mybir as mybir
import numpy as np

F32 = mybir.dt.float32
BF16 = mybir.dt.bfloat16
I32 = mybir.dt.int32
ALU = mybir.AluOpType
ACT = mybir.ActivationFunctionType
AX = mybir.AxisListType

P = 128
D = 128
J = 7
U = 4
LAG = 3
JN = 7
UB = 8
RING = 4
LEAD, DRAIN = 5, 3
AHEAD = 4
GROUPS = [(0, 4), (4, 7)]
NG = len(GROUPS)
FAR = float(1 << 20)
LOW = -1.0e30
EPS = 1.0e-5

SRC, DST, SAME, END, WGT = range(5)
FIELDS = 5


def padded(n):
    return -(-n // (P * JN * UB)) * P * JN * UB


def turns(eng, n, body):
    body(0)
    if n > 2:
        with eng.Fori(1, n - 1) as t:
            body(t)
    if n > 1:
        body(n - 1)


def wait(eng, sem, value, passed=None):
    if isinstance(value, int) and value <= 0:
        return
    eng.wait_ge(sem, value)
    if passed is not None and not isinstance(value, int):
        eng.sem_inc(passed, 1)


class Chain:

    def __init__(self, eng, sem, per=0):
        self.eng, self.sem, self.per, self.base, self.n = eng, sem, per, 0, 0

    def at(self, chunk):
        self.base, self.n = chunk * self.per, 0

    def __call__(self, ins):
        self.n += 1
        ins.then_inc(self.sem, 1)
        self.eng.wait_ge(self.sem, self.base + self.n)

    def end(self):
        assert self.n == self.per, (self.n, self.per)


class Net:
    def __init__(self, nc, args, outs):
        self.nc = nc
        self.a = args
        self.out = outs
        self.NR = args["x"].shape[0]
        self.COLS = self.NR // P
        self.NB = self.COLS // J
        self.T = self.NB // U
        self.TN = self.COLS // (JN * UB)
        self.names = 0
        self.sems = []

    def semaphore(self, what):
        handle = self.nc.alloc_semaphore(self.name(what))
        self.sems.append(handle)
        return handle

    def end_phase(self):
        self.nc.clear_and_free_semaphores(self.sems)
        self.nc.all_engine_barrier()
        self.sems = []

    def name(self, what):
        self.names += 1
        return f"{what}_{self.names}"


def rows(table, j=JN):
    n = table.shape[0] // P * P
    return table[0:n].rearrange("(p b j) d -> p b (j d)", p=P, j=j)


def wide(col, n):
    return col.to_broadcast([P, n])


def setup(k):
    nc, A = k.nc, k.a
    NB, COLS, T = k.NB, k.COLS, k.T
    with ExitStack() as c:
        sb = lambda n, s, d=F32: c.enter_context(nc.sbuf_tensor(k.name(n), s, d))
        sem = lambda n: k.semaphore(n)
        dst_i = sb("dst_i", [P, COLS], I32)
        nxt_i = sb("nxt_i", [P, COLS], I32)
        prv_i = sb("prv_i", [P, COLS], I32)
        src_i = sb("src_i", [P, COLS], I32)
        w_in = sb("w_in", [P, COLS])
        dst = sb("dst", [P, COLS])
        nxt = sb("nxt", [P, COLS])
        prv = sb("prv", [P, COLS])
        last = sb("last", [P, COLS])
        tmp = sb("tmp", [P, COLS])
        tmp_i = sb("tmp_i", [P, COLS], I32)
        hi = sb("hi", [P, COLS])
        lo = sb("lo", [P, COLS])
        rec = sb("rec", [P, NB, FIELDS, J], I32)
        zero = sb("zero", [1, D])
        ones = sb("cones", [P, COLS])
        first_slot_i = sb("first_slot_i", [P, 1], I32)
        first_slot = sb("first_slot", [P, 1])
        iota_i = sb("iota_i", [P, max(COLS, P)], I32)
        iota = sb("iota", [P, max(COLS, P)])
        upper = sb("upper", [P, P])
        lower = sb("lower", [P, P])
        any_end = sb("any_end", [P, 1])
        small = sb("small", [P, 4])
        hi1 = sb("hi1", [P, U, J, P], BF16)
        lo1 = sb("lo1", [P, U, J, COLS], BF16)
        hist = c.enter_context(nc.psum_tensor(k.name("hist"), [P, 512], F32))
        row_ps = c.enter_context(nc.psum_tensor(k.name("row_ps"), [P, 512], F32))
        loaded, zeroed, consts, made, stored = [sem(n) for n in ("loaded", "zeroed", "consts", "made", "stored")]
        zstored, hots, counted, rowed, done = [sem(n) for n in ("zstored", "hots", "counted", "rowed", "done")]
        split, pooled, degree, rooted = sem("split"), sem("pooled"), sem("degree"), sem("rooted")
        flat = lambda ap: ap.rearrange("(p c) -> p c", p=P)
        recf = rec[:].bitcast(F32)
        field = lambda r, f: r[:, :, f, :]
        col = lambda t: t[:].rearrange("p (b j) -> p b j", j=J)
        n_ext = k.NR
        with nc.Block() as b:

            @b.sync
            def _(sp):
                sp.dma_start(dst_i[:], flat(A["dst"][1 : 1 + n_ext])).then_inc(loaded, 16)
                sp.dma_start(nxt_i[:], flat(A["dst"][2 : 2 + n_ext])).then_inc(loaded, 16)
                sp.dma_start(prv_i[:], flat(A["dst"][0:n_ext])).then_inc(loaded, 16)
                sp.dma_start(src_i[:], flat(A["src"])).then_inc(loaded, 16)
                sp.dma_start(w_in[:], A["weight"].rearrange("(p c) o -> p (c o)", p=P)).then_inc(loaded, 16)
                sp.wait_ge(zeroed, 1)
                sp.dma_start(k.msg[k.NR : k.NR + 1, :], zero[:]).then_inc(zstored, 16)
                sp.wait_ge(made, 1)
                sp.dma_start(k.meta.rearrange("p b f j -> p (b f j)"),
                             rec[:].rearrange("p b f j -> p (b f j)")).then_inc(stored, 16)
                sp.wait_ge(stored, 16)
                sp.wait_ge(zstored, 16)

            @b.gpsimd
            def _(pool):
                pool.memset(zero[:], 0.0).then_inc(zeroed, 1)
                pool.memset(k.ident[:], 0.0).then_inc(pooled, 1)
                pool.memset(k.ones[:], 1.0).then_inc(pooled, 1)
                pool.memset(k.root[:], -0.5).then_inc(pooled, 1)
                pool.memset(upper[:], 1.0).then_inc(pooled, 1)
                pool.memset(lower[:], 1.0).then_inc(pooled, 1)
                pool.wait_ge(pooled, 5)
                pool.iota(first_slot_i[:], pattern=[[0, 1]], base=0, channel_multiplier=COLS).then_inc(consts, 1)
                pool.affine_select(out=k.ident[:], in_=k.ident[:], compare_op=ALU.not_equal, fill=1.0, base=0,
                                   pattern=[[-1, P]], channel_multiplier=1).then_inc(consts, 1)
                pool.affine_select(out=upper[:], in_=upper[:], compare_op=ALU.is_gt, fill=0.0, base=0,
                                   pattern=[[1, P]], channel_multiplier=-1).then_inc(consts, 1)
                pool.affine_select(out=lower[:], in_=lower[:], compare_op=ALU.is_gt, fill=0.0, base=0,
                                   pattern=[[-1, P]], channel_multiplier=1).then_inc(consts, 1)
                pool.iota(iota_i[:], pattern=[[1, max(COLS, P)]], base=0, channel_multiplier=0).then_inc(consts, 1)
                pool.wait_ge(degree, 1)
                pool.tensor_tensor(k.dinv[:], k.dinv[:], wide(k.root[:], COLS), ALU.pow).then_inc(rooted, 1)
                pool.wait_ge(rooted, 1)

            @b.vector
            def _(dve):
                step = Chain(dve, done)
                dve.wait_ge(loaded, 80)
                step(dve.tensor_copy(dst[:], dst_i[:]))
                step(dve.tensor_copy(nxt[:], nxt_i[:]))
                step(dve.tensor_copy(prv[:], prv_i[:]))
                step(dve.tensor_tensor(last[:], dst[:], nxt[:], ALU.not_equal))
                step(dve.tensor_copy(field(rec, SRC), col(src_i)))
                step(dve.tensor_copy(field(rec, DST), col(dst_i)))
                step(dve.tensor_copy(field(recf, WGT), col(w_in)))
                step(dve.tensor_tensor(tmp[:], dst[:], prv[:], ALU.is_equal))
                step(dve.memset(tmp[:, 0:1], 0.0))
                step(dve.tensor_copy(field(recf, SAME), col(tmp)))
                step(dve.tensor_scalar(tmp[:], dst[:], dst[:, 0:1], None, ALU.is_equal))
                step(dve.tensor_tensor(tmp[:], tmp[:], last[:], ALU.mult))
                step(dve.tensor_copy(field(recf, END), col(tmp)))
                step(dve.tensor_reduce(any_end[:], tmp[:], AX.X, ALU.add))
                dve.nop().then_inc(made, 1)
                step(dve.tensor_scalar(tmp_i[:], dst[:], 1.0 / COLS, None, ALU.mult))
                step(dve.tensor_copy(hi[:], tmp_i[:]))
                step(dve.scalar_tensor_tensor(lo[:], hi[:], -float(COLS), dst[:], ALU.mult, ALU.add))
                step(dve.tensor_scalar(tmp[:], lo[:], 0.0, None, ALU.is_lt))
                step(dve.tensor_tensor(hi[:], hi[:], tmp[:], ALU.subtract))
                step(dve.scalar_tensor_tensor(lo[:], tmp[:], float(COLS), lo[:], ALU.mult, ALU.add))
                step(dve.tensor_scalar(tmp[:], lo[:], float(COLS), None, ALU.is_ge))
                step(dve.tensor_tensor(hi[:], hi[:], tmp[:], ALU.add))
                step(dve.scalar_tensor_tensor(lo[:], tmp[:], -float(COLS), lo[:], ALU.mult, ALU.add))
                dve.wait_ge(consts, 5)
                step(dve.tensor_copy(iota[:], iota_i[:]))
                step(dve.tensor_copy(first_slot[:], first_slot_i[:]))
                step(dve.tensor_tensor(col(tmp), field(recf, END), iota[:, 0:COLS].rearrange("p (b j) -> p b j", j=J), ALU.mult))
                step(dve.tensor_reduce(small[:, 3:4], tmp[:], AX.X, ALU.add))
                step(dve.tensor_tensor(first_slot[:], first_slot[:], small[:, 3:4], ALU.add))
                dve.nop().then_inc(split, 1)
                dve.wait_ge(rowed, 1)
                step(dve.tensor_scalar(k.join_t[:], row_ps[:, 0:P], dst[:, COLS - 1 : COLS], None, ALU.is_equal))
                step(dve.tensor_tensor(k.join_t[:], k.join_t[:], upper[:], ALU.mult))
                step(dve.tensor_scalar(k.join[:], row_ps[:, P : 2 * P], dst[:, 0:1], None, ALU.is_equal))
                step(dve.tensor_tensor(k.join[:], k.join[:], lower[:], ALU.mult))
                step(dve.tensor_scalar(k.no_join[:], k.join[:], -LOW, LOW, ALU.mult, ALU.add))
                step(dve.tensor_reduce(small[:, 0:1], k.join[:], AX.X, ALU.max))
                step(dve.tensor_tensor(small[:, 0:1], small[:, 0:1], any_end[:], ALU.mult))
                step(dve.tensor_tensor(small[:, 1:2], small[:, 0:1], first_slot[:], ALU.mult))
                step(dve.tensor_scalar(small[:, 2:3], small[:, 0:1], -FAR, FAR, ALU.mult, ALU.add))
                step(dve.tensor_tensor(small[:, 1:2], small[:, 1:2], small[:, 2:3], ALU.add))
                step(dve.tensor_copy(k.join_row[:], small[:, 1:2]))
                hi3, lo3 = col(hi), col(lo)

                def body(t):
                    for u in range(U):
                        blk = t * U + u
                        wait(dve, counted, blk - U + 1)
                        for j in range(J):
                            dve.tensor_scalar(hi1[:, u, j, :], iota[:, 0:P], hi3[:, blk, j : j + 1], None, ALU.is_equal)
                            ins = dve.tensor_scalar(lo1[:, u, j, :], iota[:, 0:COLS], lo3[:, blk, j : j + 1], None, ALU.is_equal)
                        ins.then_inc(hots, 1)

                turns(dve, T, body)
                dve.wait_ge(counted, NB)
                h = hist[:, 0:COLS]
                step(dve.tensor_scalar(k.dinv[:], h, 1.0, None, ALU.add))
                dve.nop().then_inc(degree, 1)
                step(dve.tensor_scalar(tmp[:], h, 1.0, None, ALU.max))
                step(dve.reciprocal(k.rcnt[:], tmp[:]))
                step(dve.memset(ones[:], 1.0))
                step(dve.tensor_tensor_scan(hi[:], ones[:], h, 0.0, ALU.mult, ALU.add))
                dve.nop().then_inc(split, 1)
                dve.wait_ge(rowed, 2)
                step(dve.tensor_copy(small[:, 0:1], row_ps[:, 2 * P : 2 * P + 1]))
                step(dve.tensor_scalar(hi[:], hi[:], small[:, 0:1], -1.0 - k.NR, ALU.add, ALU.add))
                step(dve.tensor_scalar(tmp[:], h, 1.0, None, ALU.min))
                step(dve.tensor_tensor(hi[:], hi[:], tmp[:], ALU.mult))
                step(dve.tensor_scalar(k.last[:].rearrange("p b j -> p (b j)"), hi[:], float(k.NR), None, ALU.add))

            @b.tensor
            def _(pe):
                pe.wait_ge(consts, 1)
                pe.wait_ge(split, 1)
                pe.transpose(row_ps[:, 0:P], wide(dst[:, 0:1], P), k.ident[:])
                pe.transpose(row_ps[:, P : 2 * P], wide(dst[:, COLS - 1 : COLS], P), k.ident[:]).then_inc(rowed, 1)

                def chunk(blk, u, first, final):
                    pe.wait_ge(hots, blk + 1)
                    for j in range(J):
                        ins = pe.matmul(hist[:, 0:COLS], hi1[:, u, j, :], lo1[:, u, j, :],
                                        start=first and j == 0, stop=final and j == J - 1)
                    ins.then_inc(counted, 1)

                def body(t):
                    for u in range(U):
                        blk = t * U + u
                        chunk(blk, u, isinstance(blk, int) and blk == 0, isinstance(blk, int) and blk == NB - 1)

                turns(pe, T, body)
                pe.wait_ge(split, 2)
                pe.matmul(row_ps[:, 2 * P : 2 * P + 1], upper[:], hi[:, COLS - 1 : COLS], start=True, stop=True).then_inc(rowed, 1)


def scale_pass(k):
    nc = k.nc
    JS, US = 2 * J, 2
    TS = k.COLS // (JS * US)
    with ExitStack() as c:
        xin = c.enter_context(nc.sbuf_tensor(k.name("xin"), [P, US, JS, D], F32))
        xs = c.enter_context(nc.sbuf_tensor(k.name("xs"), [P, US, JS, D], F32))
        loaded = [k.semaphore(f"loaded{u}") for u in range(US)]
        stored = [k.semaphore(f"stored{u}") for u in range(US)]
        scaled, passed = k.semaphore("scaled"), k.semaphore("passed")
        src, dst = rows(k.a["x"], JS), rows(k.tab[0], JS)
        dinv = k.dinv[:].rearrange("p (b j) -> p b j", j=JS)
        with nc.Block() as b:

            @b.sync
            def _(sp):
                def body(t):
                    for u in range(US):
                        wait(sp, scaled, t * US + u - 1, passed)
                        sp.dma_start(xin[:, u].rearrange("p j d -> p (j d)"), src[:, t * US + u, :]).then_inc(loaded[u], 16)

                turns(sp, TS, body)

            @b.vector
            def _(dve):
                def body(t):
                    for u in range(US):
                        dve.wait_ge(loaded[u], (t + 1) * 16)
                        wait(dve, stored[u], t * 16)
                        dve.tensor_tensor(xs[:, u], xin[:, u], dinv[:, t * US + u, :].unsqueeze(2).to_broadcast([P, JS, D]),
                                          ALU.mult).then_inc(scaled, 1)

                turns(dve, TS, body)

            @b.scalar
            def _(act):
                def body(t):
                    for u in range(US):
                        act.wait_ge(scaled, t * US + u + 1)
                        act.dma_start(dst[:, t * US + u, :], xs[:, u].rearrange("p j d -> p (j d)")).then_inc(stored[u], 16)

                turns(act, TS, body)
                for u in range(US):
                    act.wait_ge(stored[u], TS * 16)


def load_records(sp, k, u, t, rec, rec_in):
    sp.dma_start(rec[:, u].rearrange("p f j -> p (f j)"),
                 k.meta[:, t * U + u].rearrange("p f j -> p (f j)")).then_inc(rec_in[u], 16)


def store_chunk(sp, k, blk, tile, out):
    sp.dma_start(rows(k.msg, J)[:, blk, :], tile.rearrange("p j d -> p (j d)")).then_inc(out, 16)


def load_and_store(sp, k, load, store):
    def body(t):
        for u in range(U):
            if not (isinstance(t, int) and t == k.T - 1 and u + LAG >= U):
                load(t + (u + LAG) // U, (u + LAG) % U)
            store(t, u)

    for u in range(LAG):
        load(0, u)
    turns(sp, k.T, body)


def sum_edges(k, table):
    nc = k.nc
    with ExitStack() as c:
        sb = lambda n, s, d=F32: c.enter_context(nc.sbuf_tensor(k.name(n), s, d))
        sem = lambda n: k.semaphore(n)
        rec = sb("rec", [P, U, FIELDS, J], I32)
        got = sb("got", [P, U, J, D])
        run = sb("run", [P, U, J, D])
        head = sb("head", [P, D])
        fix = sb("fix", [P, D])
        part = c.enter_context(nc.psum_tensor(k.name("part"), [P, 512], F32))
        rec_in = [sem(f"rec_in{u}") for u in range(U)]
        got_in = [sem(f"got_in{u}") for u in range(U)]
        put_out = [sem(f"put_out{u}") for u in range(U)]
        summed, ready, begun = sem("summed"), sem("ready"), sem("begun")
        joined, fixed, fix_out = sem("joined"), sem("fixed"), sem("fix_out")
        passed = sem("passed")
        recf = rec[:].bitcast(F32)
        T = k.T
        PER = 2 * J
        with nc.Block() as b:

            @b.sync
            def _(sp):
                def load(t, u):
                    wait(sp, summed, (t * U + u - U + 1) * PER, passed)
                    load_records(sp, k, u, t, rec, rec_in)

                def store(t, u):
                    wait(sp, summed, (t * U + u + 1) * PER, passed)
                    store_chunk(sp, k, t * U + u, run[:, u], put_out[u])

                load_and_store(sp, k, load, store)
                for u in range(U):
                    sp.wait_ge(put_out[u], T * 16)

            @b.gpsimd
            def _(pool):
                def gather(t, u):
                    wait(pool, rec_in[u], (t + 1) * 16, passed)
                    for j in range(J):
                        pool.indirect_dma_start(got[:, u, j, :], None, table,
                                                bass.IndirectOffsetOnAxis(ap=rec[:, u, SRC, j : j + 1], axis=0)).then_inc(got_in[u], 16)

                turns(pool, T, lambda t: [gather(t, u) for u in range(U)])
                pool.wait_ge(fixed, 1)
                for u in range(U):
                    pool.wait_ge(put_out[u], T * 16)
                pool.indirect_dma_start(k.msg, bass.IndirectOffsetOnAxis(ap=k.join_row[:], axis=0), fix[:], None,
                                        bounds_check=k.NR - 1, oob_is_err=False).then_inc(fix_out, 16)
                pool.wait_ge(fix_out, 16)

            @b.vector
            def _(dve):
                step = Chain(dve, summed, PER)
                begin = Chain(dve, begun)
                begin(dve.memset(run[:, U - 1, J - 1, :], 0.0))
                begin(dve.memset(head[:], 0.0))

                def body(t):
                    for u in range(U):
                        step.at(t * U + u)
                        dve.wait_ge(got_in[u], (t + 1) * 16 * J)
                        wait(dve, put_out[u], t * 16)
                        for j in range(J):
                            prev = run[:, u, j - 1, :] if j else run[:, (u - 1) % U, J - 1, :]
                            step(dve.scalar_tensor_tensor(run[:, u, j, :], prev, recf[:, u, SAME, j : j + 1], got[:, u, j, :],
                                                          ALU.mult, ALU.add))
                            step(dve.scalar_tensor_tensor(head[:], run[:, u, j, :], recf[:, u, END, j : j + 1], head[:],
                                                          ALU.mult, ALU.add))
                        step.end()

                turns(dve, T, body)
                dve.nop().then_inc(ready, 1)
                dve.wait_ge(joined, 1)
                dve.tensor_tensor(fix[:], part[:, 0:D], head[:], ALU.add).then_inc(fixed, 1)

            @b.tensor
            def _(pe):
                pe.wait_ge(ready, 1)
                pe.matmul(part[:, 0:D], k.join_t[:], run[:, U - 1, J - 1, :], start=True, stop=True).then_inc(joined, 1)


class Coef:

    def __init__(self, sb, H):
        self.H = H
        self.A = sb("cA", [P, H, J + 1])
        self.neg = sb("cneg", [P, H, J + 1])
        self.m = sb("cm", [P, H, J + 1])
        self.ex = sb("cex", [P, 2, H, J])
        self.f = sb("cf", [P, H, J + 1])
        self.a = sb("ca", [P, H, J + 1])
        self.z = sb("cz", [P, H, J + 1])
        self.rz = sb("crz", [P, H, J])
        self.b = sb("cb", [P, H, J])
        self.g = sb("cg", [P, H, J])
        self.pick = sb("cpick", [P, 2, H, J])
        self.got = sb("cgot", [P, 2 * H])
        self.head = sb("chead", [P, 2 * H])

    def begin(self, step, dve):
        step(dve.memset(self.neg[:], LOW))
        step(dve.memset(self.f[:], 0.0))
        step(dve.memset(self.A[:], 0.0))
        step(dve.memset(self.a[:], 1.0))
        step(dve.memset(self.head[:], 0.0))

    BEFORE, AFTER = 5, 11

    def before_exp(self, step, dve, same):
        H = self.H
        samw = same.unsqueeze(1).to_broadcast([P, H, J])
        flat = lambda t: t[:].rearrange("p h j -> p (h j)")
        step(dve.tensor_scalar(self.neg[:, :, 1:], samw, -LOW, LOW, ALU.mult, ALU.add))
        step(dve.tensor_tensor_scan(flat(self.m), flat(self.neg), flat(self.A), 0.0, ALU.add, ALU.max))
        step(dve.tensor_tensor(self.ex[:, 0], self.m[:, :, 0:J], self.m[:, :, 1:], ALU.subtract))
        step(dve.tensor_scalar(self.ex[:, 0], self.ex[:, 0], 0.0, None, ALU.min))
        step(dve.tensor_tensor(self.ex[:, 1], self.A[:, :, 1:], self.m[:, :, 1:], ALU.subtract))

    def after_exp(self, step, dve, same, end):
        H = self.H
        wide3 = lambda s: s.unsqueeze(1).to_broadcast([P, H, J])
        flat = lambda t: t[:].rearrange("p h j -> p (h j)")
        step(dve.tensor_tensor(self.f[:, :, 1:], self.ex[:, 0], wide3(same), ALU.mult))
        step(dve.tensor_copy(self.a[:, :, 1:], self.ex[:, 1]))
        step(dve.tensor_tensor_scan(flat(self.z), flat(self.f), flat(self.a), 0.0, ALU.mult, ALU.add))
        step(dve.reciprocal(self.rz[:], self.z[:, :, 1:]))
        step(dve.tensor_tensor(self.b[:], self.a[:, :, 1:], self.rz[:], ALU.mult))
        step(dve.tensor_tensor(self.g[:], self.f[:, :, 1:], self.z[:, :, 0:J], ALU.mult))
        step(dve.tensor_tensor(self.g[:], self.g[:], self.rz[:], ALU.mult))
        step(dve.tensor_tensor(self.pick[:, 0], self.m[:, :, 1:], wide3(end), ALU.mult))
        step(dve.tensor_tensor(self.pick[:, 1], self.z[:, :, 1:], wide3(end), ALU.mult))
        step(dve.tensor_reduce(self.got[:], self.pick[:].rearrange("p s h j -> p (s h) j"), AX.X, ALU.add))
        step(dve.tensor_tensor(self.head[:], self.head[:], self.got[:], ALU.add))

    CARRY = 2

    def carry(self, step, dve):
        step(dve.tensor_copy(self.A[:, :, 0:1], self.m[:, :, J : J + 1]))
        step(dve.tensor_copy(self.a[:, :, 0:1], self.z[:, :, J : J + 1]))


def merge_softmax(k, sb, sem, ps, co, tail, head, out, W):
    nc, H = k.nc, co.H
    e = sb("me", [P, P])
    w = sb("mw", [P, P])
    wt = sb("mwt", [P, P])
    t = sb("mt", [P, P])
    s = sb("ms", [P, 8])
    rowed, exped, exp_in, turned, weighed, untangled, summed, out_of, done = [
        sem(n) for n in ("rowed", "exped", "exp_in", "turned", "weighed", "untangled", "msummed", "out_of", "mdone")]
    tm = lambda h: co.m[:, h, J : J + 1]
    tz = lambda h: co.z[:, h, J : J + 1]
    with nc.Block() as b:

        @b.tensor
        def _(pe):
            for h in range(H):
                if h:
                    pe.wait_ge(out_of, h)
                pe.transpose(ps[0][:, 0:P], wide(tm(h), P), k.ident[:])
                pe.transpose(ps[0][:, P : 2 * P], wide(tz(h), P), k.ident[:]).then_inc(rowed, 1)
                pe.wait_ge(weighed, h + 1)
                pe.transpose(ps[1][:, 0:P], w[:], k.ident[:]).then_inc(turned, 1)
                pe.wait_ge(untangled, h + 1)
                pe.matmul(ps[2][:, 0:W], wt[:], tail[:, h, :], start=True, stop=True).then_inc(summed, 1)

        @b.scalar
        def _(act):
            for h in range(H):
                act.wait_ge(exp_in, h + 1)
                act.activation(s[:, 3:4], s[:, 2:3], ACT.Exp)
                act.activation(e[:], e[:], ACT.Exp).then_inc(exped, 1)

        @b.vector
        def _(dve):
            step = Chain(dve, done)
            for h in range(H):
                dve.wait_ge(rowed, h + 1)
                mrow, zrow = ps[0][:, 0:P], ps[0][:, P : 2 * P]
                step(dve.tensor_tensor(t[:], mrow, k.no_join[:], ALU.add))
                step(dve.tensor_reduce(s[:, 0:1], t[:], AX.X, ALU.max))
                step(dve.tensor_tensor(s[:, 1:2], s[:, 0:1], co.head[:, h : h + 1], ALU.max))
                step(dve.tensor_scalar(e[:], mrow, s[:, 1:2], 0.0, ALU.subtract, ALU.min))
                step(dve.tensor_tensor(s[:, 2:3], co.head[:, h : h + 1], s[:, 1:2], ALU.subtract))
                dve.nop().then_inc(exp_in, 1)
                dve.wait_ge(exped, h + 1)
                step(dve.tensor_tensor(w[:], e[:], k.join[:], ALU.mult))
                step(dve.tensor_tensor(w[:], w[:], zrow, ALU.mult))
                step(dve.tensor_reduce(s[:, 4:5], w[:], AX.X, ALU.add))
                step(dve.tensor_tensor(s[:, 5:6], s[:, 3:4], co.head[:, H + h : H + h + 1], ALU.mult))
                step(dve.tensor_tensor(s[:, 4:5], s[:, 4:5], s[:, 5:6], ALU.add))
                step(dve.tensor_scalar(s[:, 4:5], s[:, 4:5], 1.0e-30, None, ALU.max))
                step(dve.reciprocal(s[:, 6:7], s[:, 4:5]))
                step(dve.tensor_tensor(s[:, 7:8], s[:, 5:6], s[:, 6:7], ALU.mult))
                step(dve.tensor_scalar(w[:], w[:], s[:, 6:7], None, ALU.mult))
                dve.nop().then_inc(weighed, 1)
                dve.wait_ge(turned, h + 1)
                step(dve.tensor_copy(wt[:], ps[1][:, 0:P]))
                dve.nop().then_inc(untangled, 1)
                dve.wait_ge(summed, h + 1)
                step(dve.scalar_tensor_tensor(out[:, h, :], head[:, h, :], s[:, 7:8], ps[2][:, 0:W], ALU.mult, ALU.add))
                dve.nop().then_inc(out_of, 1)


X2 = D + 2
FEAT = (slice(0, D), slice(2, X2))
PAIR = (slice(D, X2), slice(0, 2))
SEEN = (slice(2, 2 + X2), slice(0, X2))


def fold_conv(k, l):
    nc, A = k.nc, k.a
    with ExitStack() as c:
        sb = lambda n, s, d=F32: c.enter_context(nc.sbuf_tensor(k.name(n), s, d))
        sem = lambda n: k.semaphore(n)
        wq = sb("wq", [P, 2, D])
        wk = sb("wk", [P, 2, D])
        wv = sb("wv", [P, 2, D])
        vb = sb("vb", [4, D])
        bq = sb("bq", [P, 2])
        wqt = sb("wqt", [P, 2, D])
        right = sb("right", [P, 2, X2])
        pt = [c.enter_context(nc.psum_tensor(k.name(f"pt{i}"), [P, 512], F32)) for i in range(2)]
        pm = [c.enter_context(nc.psum_tensor(k.name(f"pm{i}"), [P, 512], F32)) for i in range(2)]
        loaded, turned, copied, folded, done = [sem(n) for n in ("loaded", "turned", "copied", "folded", "done")]
        heads = lambda ap: ap.rearrange("i (h d) -> i h d", h=2)
        cols = lambda ap: ap.rearrange("(h d) -> d h", h=2)
        with nc.Block() as b:

            @b.sync
            def _(sp):
                with nc.allow_non_contiguous_dma(reason="two columns of biases"):
                    sp.dma_start(wq[:], heads(A["L1_gnn_Wq"][l])).then_inc(loaded, 16)
                    sp.dma_start(wk[:], heads(A["L1_gnn_Wk"][l])).then_inc(loaded, 16)
                    sp.dma_start(wv[:], heads(A["L1_gnn_Wv"][l])).then_inc(loaded, 16)
                    sp.dma_start(k.w_skip[:], A["L1_gnn_Wskip"][l]).then_inc(loaded, 16)
                    for h in range(2):
                        hd = slice(h * D, (h + 1) * D)
                        sp.dma_start(right[:, h, PAIR[h].start : PAIR[h].start + 1], A["L1_gnn_bk"][l, hd].unsqueeze(1)).then_inc(loaded, 16)
                        sp.dma_start(right[:, h, PAIR[h].start + 1 : PAIR[h].stop], A["L1_gnn_We"][l, 0, hd].unsqueeze(1)).then_inc(loaded, 16)
                        sp.dma_start(bq[:, h : h + 1], A["L1_gnn_bq"][l, hd].unsqueeze(1)).then_inc(loaded, 16)
                        sp.dma_start(vb[2 * h : 2 * h + 1, :], A["L1_gnn_bv"][l, hd].unsqueeze(0)).then_inc(loaded, 16)
                        sp.dma_start(vb[2 * h + 1 : 2 * h + 2, :], A["L1_gnn_We"][l, 0:1, hd]).then_inc(loaded, 16)
                    sp.dma_start(k.b_skip[0:1, :], A["L1_gnn_bskip"][l].unsqueeze(0)).then_inc(loaded, 16)
                    sp.dma_start(k.ln_g[:], A["L1_gnn_ln_g"][l].partition_broadcast(P)).then_inc(loaded, 16)
                    sp.dma_start(k.ln_b[:], A["L1_gnn_ln_b"][l].partition_broadcast(P)).then_inc(loaded, 16)
                sp.wait_ge(loaded, 16 * 17)

            @b.tensor
            def _(pe):
                pe.wait_ge(loaded, 16 * 17)
                for h in range(2):
                    pe.transpose(pt[0][:, h * D : (h + 1) * D], wq[:, h, :], k.ident[:])
                    pe.transpose(pt[1][:, h * D : (h + 1) * D], wk[:, h, :], k.ident[:]).then_inc(turned, 1)
                pe.wait_ge(copied, 2)
                for h in range(2):
                    pe.matmul(pm[0][:, h * X2 : (h + 1) * X2], wqt[:, h, :], right[:, h, :], start=True, stop=True)
                    pe.matmul(pm[1][0:1, h * X2 : (h + 1) * X2], bq[:, h : h + 1], right[:, h, :], start=True,
                              stop=True).then_inc(folded, 1)

            @b.vector
            def _(dve):
                step = Chain(dve, done)
                dve.wait_ge(loaded, 16 * 17)
                dve.wait_ge(turned, 2)
                step(dve.tensor_copy(wqt[:], pt[0][:, 0 : 2 * D].rearrange("p (h d) -> p h d", h=2)))
                dve.nop().then_inc(copied, 1)
                for h in range(2):
                    step(dve.tensor_copy(right[:, h, FEAT[h]], pt[1][:, h * D : (h + 1) * D]))
                dve.nop().then_inc(copied, 1)
                step(dve.tensor_scalar(k.w_val[:], wv[:], 0.5, None, ALU.mult))
                step(dve.tensor_scalar(k.b_val[:], vb[:], 0.5, None, ALU.mult))
                dve.wait_ge(folded, 2)
                step(dve.tensor_copy(k.w_qk[:].rearrange("p h d -> p (h d)"), pm[0][:, 0 : 2 * X2]))
                step(dve.tensor_copy(k.b_qk[:].rearrange("p h d -> p (h d)"), pm[1][0:1, 0 : 2 * X2]))


def conv_edges(k, table):
    nc, T = k.nc, k.T
    H = 2
    with ExitStack() as c:
        sb = lambda n, s, d=F32: c.enter_context(nc.sbuf_tensor(k.name(n), s, d))
        sem = lambda n: k.semaphore(n)
        psum = lambda n: c.enter_context(nc.psum_tensor(k.name(n), [P, 512], F32))
        rec = sb("rec", [P, U, FIELDS, J], I32)
        xs = sb("xs", [P, U, J, D + 4])
        xd = sb("xd", [P, U, J, D])
        xdt = sb("xdt", [P, 2, D])
        junk = sb("junk", [P, 2, H, X2])
        st = sb("st", [P, U, J, H, X2])
        at = sb("at", [P, 2, H * D])
        bt = sb("bt", [4, 2, P])
        head = sb("head", [P, H, X2])
        fix = sb("fix", [P, H, X2])
        mo = sb("mo", [P, U, J, D])
        fo = sb("fo", [P, D])
        co = Coef(sb, H)
        p_t = [psum(f"p_t{i}") for i in range(2)]
        p_y = [psum(f"p_y{i}") for i in range(2)]
        p_a = [psum(f"p_a{i}") for i in range(2)]
        p_m = [psum(f"p_m{i}") for i in range(2)]
        rec_in = [sem(f"rec_in{u}") for u in range(U)]
        got_in = [sem(f"got_in{u}") for u in range(U)]
        put_out = [sem(f"put_out{u}") for u in range(U)]
        xd_turned, xd_copied, y_made, scored = [sem(n) for n in ("xd_turned", "xd_copied", "y_made", "scored")]
        exp_in, exped, shares, weighted, st_done = [sem(n) for n in ("exp_in", "exped", "shares", "weighted", "st_done")]
        st_turned, st_copied, m_made, m_out = [sem(n) for n in ("st_turned", "st_copied", "m_made", "m_out")]
        dve_done, begun = sem("dve_done"), sem("begun")
        passed = sem("passed")
        recf = rec[:].bitcast(F32)
        PER = 2 + co.BEFORE + co.AFTER + co.CARRY + J * 3
        scale = float(D) ** -0.5

        def value_turn(pe, a, i):
            for h in range(H):
                pe.transpose(p_a[i][:, h * D : (h + 1) * D], a[:, h, FEAT[h]], k.ident[:])
            pair = a.rearrange("p h x -> p (h x)")[:, D : D + 4]
            return pe.transpose(p_a[i][0:4, 2 * D : 3 * D], pair, k.ident[:])

        def value_copy(act, i):
            act.activation(bt[:, i, :], p_a[i][0:4, 2 * D : 3 * D], ACT.Copy)
            return act.activation(at[:, i, :], p_a[i][:, 0 : 2 * D], ACT.Copy)

        def value_product(pe, i):
            pe.matmul(p_m[i][:, 0:D], at[:, i, 0:D], k.w_val[:, 0, :], start=True, stop=False)
            pe.matmul(p_m[i][:, 0:D], at[:, i, D : 2 * D], k.w_val[:, 1, :], start=False, stop=False)
            return pe.matmul(p_m[i][:, 0:D], bt[:, i, :], k.b_val[:], start=False, stop=True)

        with nc.Block() as b:

            @b.sync
            def _(sp):
                def load(t, u):
                    wait(sp, dve_done, (t * U + u - U + 1) * PER, passed)
                    load_records(sp, k, u, t, rec, rec_in)

                def store(t, u):
                    wait(sp, m_out, (t * U + u + 1) * J, passed)
                    store_chunk(sp, k, t * U + u, mo[:, u], put_out[u])

                load_and_store(sp, k, load, store)
                for u in range(U):
                    sp.wait_ge(put_out[u], T * 16)

            @b.gpsimd
            def _(pool):
                def gather(t, u):
                    wait(pool, rec_in[u], (t + 1) * 16, passed)
                    for j in range(J):
                        pool.indirect_dma_start(xs[:, u, j, 2 : 2 + D], None, table,
                                                bass.IndirectOffsetOnAxis(ap=rec[:, u, SRC, j : j + 1], axis=0)).then_inc(got_in[u], 16)
                        pool.indirect_dma_start(xd[:, u, j, :], None, table,
                                                bass.IndirectOffsetOnAxis(ap=rec[:, u, DST, j : j + 1], axis=0)).then_inc(got_in[u], 16)

                turns(pool, T, lambda t: [gather(t, u) for u in range(U)])

            @b.tensor
            def _(pe):
                def body(t):
                    for u in range(U):
                        blk = t * U + u
                        n0 = blk * J
                        pe.wait_ge(got_in[u], (t + 1) * 32 * J)

                        def turn_xd(j):
                            wait(pe, xd_copied, n0 + j - 1)
                            pe.transpose(p_t[(u * J + j) % 2][:, 0:D], xd[:, u, j, :], k.ident[:]).then_inc(xd_turned, 1)

                        turn_xd(0)
                        for j in range(J):
                            if j + 1 < J:
                                turn_xd(j + 1)
                            pe.wait_ge(xd_copied, n0 + j + 1)
                            wait(pe, scored, n0 + j - 1)
                            pe.matmul(p_y[(u * J + j) % 2][:, 0 : H * X2], xdt[:, (u * J + j) % 2, :], k.w_qk[:].rearrange("p h d -> p (h d)"),
                                      start=True, stop=False)
                            pe.matmul(p_y[(u * J + j) % 2][:, 0 : H * X2], k.ones[0:1, :], k.b_qk[:].rearrange("p h d -> p (h d)"),
                                      start=False, stop=True).then_inc(y_made, 1)

                        def turn_st(j):
                            pe.wait_ge(st_done, n0 + j + 1)
                            wait(pe, st_copied, n0 + j - 1)
                            value_turn(pe, st[:, u, j], (u * J + j) % 2).then_inc(st_turned, 1)

                        turn_st(0)
                        for j in range(J):
                            if j + 1 < J:
                                turn_st(j + 1)
                            pe.wait_ge(st_copied, n0 + j + 1)
                            wait(pe, m_out, n0 + j - 1)
                            value_product(pe, (u * J + j) % 2).then_inc(m_made, 1)

                turns(pe, T, body)

            @b.scalar
            def _(act):
                def body(t):
                    for u in range(U):
                        blk = t * U + u
                        n0 = blk * J
                        for j in range(J):
                            act.wait_ge(xd_turned, n0 + j + 1)
                            wait(act, y_made, n0 + j - 1)
                            act.activation(xdt[:, (u * J + j) % 2, :], p_t[(u * J + j) % 2][:, 0:D], ACT.Copy).then_inc(xd_copied, 1)
                        act.wait_ge(exp_in, blk + 1)
                        act.activation(co.ex[:], co.ex[:], ACT.Exp).then_inc(exped, 1)
                        act.wait_ge(shares, blk + 1)
                        wait(act, st_turned, (blk - U + 1) * J)
                        for j in range(J):
                            act.activation(st[:, u, j, 0, :], xs[:, u, j, SEEN[0]], ACT.Copy, scale=co.b[:, 0, j : j + 1])
                            act.activation(st[:, u, j, 1, :], xs[:, u, j, SEEN[1]], ACT.Copy,
                                           scale=co.b[:, 1, j : j + 1]).then_inc(weighted, 1)
                        wait(act, put_out[u], t * 16)

                        def evac(j):
                            act.wait_ge(m_made, n0 + j + 1)
                            act.activation(mo[:, u, j, :], p_m[(u * J + j) % 2][:, 0:D], ACT.Copy).then_inc(m_out, 1)

                        for j in range(J):
                            act.wait_ge(st_turned, n0 + j + 1)
                            wait(act, m_made, n0 + j - 1)
                            value_copy(act, (u * J + j) % 2).then_inc(st_copied, 1)
                            if j:
                                evac(j - 1)
                        evac(J - 1)

                turns(act, T, body)

            @b.vector
            def _(dve):
                begin = Chain(dve, begun)
                co.begin(begin, dve)
                begin(dve.memset(head[:], 0.0))
                begin(dve.memset(st[:, U - 1, J - 1], 0.0))
                for at_ in (0, D + 2):
                    begin(dve.memset(xs[:, :, :, at_ : at_ + 1], 1.0))
                step = Chain(dve, dve_done, PER)

                def body(t):
                    for u in range(U):
                        blk = t * U + u
                        step.at(blk)
                        n0 = blk * J
                        same, end = recf[:, u, SAME, :], recf[:, u, END, :]
                        dve.wait_ge(got_in[u], (t + 1) * 32 * J)
                        wait(dve, weighted, (blk - U + 1) * J)
                        for at_ in (1, D + 3):
                            step(dve.tensor_copy(xs[:, u, :, at_ : at_ + 1], recf[:, u, WGT, :].unsqueeze(2)))
                        for j in range(J):
                            dve.wait_ge(y_made, n0 + j + 1)
                            wait(dve, scored, n0 + j - 1)
                            dve.tensor_tensor_reduce(junk[:, (u * J + j) % 2, 0], p_y[(u * J + j) % 2][:, 0:X2], xs[:, u, j, SEEN[0]], scale, 0.0, ALU.mult,
                                                     ALU.add, co.A[:, 0, 1 + j : 2 + j])
                            ins = dve.tensor_tensor_reduce(junk[:, (u * J + j) % 2, 1], p_y[(u * J + j) % 2][:, X2 : 2 * X2], xs[:, u, j, SEEN[1]], scale, 0.0,
                                                           ALU.mult, ALU.add, co.A[:, 1, 1 + j : 2 + j])
                            ins.then_inc(scored, 1)
                        dve.wait_ge(scored, n0 + J)
                        co.before_exp(step, dve, same)
                        dve.nop().then_inc(exp_in, 1)
                        dve.wait_ge(exped, blk + 1)
                        co.after_exp(step, dve, same, end)
                        dve.nop().then_inc(shares, 1)
                        co.carry(step, dve)
                        for j in range(J):
                            dve.wait_ge(weighted, n0 + j + 1)
                            prev = st[:, u, j - 1] if j else st[:, (u - 1) % U, J - 1]
                            for h in range(H):
                                step(dve.scalar_tensor_tensor(st[:, u, j, h, :], prev[:, h, :], co.g[:, h, j : j + 1],
                                                              st[:, u, j, h, :], ALU.mult, ALU.add))
                            dve.nop().then_inc(st_done, 1)
                            step(dve.scalar_tensor_tensor(head[:], st[:, u, j], end[:, j : j + 1], head[:], ALU.mult, ALU.add))
                        step.end()

                turns(dve, T, body)

        merge_softmax(k, sb, sem, [p_t[0], p_t[1], p_y[0]], co, st[:, U - 1, J - 1], head, fix, X2)
        f_turned, f_copied, f_made, f_out, f_put = [sem(n) for n in ("f_turned", "f_copied", "f_made", "f_out", "f_put")]
        with nc.Block() as b:

            @b.tensor
            def _(pe):
                value_turn(pe, fix[:], 0).then_inc(f_turned, 1)
                pe.wait_ge(f_copied, 1)
                value_product(pe, 0).then_inc(f_made, 1)

            @b.scalar
            def _(act):
                act.wait_ge(f_turned, 1)
                value_copy(act, 0).then_inc(f_copied, 1)
                act.wait_ge(f_made, 1)
                act.activation(fo[:], p_m[0][:, 0:D], ACT.Copy).then_inc(f_out, 1)

            @b.gpsimd
            def _(pool):
                pool.wait_ge(f_out, 1)
                pool.indirect_dma_start(k.msg, bass.IndirectOffsetOnAxis(ap=k.join_row[:], axis=0), fo[:], None,
                                        bounds_check=k.NR - 1, oob_is_err=False).then_inc(f_put, 16)
                pool.wait_ge(f_put, 16)


def angle_edges(k, table):
    nc, T, A = k.nc, k.T, k.a
    H, W = 8, 16
    with ExitStack() as c:
        sb = lambda n, s, d=F32: c.enter_context(nc.sbuf_tensor(k.name(n), s, d))
        sem = lambda n: k.semaphore(n)
        psum = lambda n: c.enter_context(nc.psum_tensor(k.name(n), [P, 512], F32))
        rec = sb("rec", [P, U, FIELDS, J], I32)
        x3 = sb("x3", [P, 3, U, J, D])
        x3t = sb("x3t", [P, 2, 3 * D])
        q = sb("q", [P, 2, D])
        prod = sb("prod", [P, D])
        st = sb("st", [P, U, J, D])
        kept = sb("kept", [P, D])
        carry = sb("carry", [P, D])
        head = sb("head", [P, H, W])
        fix = sb("fix", [P, H, W])
        w_kv = sb("w_kv", [P, 2, D])
        w_q = sb("w_q", [P, D])
        w_ee = sb("w_ee", [P, D])
        b_q = sb("b_q", [P, D])
        b_kv = sb("b_kv", [1, 2 * D])
        co = Coef(sb, H)
        p_t = [psum(f"p_t{i}") for i in range(2)]
        p_q = [psum(f"p_q{i}") for i in range(2)]
        p_v = [psum(f"p_v{i}") for i in range(2)]
        rec_in = [sem(f"rec_in{u}") for u in range(U)]
        edge_in = [sem(f"edge_in{u}") for u in range(U)]
        got_in = [sem(f"got_in{u}") for u in range(U)]
        put_out = [sem(f"put_out{u}") for u in range(U)]
        w_in, turned, copied, made, v_out = [sem(n) for n in ("w_in", "turned", "copied", "made", "v_out")]
        exp_in, exped, st_done, scored = [sem(n) for n in ("exp_in", "exped", "st_done", "scored")]
        dve_done, begun, f_put = sem("dve_done"), sem("begun"), sem("f_put")
        passed = sem("passed")
        recf = rec[:].bitcast(F32)
        PER = J * 3 + co.BEFORE + co.AFTER + co.CARRY + 1 + J * 3
        scale = float(W) ** -0.5
        edge = rows(A["edge"], J)
        heads = lambda ap: ap.rearrange("p (h w) -> p h w", h=H)
        with nc.Block() as b:

            @b.sync
            def _(sp):
                sp.dma_start(w_kv[:, 0, :], A["L3_gnn_Wk"]).then_inc(w_in, 16)
                sp.dma_start(w_kv[:, 1, :], A["L3_gnn_Wv"]).then_inc(w_in, 16)
                sp.dma_start(w_q[:], A["L3_gnn_Wq"]).then_inc(w_in, 16)
                sp.dma_start(w_ee[:], A["L3_gnn_We"]).then_inc(w_in, 16)
                sp.dma_start(b_q[:], A["L3_gnn_bq"].partition_broadcast(P)).then_inc(w_in, 16)
                sp.dma_start(b_kv[:, 0:D], A["L3_gnn_bk"].unsqueeze(0)).then_inc(w_in, 16)
                sp.dma_start(b_kv[:, D : 2 * D], A["L3_gnn_bv"].unsqueeze(0)).then_inc(w_in, 16)

                def load(t, u):
                    wait(sp, dve_done, (t * U + u - U + 1) * PER, passed)
                    load_records(sp, k, u, t, rec, rec_in)
                    sp.dma_start(x3[:, 2, u].rearrange("p j d -> p (j d)"), edge[:, t * U + u, :]).then_inc(edge_in[u], 16)

                def store(t, u):
                    wait(sp, st_done, t * U + u + 1, passed)
                    store_chunk(sp, k, t * U + u, st[:, u], put_out[u])

                load_and_store(sp, k, load, store)
                for u in range(U):
                    sp.wait_ge(put_out[u], T * 16)

            @b.gpsimd
            def _(pool):
                def gather(t, u):
                    wait(pool, rec_in[u], (t + 1) * 16, passed)
                    for j in range(J):
                        for s, f in ((0, SRC), (1, DST)):
                            pool.indirect_dma_start(x3[:, s, u, j, :], None, table,
                                                    bass.IndirectOffsetOnAxis(ap=rec[:, u, f, j : j + 1], axis=0)).then_inc(got_in[u], 16)

                turns(pool, T, lambda t: [gather(t, u) for u in range(U)])

            @b.tensor
            def _(pe):
                pe.wait_ge(w_in, 16 * 7)

                def body(t):
                    for u in range(U):
                        n0 = (t * U + u) * J
                        pe.wait_ge(got_in[u], (t + 1) * 32 * J)
                        pe.wait_ge(edge_in[u], (t + 1) * 16)

                        def turn(j):
                            wait(pe, copied, n0 + j - 1)
                            for s in range(3):
                                ins = pe.transpose(p_t[(u * J + j) % 2][:, s * D : (s + 1) * D], x3[:, s, u, j, :], k.ident[:])
                            ins.then_inc(turned, 1)

                        turn(0)
                        for j in range(J):
                            if j + 1 < J:
                                turn(j + 1)
                            pe.wait_ge(copied, n0 + j + 1)
                            wait(pe, v_out, n0 + j - 1)
                            wait(pe, scored, n0 + j - 1)
                            tj = x3t[:, (u * J + j) % 2, :]
                            pe.matmul(p_q[(u * J + j) % 2][:, 0:D], tj[:, D : 2 * D], w_q[:], start=True, stop=True)
                            for s, o in enumerate((p_q[(u * J + j) % 2][:, D : 2 * D], p_v[(u * J + j) % 2][:, 0:D])):
                                pe.matmul(o, tj[:, 0:D], w_kv[:, s, :], start=True, stop=False)
                                pe.matmul(o, tj[:, 2 * D : 3 * D], w_ee[:], start=False, stop=False)
                                ins = pe.matmul(o, k.ones[0:1, :], b_kv[:, s * D : (s + 1) * D], start=False, stop=True)
                            ins.then_inc(made, 1)

                turns(pe, T, body)

            @b.scalar
            def _(act):
                def body(t):
                    for u in range(U):
                        blk = t * U + u
                        n0 = blk * J

                        def values(j):
                            act.wait_ge(made, n0 + j + 1)
                            act.activation(st[:, u, j, :], p_v[(u * J + j) % 2][:, 0:D], ACT.Copy).then_inc(v_out, 1)

                        for j in range(J):
                            act.wait_ge(turned, n0 + j + 1)
                            wait(act, made, n0 + j - 1)
                            act.activation(x3t[:, (u * J + j) % 2, :], p_t[(u * J + j) % 2][:, 0 : 3 * D], ACT.Copy).then_inc(copied, 1)
                            if j == 0:
                                wait(act, put_out[u], t * 16)
                            else:
                                values(j - 1)
                        values(J - 1)
                        act.wait_ge(exp_in, blk + 1)
                        act.activation(co.ex[:], co.ex[:], ACT.Exp).then_inc(exped, 1)

                turns(act, T, body)

            @b.vector
            def _(dve):
                begin = Chain(dve, begun)
                co.begin(begin, dve)
                begin(dve.memset(head[:], 0.0))
                begin(dve.memset(st[:, U - 1, J - 1], 0.0))
                begin(dve.memset(kept[:], 0.0))
                dve.wait_ge(w_in, 16 * 7)
                step = Chain(dve, dve_done, PER)

                def body(t):
                    for u in range(U):
                        blk = t * U + u
                        step.at(blk)
                        n0 = blk * J
                        same, end = recf[:, u, SAME, :], recf[:, u, END, :]
                        dve.wait_ge(rec_in[u], (t + 1) * 16)
                        for j in range(J):
                            dve.wait_ge(made, n0 + j + 1)
                            step(dve.tensor_tensor(q[:, (u * J + j) % 2, :], p_q[(u * J + j) % 2][:, 0:D], b_q[:], ALU.add))
                            step(dve.scalar_tensor_tensor(prod[:], q[:, (u * J + j) % 2, :], scale, p_q[(u * J + j) % 2][:, D : 2 * D], ALU.mult, ALU.mult))
                            dve.nop().then_inc(scored, 1)
                            step(dve.tensor_reduce(co.A[:, :, 1 + j : 2 + j], heads(prod[:]), AX.X, ALU.add))
                        co.before_exp(step, dve, same)
                        dve.nop().then_inc(exp_in, 1)
                        dve.wait_ge(exped, blk + 1)
                        co.after_exp(step, dve, same, end)
                        co.carry(step, dve)
                        dve.wait_ge(v_out, n0 + J)
                        step(dve.tensor_tensor(st[:, u].rearrange("p j (h w) -> p j h w", h=H),
                                               st[:, u].rearrange("p j (h w) -> p j h w", h=H),
                                               co.b[:].rearrange("p h j -> p j h").unsqueeze(3).to_broadcast([P, J, H, W]), ALU.mult))
                        for j in range(J):
                            prev = st[:, u, j - 1, :] if j else carry[:]
                            step(dve.tensor_tensor(heads(kept[:]), heads(prev), co.g[:, :, j : j + 1].to_broadcast([P, H, W]), ALU.mult))
                            step(dve.tensor_tensor(st[:, u, j, :], st[:, u, j, :], kept[:], ALU.add))
                            step(dve.scalar_tensor_tensor(head[:].rearrange("p h w -> p (h w)"), st[:, u, j, :], end[:, j : j + 1],
                                                          head[:].rearrange("p h w -> p (h w)"), ALU.mult, ALU.add))
                        dve.tensor_copy(carry[:], st[:, u, J - 1, :]).then_inc(st_done, 1)
                        dve.wait_ge(st_done, blk + 1)
                        step.end()

                dve.memset(carry[:], 0.0).then_inc(begun, 1)
                dve.wait_ge(begun, begin.n + 1)
                turns(dve, T, body)

        merge_softmax(k, sb, sem, [p_t[0], p_t[1], p_q[0]], co, heads(carry[:]), head, fix, W)
        with nc.Block() as b:

            @b.gpsimd
            def _(pool):
                pool.indirect_dma_start(k.msg, bass.IndirectOffsetOnAxis(ap=k.join_row[:], axis=0),
                                        fix[:].rearrange("p h w -> p (h w)"), None,
                                        bounds_check=k.NR - 1, oob_is_err=False).then_inc(f_put, 16)
                pool.wait_ge(f_put, 16)


class Chunk:

    def __init__(self, k, t, u, lag=0):
        self.t, self.u = t, u + lag
        self.n = t * UB + self.u
        self.there = not isinstance(t, int) or 0 <= self.n < k.NB

    def slot(self, ring):
        return self.u % ring

    def use(self, ring):
        return self.t * (UB // ring) + self.u // ring


class Steps:

    def __init__(self, eng, sem):
        self.eng, self.sem, self.per, self.base, self.n = eng, sem, None, 0, 0

    def at(self, chunk):
        self.base, self.n = (0 if self.per is None else chunk.n * self.per), 0

    def __call__(self, *independent):
        for ins in independent:
            ins.then_inc(self.sem, 1)
        self.n += len(independent)
        self.eng.wait_ge(self.sem, self.base + self.n)

    def before_form_without_wait(self, passed):
        if not isinstance(self.base, int):
            self.eng.sem_inc(passed, 1)

    def end(self):
        assert self.per in (None, self.n)
        self.per = self.n


class Norm:

    def __init__(self, k, c, i):
        sb = lambda n, s, d=F32: c.enter_context(k.nc.sbuf_tensor(k.name(n), s, d))
        self.k = k
        self.raw = sb(f"raw{i}", [P, JN, 6])
        self.mv = sb(f"mv{i}", [P, JN, 2])
        self.s = sb(f"norm{i}", [P, RING, 3, JN])
        self.passed = k.semaphore(f"passed{i}")
        self.radicand, self.powed = k.semaphore(f"radicand{i}"), k.semaphore(f"powed{i}")
        self.rooted, self.applied = k.semaphore(f"rooted{i}"), k.semaphore(f"applied{i}")

    def stats(self, dve, step, c, v):
        s = self.s[:, c.slot(RING)]
        step(*[dve.bn_stats(out=self.raw[:, r, :], in_=v[:, r, :]) for r in range(JN)])
        step.before_form_without_wait(self.passed)
        step(*[dve.bn_aggr(out=self.mv[:, r, :], in_=self.raw[:, r, :]) for r in range(JN)])
        wait(dve, self.applied, c.n - RING + 1)
        step(dve.tensor_scalar(s[:, 0, :], self.mv[:, :, 0], -1.0, None, ALU.mult),
             dve.tensor_scalar(s[:, 1, :], self.mv[:, :, 1], EPS, None, ALU.add))
        dve.nop().then_inc(self.radicand, 1)

    def root(self, pool, c):
        s = self.s[:, c.slot(RING)]
        pool.wait_ge(self.radicand, c.n + 1)
        pool.tensor_tensor(s[:, 1, :], s[:, 1, :], wide(self.k.root[:], JN), ALU.pow).then_inc(self.powed, 1)
        pool.wait_ge(self.powed, c.n + 1)
        pool.tensor_tensor(s[:, 2, :], s[:, 0, :], s[:, 1, :], ALU.mult).then_inc(self.rooted, 1)

    def apply(self, act, c, v, o, then=None):
        s = self.s[:, c.slot(RING)]
        act.wait_ge(self.rooted, c.n + 1)
        for r in range(JN):
            ins = act.activation(o[:, r, :], v[:, r, :], ACT.Identity, bias=s[:, 2, r : r + 1], scale=s[:, 1, r : r + 1])
        ins.then_inc(self.applied, 1)


class Nodes:

    def __init__(self, k, c, n_in, n_out, n_src, message=1):
        nc = self.nc = k.nc
        self.k, self.c = k, c
        sem = lambda n: k.semaphore(n)
        psum = lambda n: c.enter_context(nc.psum_tensor(k.name(n), [P, 512], F32))
        self.x = [self.ring(f"in{i}", UB) for i in range(n_in)]
        self.o = [self.ring(f"out{i}", RING) for i in range(n_out)]
        self.n_in, self.n_out, self.n_src = n_in - message, n_out, n_src
        if n_src:
            self.z = self.ring("z", RING)
            self.xt = c.enter_context(nc.sbuf_tensor(k.name("xt"), [P, 2, n_src, 4 * D], F32))
            self.p_t = [[psum(f"p_t{i}{s}") for s in range(n_src)] for i in range(2)]
            self.p_m = [psum(f"p_m{i}") for i in range(2)]
        self.loaded = [sem(f"loaded{u}") for u in range(UB)]
        self.stored = [sem(f"stored{u}") for u in range(RING)]
        self.prepped, self.turned, self.copied = sem("prepped"), sem("turned"), sem("copied")
        self.made, self.z_in, self.passed = sem("made"), sem("z_in"), sem("passed")
        self.finished, self.idx_in = sem("finished"), sem("idx_in")
        self.got = [sem(f"got{u}") for u in range(UB)]
        self.idx = c.enter_context(nc.sbuf_tensor(k.name("idx"), [P, UB, JN], I32))
        self.z_free = None

    def ring(self, name, n, d=D):
        return self.c.enter_context(self.nc.sbuf_tensor(self.k.name(name), [P, n, JN, d], F32))

    def wait_loaded(self, eng, c):
        eng.wait_ge(self.loaded[c.slot(UB)], (c.use(UB) + 1) * 16 * self.n_in)

    def wait_message(self, eng, c):
        eng.wait_ge(self.got[c.slot(UB)], (c.use(UB) + 1) * 16 * JN)

    def wait_stored(self, eng, c):
        wait(eng, self.stored[c.slot(RING)], c.use(RING) * 16 * self.n_out)

    def walk(self, eng, one):
        for u in range(-LEAD, 0):
            one(0, u)

        def body(t):
            for u in range(UB):
                one(t, u)

        turns(eng, self.k.TN, body)
        for u in range(UB, UB + DRAIN):
            one(self.k.TN - 1, u)

    def run(self, ins, outs, srcs, weights, bias, dve_stages, act_stages, pool_stages, prep=False, pe_stages=(), begin=None):
        k, nc, n_src = self.k, self.nc, self.n_src
        chunk = lambda t, u, lag=0: Chunk(k, t, u, lag)

        def run_stages(eng, stages, t, u):
            for lag, stage in stages:
                c = chunk(t, u, lag)
                if c.there:
                    stage(eng, c)

        with nc.Block() as b:

            @b.sync
            def _(sp):
                def one(t, u):
                    c = chunk(t, u, AHEAD)
                    if c.there:
                        wait(sp, self.finished, c.n - UB + 1, self.passed)
                        for i, table in enumerate(ins):
                            if table is k.msg:
                                continue
                            sp.dma_start(self.x[i][:, c.slot(UB)].rearrange("p j d -> p (j d)"),
                                         rows(table)[:, c.n, :]).then_inc(self.loaded[c.slot(UB)], 16)
                    c = chunk(t, u, -DRAIN)
                    if c.there:
                        wait(sp, self.finished, c.n + 1, self.passed)
                        for i, table in enumerate(outs):
                            sp.dma_start(rows(table)[:, c.n, :],
                                         self.o[i][:, c.slot(RING)].rearrange("p j d -> p (j d)")).then_inc(self.stored[c.slot(RING)], 16)

                self.walk(sp, one)
                for u in range(RING):
                    sp.wait_ge(self.stored[u], k.NB // RING * 16 * len(outs))

            @b.tensor
            def _(pe):
                def turn(c, g):
                    a, z = GROUPS[g]
                    if g == 0:
                        self.wait_loaded(pe, c)
                        if prep:
                            pe.wait_ge(self.prepped, c.n + 1)
                    wait(pe, self.copied, c.n * NG + g - 1)
                    for s, x in enumerate(srcs(c)):
                        for r in range(a, z):
                            ins_ = pe.transpose(self.p_t[g % 2][s][:, (r - a) * D : (r - a + 1) * D], x[:, r, :], k.ident[:])
                    ins_.then_inc(self.turned, 1)

                def product(c, g):
                    a, z = GROUPS[g]
                    pe.wait_ge(self.copied, c.n * NG + g + 1)
                    wait(pe, self.z_in, c.n * NG + g - 1)
                    for r in range(z - a):
                        o = self.p_m[g % 2][:, r * D : (r + 1) * D]
                        for s in range(n_src):
                            pe.matmul(o, self.xt[:, g % 2, s, r * D : (r + 1) * D], weights[s][:], start=s == 0, stop=False)
                        ins_ = pe.matmul(o, k.ones[0:1, :], bias[0:1, :], start=False, stop=True)
                    ins_.then_inc(self.made, 1)

                def one(t, u):
                    if n_src:
                        for g in range(NG):
                            nxt = chunk(t, u, 1 + (g + 1) // NG)
                            if nxt.there:
                                turn(nxt, (g + 1) % NG)
                            c = chunk(t, u, 1)
                            if c.there:
                                product(c, g)
                    run_stages(pe, pe_stages, t, u)

                self.walk(pe, one)

            @b.scalar
            def _(act):
                def carry_turned(c, g):
                    a, z = GROUPS[g]
                    act.wait_ge(self.turned, c.n * NG + g + 1)
                    wait(act, self.made, c.n * NG + g - 1)
                    for s in range(n_src):
                        ins_ = act.activation(self.xt[:, g % 2, s, 0 : (z - a) * D], self.p_t[g % 2][s][:, 0 : (z - a) * D], ACT.Copy)
                    ins_.then_inc(self.copied, 1)

                def carry_product(c, g):
                    a, z = GROUPS[g]
                    act.wait_ge(self.made, c.n * NG + g + 1)
                    if g == 0 and self.z_free is not None:
                        wait(act, self.z_free, c.n - RING + 1)
                    act.activation(self.z[:, c.slot(RING), a:z, :].rearrange("p j d -> p (j d)"),
                                   self.p_m[g % 2][:, 0 : (z - a) * D], ACT.Copy).then_inc(self.z_in, 1)

                def one(t, u):
                    half = len(act_stages) // 2
                    for g in range(NG):
                        if n_src:
                            nxt = chunk(t, u, 1 + (g + 1) // NG)
                            if nxt.there:
                                carry_turned(nxt, (g + 1) % NG)
                        run_stages(act, act_stages[:half] if g == 0 else act_stages[half:], t, u)
                        if n_src:
                            c = chunk(t, u, 1)
                            if c.there:
                                carry_product(c, g)

                self.walk(act, one)

            @b.gpsimd
            def _(pool):
                def gather(c, js):
                    for j in js:
                        pool.indirect_dma_start(x[:, c.slot(UB), j, :], None, k.msg,
                                                bass.IndirectOffsetOnAxis(ap=self.idx[:, c.slot(UB), j : j + 1], axis=0)).then_inc(self.got[c.slot(UB)], 16)

                def begin_message(pool, c):
                    wait(pool, self.finished, c.n - UB + 1, self.passed)
                    pool.tensor_copy(self.idx[:, c.slot(UB), :], k.last[:, c.n, :]).then_inc(self.idx_in, 1)
                    wait(pool, self.idx_in, c.n + 1, self.passed)
                    gather(c, range(0, JN // 2))

                def end_message(pool, c):
                    gather(c, range(JN // 2, JN))

                stages = list(pool_stages)
                if any(table is k.msg for table in ins):
                    x = self.x[[table is k.msg for table in ins].index(True)]
                    half = (len(stages) + 1) // 2
                    stages = [(AHEAD, begin_message)] + stages[:half] + [(AHEAD, end_message)] + stages[half:]
                self.walk(pool, lambda t, u: run_stages(pool, stages, t, u))

            @b.vector
            def _(dve):
                if begin:
                    begin(dve)
                steps = [Steps(dve, k.semaphore(f"done{i}")) for i in range(len(dve_stages))]

                def one(t, u):
                    for step, (lag, stage) in zip(steps, dve_stages):
                        c = chunk(t, u, lag)
                        if c.there:
                            step.at(c)
                            stage(dve, step, c)
                            step.end()

                self.walk(dve, one)

    def wait_z(self, dve, c):
        dve.wait_ge(self.z_in, (c.n + 1) * NG)


def load_rows(k, pairs):
    nc = k.nc
    with ExitStack() as c:
        loaded = k.semaphore("loaded")
        with nc.Block() as b:

            @b.sync
            def _(sp):
                for tile, ap in pairs:
                    sp.dma_start(tile, ap).then_inc(loaded, 16)
                sp.wait_ge(loaded, 16 * len(pairs))


def gcn_nodes(k):
    nc, A = k.nc, k.a
    bc = lambda n: A[n].partition_broadcast(P)
    with ExitStack() as c:
        sb = lambda n, s: c.enter_context(nc.sbuf_tensor(k.name(n), s, F32))
        g2, b2 = sb("g2", [P, D]), sb("b2", [P, D])
        load_rows(k, [(k.w_skip[:], A["L0_gnn_W"]), (k.b_skip[0:1, :], A["L0_gnn_b"].unsqueeze(0)),
                      (k.ln_g[:], bc("L0_gnn_ln_gamma")), (k.ln_b[:], bc("L0_gnn_ln_beta")),
                      (g2[:], bc("L1_gnn_ln_in_g")), (b2[:], bc("L1_gnn_ln_in_b"))])
        n = Nodes(k, c, 3, 2, 1)
        first, second, third = [Norm(k, c, i) for i in range(3)]
        summed, y = n.ring("summed", 4), n.ring("y", RING)
        dinv = k.dinv[:].rearrange("p (b j) -> p b j", j=JN)
        R = lambda t, c: t[:, c.slot(RING)]
        every = lambda g: g[:].unsqueeze(1).to_broadcast([P, JN, D])

        def prep(dve, step, c):
            n.wait_loaded(dve, c)
            n.wait_message(dve, c)
            i, o = c.slot(UB), summed[:, c.slot(4)]
            wait(dve, n.turned, (c.n - 3) * NG)
            step(dve.tensor_tensor(o, n.x[0][:, i], n.x[1][:, i], ALU.add))
            step(dve.tensor_tensor(o, o, dinv[:, c.n, :].unsqueeze(2).to_broadcast([P, JN, D]), ALU.mult))
            dve.nop().then_inc(n.prepped, 1)

        def gcn(dve, step, c):
            n.wait_z(dve, c)
            first.stats(dve, step, c, R(n.z, c))

        def residual(dve, step, c):
            v = R(y, c)
            dve.wait_ge(first.applied, c.n + 1)
            step(dve.tensor_tensor(v, v, every(k.ln_g), ALU.mult))
            step(dve.tensor_tensor(v, v, every(k.ln_b), ALU.add))
            step(dve.scalar_tensor_tensor(v, v, 0.0, n.x[2][:, c.slot(UB)], ALU.max, ALU.add))
            second.stats(dve, step, c, v)

        def again(dve, step, c):
            dve.wait_ge(second.applied, c.n + 1)
            third.stats(dve, step, c, R(n.o[0], c))

        def finish(dve, step, c):
            o = R(n.o[1], c)
            dve.wait_ge(third.applied, c.n + 1)
            step(dve.tensor_tensor(o, o, every(g2), ALU.mult))
            step(dve.tensor_tensor(o, o, every(b2), ALU.add))
            dve.nop().then_inc(n.finished, 1)

        def apply_second(act, c):
            n.wait_stored(act, c)
            second.apply(act, c, R(y, c), R(n.o[0], c))

        n.z_free = first.applied
        n.run([k.msg, k.tab[0], A["x"]], [k.res, k.tab[1]], lambda c: [summed[:, c.slot(4)]], [k.w_skip], k.b_skip,
              [(-3, finish), (-2, again), (-1, residual), (0, gcn), (2, prep)],
              [(-2, lambda act, c: third.apply(act, c, R(n.o[0], c), R(n.o[1], c))), (-1, apply_second),
               (0, lambda act, c: first.apply(act, c, R(n.z, c), R(y, c)))],
              [(-2, third.root), (-1, second.root), (0, first.root)], prep=True)


def conv_nodes(k, src, dst, last):
    nc = k.nc
    with ExitStack() as c:
        n = Nodes(k, c, 3 if last else 2, 1, 1)
        e, y = n.ring("e", RING), n.ring("y", RING)
        norms = [Norm(k, c, i) for i in range(2 if last else 1)]
        e_in, e_out = k.semaphore("e_in"), k.semaphore("e_out")
        R = lambda t, c: t[:, c.slot(RING)]
        every = lambda g: g[:].unsqueeze(1).to_broadcast([P, JN, D])

        def message(dve, step, c):
            z = R(n.z, c)
            n.wait_z(dve, c)
            n.wait_message(dve, c)
            step(dve.tensor_tensor(z, z, n.x[1][:, c.slot(UB)], ALU.add))
            step(dve.tensor_scalar(R(e, c), z, 0.0, None, ALU.min))
            dve.nop().then_inc(e_in, 1)

        def exponential(act, c):
            act.wait_ge(e_in, c.n + 1)
            act.activation(R(e, c), R(e, c), ACT.Exp).then_inc(e_out, 1)

        def residual(dve, step, c):
            z, v = R(n.z, c), R(y, c)
            dve.wait_ge(e_out, c.n + 1)
            step(dve.scalar_tensor_tensor(v, z, 0.0, R(e, c), ALU.max, ALU.add))
            step(dve.scalar_tensor_tensor(v, v, -1.0, n.x[0][:, c.slot(UB)], ALU.add, ALU.add))
            norms[0].stats(dve, step, c, v)

        def affine(dve, step, c):
            v = R(y if last else n.o[0], c)
            dve.wait_ge(norms[0].applied, c.n + 1)
            step(dve.tensor_tensor(v, v, every(k.ln_g), ALU.mult))
            step(dve.tensor_tensor(v, v, every(k.ln_b), ALU.add))
            if last:
                step(dve.tensor_tensor(v, v, n.x[2][:, c.slot(UB)], ALU.add))
                norms[1].stats(dve, step, c, v)
            else:
                dve.nop().then_inc(n.finished, 1)

        def apply_first(act, c):
            if not last:
                n.wait_stored(act, c)
            norms[0].apply(act, c, R(y, c), R(y if last else n.o[0], c))

        def apply_last(act, c):
            n.wait_stored(act, c)
            norms[1].apply(act, c, R(y, c), R(n.o[0], c))

        n.z_free = norms[0].radicand
        if last:
            n.finished = norms[1].applied
        n.run([src, k.msg] + ([k.res] if last else []), [dst], lambda c: [n.x[0][:, c.slot(UB)]], [k.w_skip], k.b_skip,
              [(-2, affine), (-1, residual), (0, message)],
              ([(-2, apply_last)] if last else []) + [(-1, apply_first), (0, exponential)],
              ([(-2, norms[1].root)] if last else []) + [(-1, norms[0].root)])


def sage_nodes(k):
    nc, A = k.nc, k.a
    with ExitStack() as c:
        sb = lambda n, s, d=F32: c.enter_context(nc.sbuf_tensor(k.name(n), s, d))
        sem = lambda n: k.semaphore(n)
        w = sb("w", [P, 2, D])
        wt = sb("wt", [P, 2, D])
        gb = sb("gb", [1, 2, D])
        real_i = sb("real_i", [P, k.COLS], I32)
        real = sb("real", [P, k.COLS])
        load_rows(k, [(w[:, 0, :], A["L2_gnn_W_l"]), (w[:, 1, :], A["L2_gnn_W_r"]), (k.b_skip[0:1, :], A["L2_gnn_b_l"].unsqueeze(0)),
                      (gb[:, 0, :], A["L2_gnn_gamma"].unsqueeze(0)), (gb[:, 1, :], A["L2_gnn_beta"].unsqueeze(0))])
        with ExitStack() as c2:
            turned, row_no, done = [k.semaphore(s) for s in ("turned", "row_no", "done")]
            pw = c2.enter_context(nc.psum_tensor(k.name("pw"), [P, 512], F32))
            with nc.Block() as b:

                @b.tensor
                def _(pe):
                    pe.transpose(pw[:, 0:D], w[:, 0, :], k.ident[:])
                    pe.transpose(pw[:, D : 2 * D], w[:, 1, :], k.ident[:]).then_inc(turned, 1)

                @b.gpsimd
                def _(pool):
                    pool.iota(real_i[:], pattern=[[1, k.COLS]], base=0, channel_multiplier=k.COLS).then_inc(row_no, 1)

                @b.vector
                def _(dve):
                    step = Chain(dve, done)
                    dve.wait_ge(turned, 1)
                    step(dve.tensor_copy(wt[:].rearrange("p s d -> p (s d)"), pw[:, 0 : 2 * D]))
                    dve.wait_ge(row_no, 1)
                    step(dve.tensor_copy(real[:], real_i[:]))
                    step(dve.tensor_scalar(real[:], real[:], float(k.N), None, ALU.is_lt))

        n = Nodes(k, c, 2, 1, 2)
        p_s = [c.enter_context(nc.psum_tensor(k.name(f"p_s{i}"), [P, 512], F32)) for i in range(2)]
        row = sb("row", [1, 6, D])
        mean, sq, o2 = n.ring("mean", 4), n.ring("sq", RING), n.ring("o2", RING)
        inv = sb("inv", [P, RING, JN])
        squared, radicand, rooted, scaled, both, counted = [
            sem(x) for x in ("squared", "radicand", "rooted", "scaled", "both", "counted")]
        R = lambda t, c: t[:, c.slot(RING)]
        part = lambda t: t[:].rearrange("p (b j) -> p b j", j=JN)
        wide3 = lambda a: a.unsqueeze(2).to_broadcast([P, JN, D])

        def prep(dve, step, c):
            n.wait_message(dve, c)
            wait(dve, n.turned, (c.n - 3) * NG)
            step(dve.tensor_tensor(mean[:, c.slot(4)], n.x[0][:, c.slot(UB)], wide3(part(k.rcnt)[:, c.n, :]), ALU.mult))
            dve.nop().then_inc(n.prepped, 1)

        def square(act, c):
            act.wait_ge(n.z_in, (c.n + 1) * NG)
            act.activation(R(sq, c), R(n.z, c), ACT.Square).then_inc(squared, 1)

        def length(dve, step, c):
            dve.wait_ge(squared, c.n + 1)
            step(dve.tensor_reduce(R(inv, c), R(sq, c), AX.X, ALU.add))
            step(dve.tensor_scalar(R(inv, c), R(inv, c), 1.0e-24, None, ALU.max))
            dve.nop().then_inc(radicand, 1)

        def root(pool, c):
            pool.wait_ge(radicand, c.n + 1)
            pool.tensor_tensor(R(inv, c), R(inv, c), wide(k.root[:], JN), ALU.pow).then_inc(rooted, 1)

        def scale(dve, step, c):
            dve.wait_ge(rooted, c.n + 1)
            n.wait_stored(dve, c)
            wait(dve, counted, c.n - RING + 1)
            step(dve.tensor_tensor(R(inv, c), R(inv, c), part(real)[:, c.n, :], ALU.mult))
            step(dve.scalar_tensor_tensor(R(n.o[0], c), R(n.z, c), 0.0, wide3(R(inv, c)), ALU.max, ALU.mult))
            dve.nop().then_inc(n.finished, 1)

        def square_scaled(act, c):
            act.wait_ge(n.finished, c.n + 1)
            wait(act, counted, c.n - RING + 1)
            act.activation(R(o2, c), R(n.o[0], c), ACT.Square).then_inc(both, 1)

        def sums(pe, c):
            pe.wait_ge(both, c.n + 1)
            first = isinstance(c.n, int) and c.n == 0
            final = isinstance(c.n, int) and c.n == k.NB - 1
            for a, z in GROUPS:
                for i, src in enumerate((n.o[0], o2)):
                    ins = pe.matmul(p_s[i][0:1, 0 : (z - a) * D], k.ones[:, 0:1], R(src, c)[:, a:z, :].rearrange("p j d -> p (j d)"),
                                    start=first and a == 0, stop=final and z == JN)
            ins.then_inc(counted, 1)

        n.z_free = n.finished
        n.run([k.msg, k.tab[0]], [k.tab[1]], lambda c: [mean[:, c.slot(4)], n.x[1][:, c.slot(UB)]], [wt[:, 0, :], wt[:, 1, :]],
              k.b_skip, [(-1, scale), (0, length), (2, prep)], [(0, square), (-1, square_scaled)], [(0, root)],
              prep=True, pe_stages=[(-2, sums)])
        ready, spread, done, radicand, rooted = [sem(x) for x in ("ready", "spread", "bdone", "bradicand", "brooted")]
        wide_row = sb("wide_row", [1, 2, 4 * D])
        sh = sb("sh", [1, 2 * D])
        with nc.Block() as b:

            @b.gpsimd
            def _(pool):
                pool.wait_ge(radicand, 1)
                pool.tensor_tensor(row[:, 2, :], row[:, 2, :], k.root[0:1, :].to_broadcast([1, D]), ALU.pow).then_inc(rooted, 1)

            @b.vector
            def _(dve):
                step = Chain(dve, done)
                f = lambda i: row[:, i, :]
                for i in range(2):
                    step(dve.tensor_copy(wide_row[:, i, :], p_s[i][0:1, :]))
                    step(dve.tensor_reduce(f(i), wide_row[:, i, :].rearrange("p (r d) -> p d r", d=D), AX.X, ALU.add))
                    step(dve.tensor_scalar(f(i), f(i), 1.0 / k.N, None, ALU.mult))
                step(dve.tensor_tensor(f(2), f(0), f(0), ALU.mult))
                step(dve.tensor_tensor(f(2), f(1), f(2), ALU.subtract))
                step(dve.tensor_scalar(f(2), f(2), 0.0, EPS, ALU.max, ALU.add))
                dve.nop().then_inc(radicand, 1)
                dve.wait_ge(rooted, 1)
                step(dve.tensor_tensor(sh[:, 0:D], f(2), gb[:, 0, :], ALU.mult))
                step(dve.tensor_tensor(f(4), f(0), sh[:, 0:D], ALU.mult))
                step(dve.tensor_tensor(sh[:, D : 2 * D], gb[:, 1, :], f(4), ALU.subtract))
                dve.nop().then_inc(ready, 1)
                dve.wait_ge(spread, 1)
                step(dve.tensor_copy(k.bn[:].rearrange("p s d -> p (s d)"), n.p_m[0][:, 0 : 2 * D]))

            @b.tensor
            def _(pe):
                pe.wait_ge(ready, 1)
                pe.matmul(n.p_m[0][:, 0 : 2 * D], k.ones[0:1, :], sh[:], start=True, stop=True).then_inc(spread, 1)


def batch_norm_nodes(k):
    with ExitStack() as c:
        n = Nodes(k, c, 2, 1, 0, message=0)
        y = n.ring("y", RING)
        norm = Norm(k, c, 0)
        every = lambda i: k.bn[:, i : i + 1, :].to_broadcast([P, JN, D])
        R = lambda t, c: t[:, c.slot(RING)]

        def residual(dve, step, c):
            v, i = R(y, c), c.slot(UB)
            n.wait_loaded(dve, c)
            wait(dve, norm.applied, c.n - RING + 1)
            step(dve.tensor_tensor(v, n.x[0][:, i], every(0), ALU.mult))
            step(dve.tensor_tensor(v, v, every(1), ALU.add))
            step(dve.tensor_tensor(v, v, n.x[1][:, i], ALU.add))
            norm.stats(dve, step, c, v)

        def apply(act, c):
            n.wait_stored(act, c)
            norm.apply(act, c, R(y, c), R(n.o[0], c))

        n.finished = norm.applied
        n.run([k.tab[1], k.tab[0]], [k.res], None, [], None, [(0, residual)], [(0, apply)], [(0, norm.root)])


def angle_nodes(k):
    nc, A = k.nc, k.a
    with ExitStack() as c:
        sb = lambda n, s, d=F32: c.enter_context(nc.sbuf_tensor(k.name(n), s, d))
        wb = sb("wb", [P, 3, D])
        bc = lambda n: A[n].partition_broadcast(P)
        load_rows(k, [(k.w_skip[:], A["L3_gnn_Wskip"]), (k.b_skip[0:1, :], A["L3_gnn_bskip"].unsqueeze(0)),
                      (k.ln_g[:], bc("L3_gnn_ln_gamma")), (k.ln_b[:], bc("L3_gnn_ln_beta"))]
                  + [(wb[:, i, :], A["L3_gnn_Wbeta"][i * D : (i + 1) * D, :].rearrange("d o -> (d o)").partition_broadcast(P)) for i in range(3)])
        n = Nodes(k, c, 2, 1, 1)
        e, y = n.ring("e", RING), n.ring("y", RING)
        t = n.ring("t", 1)[:, 0]
        gate = sb("gate", [P, RING, 2, JN])
        first, second = [Norm(k, c, i) for i in range(2)]
        begun, gate_in, gate_out = [k.semaphore(x) for x in ("begun", "gate_in", "gate_out")]
        R = lambda t, c: t[:, c.slot(RING)]
        wide_rows = lambda g: g.unsqueeze(2).to_broadcast([P, JN, D])
        weight = lambda i: wb[:, i : i + 1, :].to_broadcast([P, JN, D])
        every = lambda g: g[:].unsqueeze(1).to_broadcast([P, JN, D])

        def begin(dve):
            step = Chain(dve, begun)
            step(dve.tensor_tensor(wb[:, 0, :], wb[:, 0, :], wb[:, 2, :], ALU.add))
            step(dve.tensor_tensor(wb[:, 1, :], wb[:, 1, :], wb[:, 2, :], ALU.subtract))

        def logit(dve, step, c):
            m, z = n.x[1][:, c.slot(UB)], R(n.z, c)
            n.wait_z(dve, c)
            n.wait_message(dve, c)
            step(dve.tensor_tensor(R(e, c), m, weight(0), ALU.mult), dve.tensor_tensor(t, z, weight(1), ALU.mult))
            step(dve.tensor_tensor(t, t, R(e, c), ALU.add))
            step(dve.tensor_reduce(R(gate, c)[:, 0, :], t, AX.X, ALU.add))
            step(dve.tensor_scalar(R(gate, c)[:, 0, :], R(gate, c)[:, 0, :], -80.0, None, ALU.max))
            dve.nop().then_inc(gate_in, 1)

        def exponential(act, c):
            act.wait_ge(gate_in, c.n + 1)
            act.activation(R(gate, c)[:, 0, :], R(gate, c)[:, 0, :], ACT.Exp, scale=-1.0).then_inc(gate_out, 1)

        def mix(dve, step, c):
            m, z, v, g = n.x[1][:, c.slot(UB)], R(n.z, c), R(y, c), R(gate, c)
            dve.wait_ge(gate_out, c.n + 1)
            step(dve.tensor_scalar(g[:, 0, :], g[:, 0, :], 1.0, None, ALU.add), dve.tensor_tensor(v, z, m, ALU.subtract))
            step(dve.reciprocal(g[:, 1, :], g[:, 0, :]))
            step(dve.tensor_tensor(v, v, wide_rows(g[:, 1, :]), ALU.mult))
            step(dve.tensor_tensor(v, v, m, ALU.add))
            first.stats(dve, step, c, v)

        def residual(dve, step, c):
            v, x = R(e, c), n.x[0][:, c.slot(UB)]
            dve.wait_ge(first.applied, c.n + 1)
            step(dve.tensor_tensor(v, v, every(k.ln_g), ALU.mult))
            step(dve.tensor_tensor(v, v, every(k.ln_b), ALU.add))
            step(dve.scalar_tensor_tensor(v, v, 0.0, x, ALU.max, ALU.add))
            step(dve.tensor_tensor(v, v, x, ALU.add))
            second.stats(dve, step, c, v)

        def apply_second(act, c):
            n.wait_stored(act, c)
            second.apply(act, c, R(e, c), R(n.o[0], c))

        n.z_free = first.radicand
        n.finished = second.applied
        n.run([k.res, k.msg], [k.out], lambda c: [n.x[0][:, c.slot(UB)]], [k.w_skip], k.b_skip,
              [(-2, residual), (-1, mix), (0, logit)],
              [(-2, apply_second), (-1, lambda act, c: first.apply(act, c, R(y, c), R(e, c))), (0, exponential)],
              [(-2, second.root), (-1, first.root)], begin=begin)


def build(nc, args, out, n_nodes):
    args["n_nodes"] = n_nodes
    k = Net(nc, args, out)
    k.N = n_nodes
    dram = lambda n, s, d=F32: nc.dram_tensor(n, s, d, kind="Internal").ap()
    k.msg = dram("msg", [k.NR + 1, D])
    k.tab = [dram("tab0", [k.NR, D]), dram("tab1", [k.NR, D])]
    k.res = dram("res", [k.NR, D])
    k.meta = dram("meta", [P, k.NB, FIELDS, J], I32)
    with ExitStack() as c:
        sb = lambda n, s, d=F32: c.enter_context(nc.sbuf_tensor(k.name(n), s, d))
        k.ident, k.ones = sb("ident", [P, P]), sb("ones", [P, P])
        k.dinv, k.rcnt = sb("dinv", [P, k.COLS]), sb("rcnt", [P, k.COLS])
        k.join, k.join_t, k.no_join = sb("join", [P, P]), sb("join_t", [P, P]), sb("no_join", [P, P])
        k.last = sb("last", [P, k.NB, J], I32)
        k.root = sb("root", [P, 1])
        k.join_row = sb("join_row", [P, 1], I32)
        k.w_skip, k.b_skip = sb("w_skip", [P, D]), sb("b_skip", [1, D])
        k.ln_g, k.ln_b = sb("ln_g", [P, D]), sb("ln_b", [P, D])
        k.w_qk, k.b_qk = sb("w_qk", [P, 2, X2]), sb("b_qk", [1, 2, X2])
        k.w_val, k.b_val = sb("w_val", [P, 2, D]), sb("b_val", [4, D])
        k.bn = sb("bn", [P, 2, D])
        setup(k)
        k.end_phase()
        scale_pass(k)
        k.end_phase()
        sum_edges(k, k.tab[0])
        k.end_phase()
        gcn_nodes(k)
        k.end_phase()
        src, dst = k.tab[1], k.tab[0]
        for l in range(args["L1_gnn_Wq"].shape[0]):
            last = l == args["L1_gnn_Wq"].shape[0] - 1
            fold_conv(k, l)
            k.end_phase()
            conv_edges(k, src)
            k.end_phase()
            conv_nodes(k, src, dst, last)
            k.end_phase()
            src, dst = dst, src
        sum_edges(k, k.tab[0])
        k.end_phase()
        sage_nodes(k)
        k.end_phase()
        batch_norm_nodes(k)
        k.end_phase()
        angle_edges(k, k.res)
        k.end_phase()
        angle_nodes(k)
        k.end_phase()


_ORDER = {"x": "x", "src": "src", "dst": "dst", "edge_attr_128": "edge", "edge_weight1": "weight"}


def kernel(**inputs):
    import concourse.bacc as _bacc
    from concourse.bass_utils import run_bass_kernel_spmd as _run

    nc = _bacc.Bacc("TRN2", target_bir_lowering=False, num_devices=1)
    n = inputs["x"].shape[0]
    nr = padded(n)

    def fill(a, rows_, value):
        return np.concatenate([a, np.full((rows_,) + a.shape[1:], value, a.dtype)])

    arrays, args = {}, {}
    for name, a in inputs.items():
        if name == "L2_gnn_adj_norm_sp":
            continue
        a = np.ascontiguousarray(a)
        if name in ("x", "edge_attr_128", "edge_weight1", "src"):
            a = fill(a, nr - n, 0)
        elif name == "dst":
            a = np.concatenate([np.full((1,), -1, a.dtype), a, np.full((nr - n,), n, a.dtype), np.full((1,), -1, a.dtype)])
        arrays[f"in_{name}"] = a
        args[_ORDER.get(name, name)] = nc.dram_tensor(f"in_{name}", a.shape, mybir.dt.from_np(a.dtype), kind="ExternalInput").ap()
    out = nc.dram_tensor("out_0", (nr, D), F32, kind="ExternalOutput").ap()
    build(nc, args, out, n)
    r = _run(nc, [arrays], core_ids=[0])
    return r.results[0]["out_0"][0:n]
```

```python
from contextlib import ExitStack

import concourse.bass as bass
import concourse.mybir as mybir
import numpy as np

F32 = mybir.dt.float32
BF16 = mybir.dt.bfloat16
F16 = mybir.dt.float16
I32 = mybir.dt.int32
ALU = mybir.AluOpType
ACT = mybir.ActivationFunctionType
AX = mybir.AxisListType

P = 128
D = 128
J = 7
U = 4
SCORE, SHARE = 2, 1
EAHEAD = 5
JN = 7
UB = 8
RING = 4
LEAD, DRAIN = 5, 3
AHEAD = 4
GROUPS = [(0, 4), (4, 7)]
NG = len(GROUPS)
FAR = float(1 << 20)
LOW = -1.0e30
EPS = 1.0e-5

SRC, DST, SAME, END, WGT = range(5)
FIELDS = 5


def padded(n):
    return -(-n // (P * JN * UB)) * P * JN * UB


def turns(eng, n, body):
    body(0)
    if n > 2:
        with eng.Fori(1, n - 1) as t:
            body(t)
    if n > 1:
        body(n - 1)


def wait(eng, sem, value, passed=None):
    if isinstance(value, int) and value <= 0:
        return
    eng.wait_ge(sem, value)
    if passed is not None and not isinstance(value, int):
        eng.sem_inc(passed, 1)


class Chain:

    def __init__(self, eng, sem, per=0):
        self.eng, self.sem, self.per, self.base, self.n = eng, sem, per, 0, 0

    def at(self, chunk):
        self.base, self.n = chunk * self.per, 0

    def __call__(self, ins):
        self.n += 1
        ins.then_inc(self.sem, 1)
        self.eng.wait_ge(self.sem, self.base + self.n)

    def end(self):
        assert self.n == self.per, (self.n, self.per)


class Net:
    def __init__(self, nc, args, outs):
        self.nc = nc
        self.a = args
        self.out = outs
        self.NR = args["x"].shape[0]
        self.COLS = self.NR // P
        self.NB = self.COLS // J
        self.T = self.NB // U
        self.TN = self.COLS // (JN * UB)
        self.names = 0
        self.sems = []

    def semaphore(self, what):
        handle = self.nc.alloc_semaphore(self.name(what))
        self.sems.append(handle)
        return handle

    def end_phase(self):
        self.nc.clear_and_free_semaphores(self.sems)
        self.nc.all_engine_barrier()
        self.sems = []

    def name(self, what):
        self.names += 1
        return f"{what}_{self.names}"


def rows(table, j=JN):
    n = table.shape[0] // P * P
    return table[0:n].rearrange("(p b j) d -> p b (j d)", p=P, j=j)


def wide(col, n):
    return col.to_broadcast([P, n])


def setup(k):
    nc, A = k.nc, k.a
    NB, COLS, T = k.NB, k.COLS, k.T
    with ExitStack() as c:
        sb = lambda n, s, d=F32: c.enter_context(nc.sbuf_tensor(k.name(n), s, d))
        sem = lambda n: k.semaphore(n)
        dst_i = sb("dst_i", [P, COLS], I32)
        nxt_i = sb("nxt_i", [P, COLS], I32)
        prv_i = sb("prv_i", [P, COLS], I32)
        src_i = sb("src_i", [P, COLS], I32)
        w_in = sb("w_in", [P, COLS])
        dst = sb("dst", [P, COLS])
        nxt = sb("nxt", [P, COLS])
        prv = sb("prv", [P, COLS])
        last = sb("last", [P, COLS])
        tmp = sb("tmp", [P, COLS])
        tmp_i = sb("tmp_i", [P, COLS], I32)
        hi = sb("hi", [P, COLS])
        lo = sb("lo", [P, COLS])
        rec = sb("rec", [P, NB, FIELDS, J], I32)
        zero = sb("zero", [1, D])
        ones = sb("cones", [P, COLS])
        first_slot_i = sb("first_slot_i", [P, 1], I32)
        first_slot = sb("first_slot", [P, 1])
        iota_i = sb("iota_i", [P, max(COLS, P)], I32)
        iota = sb("iota", [P, max(COLS, P)])
        iota_h = sb("iota_h", [P, max(COLS, P)], F16)
        upper = sb("upper", [P, P])
        lower = sb("lower", [P, P])
        any_end = sb("any_end", [P, 1])
        small = sb("small", [P, 4])
        hi1 = sb("hi1", [P, U, J, P], BF16)
        lo1 = sb("lo1", [P, U, J, COLS], BF16)
        hist = c.enter_context(nc.psum_tensor(k.name("hist"), [P, 512], F32))
        row_ps = c.enter_context(nc.psum_tensor(k.name("row_ps"), [P, 512], F32))
        loaded, zeroed, consts, made, stored = [sem(n) for n in ("loaded", "zeroed", "consts", "made", "stored")]
        zstored, hots, counted, rowed, done = [sem(n) for n in ("zstored", "hots", "counted", "rowed", "done")]
        split, pooled, degree, rooted = sem("split"), sem("pooled"), sem("degree"), sem("rooted")
        flat = lambda ap: ap.rearrange("(p c) -> p c", p=P)
        recf = rec[:].bitcast(F32)
        field = lambda r, f: r[:, :, f, :]
        col = lambda t: t[:].rearrange("p (b j) -> p b j", j=J)
        n_ext = k.NR
        with nc.Block() as b:

            @b.sync
            def _(sp):
                sp.dma_start(dst_i[:], flat(A["dst"][1 : 1 + n_ext])).then_inc(loaded, 16)
                sp.dma_start(nxt_i[:], flat(A["dst"][2 : 2 + n_ext])).then_inc(loaded, 16)
                sp.dma_start(prv_i[:], flat(A["dst"][0:n_ext])).then_inc(loaded, 16)
                sp.dma_start(src_i[:], flat(A["src"])).then_inc(loaded, 16)
                sp.dma_start(w_in[:], A["weight"].rearrange("(p c) o -> p (c o)", p=P)).then_inc(loaded, 16)
                sp.wait_ge(zeroed, 1)
                sp.dma_start(k.msg[k.NR : k.NR + 1, :], zero[:]).then_inc(zstored, 16)
                sp.wait_ge(made, 1)
                sp.dma_start(k.meta.rearrange("p b f j -> p (b f j)"),
                             rec[:].rearrange("p b f j -> p (b f j)")).then_inc(stored, 16)
                sp.wait_ge(stored, 16)
                sp.wait_ge(zstored, 16)

            @b.gpsimd
            def _(pool):
                pool.memset(zero[:], 0.0).then_inc(zeroed, 1)
                pool.memset(k.ident[:], 0.0).then_inc(pooled, 1)
                pool.memset(k.ones[:], 1.0).then_inc(pooled, 1)
                pool.memset(k.ones_bf[:], 1.0).then_inc(pooled, 1)
                pool.memset(k.root[:], -0.5).then_inc(pooled, 1)
                pool.memset(k.eps[:], EPS).then_inc(pooled, 1)
                pool.memset(upper[:], 1.0).then_inc(pooled, 1)
                pool.memset(lower[:], 1.0).then_inc(pooled, 1)
                pool.wait_ge(pooled, 7)
                pool.iota(first_slot_i[:], pattern=[[0, 1]], base=0, channel_multiplier=COLS).then_inc(consts, 1)
                pool.affine_select(out=k.ident[:], in_=k.ident[:], compare_op=ALU.not_equal, fill=1.0, base=0,
                                   pattern=[[-1, P]], channel_multiplier=1).then_inc(consts, 1)
                pool.affine_select(out=upper[:], in_=upper[:], compare_op=ALU.is_gt, fill=0.0, base=0,
                                   pattern=[[1, P]], channel_multiplier=-1).then_inc(consts, 1)
                pool.affine_select(out=lower[:], in_=lower[:], compare_op=ALU.is_gt, fill=0.0, base=0,
                                   pattern=[[-1, P]], channel_multiplier=1).then_inc(consts, 1)
                pool.iota(iota_i[:], pattern=[[1, max(COLS, P)]], base=0, channel_multiplier=0).then_inc(consts, 1)
                pool.wait_ge(degree, 1)
                pool.tensor_tensor(k.dinv[:], k.dinv[:], wide(k.root[:], COLS), ALU.pow).then_inc(rooted, 1)
                pool.wait_ge(rooted, 1)

            @b.vector
            def _(dve):
                step = Chain(dve, done)
                dve.wait_ge(loaded, 80)
                step(dve.tensor_copy(dst[:], dst_i[:]))
                step(dve.tensor_copy(nxt[:], nxt_i[:]))
                step(dve.tensor_copy(prv[:], prv_i[:]))
                step(dve.tensor_tensor(last[:], dst[:], nxt[:], ALU.not_equal))
                step(dve.tensor_copy(field(rec, SRC), col(src_i)))
                step(dve.tensor_copy(field(rec, DST), col(dst_i)))
                step(dve.tensor_copy(field(recf, WGT), col(w_in)))
                step(dve.tensor_tensor(tmp[:], dst[:], prv[:], ALU.is_equal))
                step(dve.memset(tmp[:, 0:1], 0.0))
                step(dve.tensor_copy(field(recf, SAME), col(tmp)))
                step(dve.tensor_scalar(tmp[:], dst[:], dst[:, 0:1], None, ALU.is_equal))
                step(dve.tensor_tensor(tmp[:], tmp[:], last[:], ALU.mult))
                step(dve.tensor_copy(field(recf, END), col(tmp)))
                step(dve.tensor_reduce(any_end[:], tmp[:], AX.X, ALU.add))
                dve.nop().then_inc(made, 1)
                step(dve.tensor_scalar(tmp_i[:], dst[:], 1.0 / COLS, None, ALU.mult))
                step(dve.tensor_copy(hi[:], tmp_i[:]))
                step(dve.scalar_tensor_tensor(lo[:], hi[:], -float(COLS), dst[:], ALU.mult, ALU.add))
                step(dve.tensor_scalar(tmp[:], lo[:], 0.0, None, ALU.is_lt))
                step(dve.tensor_tensor(hi[:], hi[:], tmp[:], ALU.subtract))
                step(dve.scalar_tensor_tensor(lo[:], tmp[:], float(COLS), lo[:], ALU.mult, ALU.add))
                step(dve.tensor_scalar(tmp[:], lo[:], float(COLS), None, ALU.is_ge))
                step(dve.tensor_tensor(hi[:], hi[:], tmp[:], ALU.add))
                step(dve.scalar_tensor_tensor(lo[:], tmp[:], -float(COLS), lo[:], ALU.mult, ALU.add))
                dve.wait_ge(consts, 5)
                step(dve.tensor_copy(iota[:], iota_i[:]))
                step(dve.tensor_copy(iota_h[:], iota[:]))
                step(dve.tensor_copy(first_slot[:], first_slot_i[:]))
                step(dve.tensor_tensor(col(tmp), field(recf, END), iota[:, 0:COLS].rearrange("p (b j) -> p b j", j=J), ALU.mult))
                step(dve.tensor_reduce(small[:, 3:4], tmp[:], AX.X, ALU.add))
                step(dve.tensor_tensor(first_slot[:], first_slot[:], small[:, 3:4], ALU.add))
                dve.nop().then_inc(split, 1)
                dve.wait_ge(rowed, 1)
                step(dve.tensor_scalar(k.join_t[:], row_ps[:, 0:P], dst[:, COLS - 1 : COLS], None, ALU.is_equal))
                step(dve.tensor_tensor(k.join_t[:], k.join_t[:], upper[:], ALU.mult))
                step(dve.tensor_scalar(k.join[:], row_ps[:, P : 2 * P], dst[:, 0:1], None, ALU.is_equal))
                step(dve.tensor_tensor(k.join[:], k.join[:], lower[:], ALU.mult))
                step(dve.tensor_scalar(k.no_join[:], k.join[:], -LOW, LOW, ALU.mult, ALU.add))
                step(dve.tensor_reduce(small[:, 0:1], k.join[:], AX.X, ALU.max))
                step(dve.tensor_tensor(small[:, 0:1], small[:, 0:1], any_end[:], ALU.mult))
                step(dve.tensor_tensor(small[:, 1:2], small[:, 0:1], first_slot[:], ALU.mult))
                step(dve.tensor_scalar(small[:, 2:3], small[:, 0:1], -FAR, FAR, ALU.mult, ALU.add))
                step(dve.tensor_tensor(small[:, 1:2], small[:, 1:2], small[:, 2:3], ALU.add))
                step(dve.tensor_copy(k.join_row[:], small[:, 1:2]))
                hi3, lo3 = col(hi), col(lo)

                def body(t):
                    for u in range(U):
                        blk = t * U + u
                        wait(dve, counted, blk - U + 1)
                        for j in range(J):
                            dve.tensor_scalar(hi1[:, u, j, :], iota_h[:, 0:P], hi3[:, blk, j : j + 1], None, ALU.is_equal)
                            ins = dve.tensor_scalar(lo1[:, u, j, :], iota_h[:, 0:COLS], lo3[:, blk, j : j + 1], None, ALU.is_equal)
                        ins.then_inc(hots, 1)

                turns(dve, T, body)
                dve.wait_ge(counted, NB)
                h = hist[:, 0:COLS]
                step(dve.tensor_scalar(k.dinv[:], h, 1.0, None, ALU.add))
                dve.nop().then_inc(degree, 1)
                step(dve.tensor_scalar(tmp[:], h, 1.0, None, ALU.max))
                step(dve.reciprocal(k.rcnt[:], tmp[:]))
                step(dve.memset(ones[:], 1.0))
                step(dve.tensor_tensor_scan(hi[:], ones[:], h, 0.0, ALU.mult, ALU.add))
                dve.nop().then_inc(split, 1)
                dve.wait_ge(rowed, 2)
                step(dve.tensor_copy(small[:, 0:1], row_ps[:, 2 * P : 2 * P + 1]))
                step(dve.tensor_scalar(hi[:], hi[:], small[:, 0:1], -1.0 - k.NR, ALU.add, ALU.add))
                step(dve.tensor_scalar(tmp[:], h, 1.0, None, ALU.min))
                step(dve.tensor_tensor(hi[:], hi[:], tmp[:], ALU.mult))
                step(dve.tensor_scalar(k.last[:].rearrange("p b j -> p (b j)"), hi[:], float(k.NR), None, ALU.add))

            @b.tensor
            def _(pe):
                pe.wait_ge(consts, 1)
                pe.wait_ge(split, 1)
                pe.transpose(row_ps[:, 0:P], wide(dst[:, 0:1], P), k.ident[:])
                pe.transpose(row_ps[:, P : 2 * P], wide(dst[:, COLS - 1 : COLS], P), k.ident[:]).then_inc(rowed, 1)

                def chunk(blk, u, first, final):
                    pe.wait_ge(hots, blk + 1)
                    for j in range(J):
                        ins = pe.matmul(hist[:, 0:COLS], hi1[:, u, j, :], lo1[:, u, j, :],
                                        start=first and j == 0, stop=final and j == J - 1)
                    ins.then_inc(counted, 1)

                def body(t):
                    for u in range(U):
                        blk = t * U + u
                        chunk(blk, u, isinstance(blk, int) and blk == 0, isinstance(blk, int) and blk == NB - 1)

                turns(pe, T, body)
                pe.wait_ge(split, 2)
                pe.matmul(row_ps[:, 2 * P : 2 * P + 1], upper[:], hi[:, COLS - 1 : COLS], start=True, stop=True).then_inc(rowed, 1)


def scale_pass(k):
    nc = k.nc
    JS, US = 2 * J, 2
    TS = k.COLS // (JS * US)
    with ExitStack() as c:
        xin = c.enter_context(nc.sbuf_tensor(k.name("xin"), [P, US, JS, D], F32))
        xs = c.enter_context(nc.sbuf_tensor(k.name("xs"), [P, US, JS, D], F32))
        loaded = [k.semaphore(f"loaded{u}") for u in range(US)]
        stored = [k.semaphore(f"stored{u}") for u in range(US)]
        scaled, passed = k.semaphore("scaled"), k.semaphore("passed")
        src, dst = rows(k.a["x"], JS), rows(k.tab[0], JS)
        dinv = k.dinv[:].rearrange("p (b j) -> p b j", j=JS)
        with nc.Block() as b:

            @b.sync
            def _(sp):
                def body(t):
                    for u in range(US):
                        wait(sp, scaled, t * US + u - 1, passed)
                        sp.dma_start(xin[:, u].rearrange("p j d -> p (j d)"), src[:, t * US + u, :]).then_inc(loaded[u], 16)

                turns(sp, TS, body)

            @b.vector
            def _(dve):
                def body(t):
                    for u in range(US):
                        dve.wait_ge(loaded[u], (t + 1) * 16)
                        wait(dve, stored[u], t * 16)
                        dve.tensor_tensor(xs[:, u], xin[:, u], dinv[:, t * US + u, :].unsqueeze(2).to_broadcast([P, JS, D]),
                                          ALU.mult).then_inc(scaled, 1)

                turns(dve, TS, body)

            @b.scalar
            def _(act):
                def body(t):
                    for u in range(US):
                        act.wait_ge(scaled, t * US + u + 1)
                        act.dma_start(dst[:, t * US + u, :], xs[:, u].rearrange("p j d -> p (j d)")).then_inc(stored[u], 16)

                turns(act, TS, body)
                for u in range(US):
                    act.wait_ge(stored[u], TS * 16)


def load_records(sp, k, c, rec, rec_in):
    sp.dma_start(rec[:, c.slot(UB)].rearrange("p f j -> p (f j)"),
                 k.meta[:, c.n].rearrange("p f j -> p (f j)")).then_inc(rec_in[c.slot(UB)], 16)


def store_chunk(sp, k, c, tile, out):
    sp.dma_start(rows(k.msg, J)[:, c.n, :], tile[:, c.slot(RING)].rearrange("p j d -> p (j d)")).then_inc(out[c.slot(RING)], 16)


def sum_edges(k, table):
    nc = k.nc
    with ExitStack() as c:
        sb = lambda n, s, d=F32: c.enter_context(nc.sbuf_tensor(k.name(n), s, d))
        sem = lambda n: k.semaphore(n)
        rec = sb("rec", [P, UB, FIELDS, J], I32)
        got = sb("got", [P, UB, J, D])
        run = sb("run", [P, RING, J, D])
        head = sb("head", [P, D])
        fix = sb("fix", [P, D])
        part = c.enter_context(nc.psum_tensor(k.name("part"), [P, 512], F32))
        rec_in = [sem(f"rec_in{u}") for u in range(UB)]
        got_in = [sem(f"got_in{u}") for u in range(UB)]
        put_out = [sem(f"put_out{u}") for u in range(RING)]
        summed, ready, begun = sem("summed"), sem("ready"), sem("begun")
        joined, fixed, fix_out = sem("joined"), sem("fixed"), sem("fix_out")
        passed = sem("passed")
        recf = rec[:].bitcast(F32)
        PER = 2 * J
        with nc.Block() as b:

            @b.sync
            def _(sp):
                def one(t, u):
                    c = Chunk(k, t, u, EAHEAD)
                    if c.there:
                        wait(sp, summed, (c.n - UB + 1) * PER, passed)
                        load_records(sp, k, c, rec, rec_in)
                    c = Chunk(k, t, u)
                    if c.there:
                        wait(sp, summed, (c.n + 1) * PER, passed)
                        store_chunk(sp, k, c, run, put_out)

                walk(k, sp, one, EAHEAD, 0)
                for u in range(RING):
                    sp.wait_ge(put_out[u], k.NB // RING * 16)

            @b.gpsimd
            def _(pool):
                def one(t, u):
                    c, i = Chunk(k, t, u), u % UB
                    wait(pool, rec_in[i], (c.use(UB) + 1) * 16, passed)
                    for j in range(J):
                        pool.indirect_dma_start(got[:, i, j, :], None, table,
                                                bass.IndirectOffsetOnAxis(ap=rec[:, i, SRC, j : j + 1], axis=0)).then_inc(got_in[i], 16)

                walk(k, pool, one, 0, 0)
                pool.wait_ge(fixed, 1)
                for u in range(RING):
                    pool.wait_ge(put_out[u], k.NB // RING * 16)
                pool.indirect_dma_start(k.msg, bass.IndirectOffsetOnAxis(ap=k.join_row[:], axis=0), fix[:], None,
                                        bounds_check=k.NR - 1, oob_is_err=False).then_inc(fix_out, 16)
                pool.wait_ge(fix_out, 16)

            @b.vector
            def _(dve):
                step = Chain(dve, summed, PER)
                begin = Chain(dve, begun)
                begin(dve.memset(run[:, RING - 1, J - 1, :], 0.0))
                begin(dve.memset(head[:], 0.0))

                def one(t, u):
                    c = Chunk(k, t, u)
                    i, r = c.slot(UB), c.slot(RING)
                    step.at(c.n)
                    dve.wait_ge(got_in[i], (c.use(UB) + 1) * 16 * J)
                    wait(dve, put_out[r], c.use(RING) * 16)
                    for j in range(J):
                        prev = run[:, r, j - 1, :] if j else run[:, (r - 1) % RING, J - 1, :]
                        step(dve.scalar_tensor_tensor(run[:, r, j, :], prev, recf[:, i, SAME, j : j + 1], got[:, i, j, :],
                                                      ALU.mult, ALU.add))
                        step(dve.scalar_tensor_tensor(head[:], run[:, r, j, :], recf[:, i, END, j : j + 1], head[:],
                                                      ALU.mult, ALU.add))
                    step.end()

                walk(k, dve, one, 0, 0)
                dve.nop().then_inc(ready, 1)
                dve.wait_ge(joined, 1)
                dve.tensor_tensor(fix[:], part[:, 0:D], head[:], ALU.add).then_inc(fixed, 1)

            @b.tensor
            def _(pe):
                pe.wait_ge(ready, 1)
                pe.matmul(part[:, 0:D], k.join_t[:], run[:, RING - 1, J - 1, :], start=True, stop=True).then_inc(joined, 1)


class Chunk:

    def __init__(self, k, t, u, lag=0):
        self.t, self.u = t, u + lag
        self.n = t * UB + self.u
        self.there = not isinstance(t, int) or 0 <= self.n < k.NB

    def slot(self, ring):
        return self.u % ring

    def use(self, ring):
        return self.t * (UB // ring) + self.u // ring


def column(k, t, u, lag, j):
    return Chunk(k, t, u, lag + j // J), j % J


class Steps:

    def __init__(self, eng, sem):
        self.eng, self.sem, self.per, self.base, self.n = eng, sem, None, 0, 0

    def at(self, chunk):
        self.base, self.n = (0 if self.per is None else chunk.n * self.per), 0

    def put(self, *steps):
        for ins in steps:
            ins.then_inc(self.sem, 1)
        self.n += len(steps)

    def land(self):
        wait(self.eng, self.sem, self.base + self.n)

    def __call__(self, *independent):
        self.put(*independent)
        self.land()

    def before_form_without_wait(self, passed):
        if not isinstance(self.base, int):
            self.eng.sem_inc(passed, 1)

    def end(self):
        assert self.per in (None, self.n)
        self.per = self.n


def walk(k, eng, one, lead, drain):
    for u in range(-lead, 0):
        one(0, u)

    def body(t):
        for u in range(UB):
            one(t, u)

    turns(eng, k.TN, body)
    for u in range(UB, UB + drain):
        one(k.TN - 1, u)


def split_in_three(step, dve, value, rest, parts, out, ident):
    for i in range(3):
        step(dve.tensor_copy(out[:], (rest if i else value)[:]))
        step(dve.tensor_copy(parts[:, i, :], out[:]))
        if i < 2:
            step(dve.tensor_tensor(rest[:], (rest if i else value)[:], parts[:, i, :], ALU.subtract))
    step(dve.tensor_scalar(rest[:], parts[:, 0, :], ident[0:3, 0:1], None, ALU.mult))
    for i in (1, 2):
        step(dve.scalar_tensor_tensor(rest[:], parts[:, i, :], ident[0:3, i : i + 1], rest[:], ALU.mult, ALU.add))
    step(dve.tensor_copy(out[:], rest[:]))


class Coef:

    def __init__(self, sb, H):
        self.H = H
        self.A = sb("cA", [P, 2, H, J + 1])
        self.neg = sb("cneg", [P, H, J + 1])
        self.m = sb("cm", [P, H, J + 1])
        self.ex = sb("cex", [P, 2, H, J])
        self.f = sb("cf", [P, H, J + 1])
        self.a = sb("ca", [P, H, J + 1])
        self.z = sb("cz", [P, H, J + 1])
        self.rz = sb("crz", [P, H, J])
        self.h = sb("ch", [P, H, J])
        self.b = sb("cb", [P, 2, H, J])
        self.g = sb("cg", [P, 2, H, J])
        self.pick = sb("cpick", [P, 2, H, J])
        self.got = sb("cgot", [P, 2 * H])
        self.head = sb("chead", [P, 2 * H])

    def begin(self, step, dve):
        step(dve.memset(self.neg[:], LOW))
        step(dve.memset(self.f[:], 0.0))
        step(dve.memset(self.A[:], 0.0))
        step(dve.memset(self.a[:], 1.0))
        step(dve.memset(self.head[:], 0.0))

    def level(self, n, step, dve, i, same, end):
        H = self.H
        wide3 = lambda s: s.unsqueeze(1).to_broadcast([P, H, J])
        flat = lambda t: t.rearrange("p h j -> p (h j)")
        step.land()
        if n == 0:
            step.put(dve.tensor_scalar(self.neg[:, :, 1:], wide3(same), -LOW, LOW, ALU.mult, ALU.add))
        elif n == 1:
            step.put(dve.tensor_tensor_scan(flat(self.m[:]), flat(self.neg[:]), flat(self.A[:, i]), 0.0, ALU.add, ALU.max))
        elif n == 2:
            step.put(dve.tensor_tensor(self.ex[:, 0], self.m[:, :, 0:J], self.m[:, :, 1:], ALU.subtract),
                     dve.tensor_tensor(self.ex[:, 1], self.A[:, i, :, 1:], self.m[:, :, 1:], ALU.subtract))
        elif n == 3:
            step.put(dve.tensor_scalar(self.ex[:, 0], self.ex[:, 0], 0.0, None, ALU.min))
        elif n == 4:
            step.put(dve.tensor_tensor(self.f[:, :, 1:], self.ex[:, 0], wide3(same), ALU.mult),
                     dve.tensor_copy(self.a[:, :, 1:], self.ex[:, 1]),
                     dve.tensor_tensor(self.pick[:, 0], self.m[:, :, 1:], wide3(end), ALU.mult))
        elif n == 5:
            step.put(dve.tensor_tensor_scan(flat(self.z[:]), flat(self.f[:]), flat(self.a[:]), 0.0, ALU.mult, ALU.add))
        elif n == 6:
            step.put(dve.reciprocal(self.rz[:], self.z[:, :, 1:]),
                     dve.tensor_tensor(self.h[:], self.f[:, :, 1:], self.z[:, :, 0:J], ALU.mult),
                     dve.tensor_tensor(self.pick[:, 1], self.z[:, :, 1:], wide3(end), ALU.mult))
        elif n == 7:
            step.put(dve.tensor_tensor(self.b[:, i], self.a[:, :, 1:], self.rz[:], ALU.mult),
                     dve.tensor_tensor(self.g[:, i], self.h[:], self.rz[:], ALU.mult),
                     dve.tensor_reduce(self.got[:], self.pick[:].rearrange("p s h j -> p (s h) j"), AX.X, ALU.add))
        elif n == 8:
            step.put(dve.tensor_tensor(self.head[:], self.head[:], self.got[:], ALU.add),
                     dve.tensor_copy(self.A[:, 1 - i, :, 0:1], self.m[:, :, J : J + 1]),
                     dve.tensor_copy(self.a[:, :, 0:1], self.z[:, :, J : J + 1]))

    EARLY = {0: 0, 1: 2, 4: 4, 5: 6, 6: 8}
    MIDDLE = {0: 1, 1: 3, 4: 5, 5: 7}
    EXP = 2


def merge_softmax(k, sb, sem, ps, co, tail, head, out, W):
    nc, H = k.nc, co.H
    e = sb("me", [P, P])
    w = sb("mw", [P, P])
    wt = sb("mwt", [P, P])
    t = sb("mt", [P, P])
    s = sb("ms", [P, 8])
    rowed, exped, exp_in, turned, weighed, untangled, summed, out_of, done = [
        sem(n) for n in ("rowed", "exped", "exp_in", "turned", "weighed", "untangled", "msummed", "out_of", "mdone")]
    tm = lambda h: co.m[:, h, J : J + 1]
    tz = lambda h: co.z[:, h, J : J + 1]
    with nc.Block() as b:

        @b.tensor
        def _(pe):
            for h in range(H):
                if h:
                    pe.wait_ge(out_of, h)
                pe.transpose(ps[0][:, 0:P], wide(tm(h), P), k.ident[:])
                pe.transpose(ps[0][:, P : 2 * P], wide(tz(h), P), k.ident[:]).then_inc(rowed, 1)
                pe.wait_ge(weighed, h + 1)
                pe.transpose(ps[1][:, 0:P], w[:], k.ident[:]).then_inc(turned, 1)
                pe.wait_ge(untangled, h + 1)
                pe.matmul(ps[2][:, 0:W], wt[:], tail[:, h, :], start=True, stop=True).then_inc(summed, 1)

        @b.scalar
        def _(act):
            for h in range(H):
                act.wait_ge(exp_in, h + 1)
                act.activation(s[:, 3:4], s[:, 2:3], ACT.Exp)
                act.activation(e[:], e[:], ACT.Exp).then_inc(exped, 1)

        @b.vector
        def _(dve):
            step = Chain(dve, done)
            for h in range(H):
                dve.wait_ge(rowed, h + 1)
                mrow, zrow = ps[0][:, 0:P], ps[0][:, P : 2 * P]
                step(dve.tensor_tensor(t[:], mrow, k.no_join[:], ALU.add))
                step(dve.tensor_reduce(s[:, 0:1], t[:], AX.X, ALU.max))
                step(dve.tensor_tensor(s[:, 1:2], s[:, 0:1], co.head[:, h : h + 1], ALU.max))
                step(dve.tensor_scalar(e[:], mrow, s[:, 1:2], 0.0, ALU.subtract, ALU.min))
                step(dve.tensor_tensor(s[:, 2:3], co.head[:, h : h + 1], s[:, 1:2], ALU.subtract))
                dve.nop().then_inc(exp_in, 1)
                dve.wait_ge(exped, h + 1)
                step(dve.tensor_tensor(w[:], e[:], k.join[:], ALU.mult))
                step(dve.tensor_tensor(w[:], w[:], zrow, ALU.mult))
                step(dve.tensor_reduce(s[:, 4:5], w[:], AX.X, ALU.add))
                step(dve.tensor_tensor(s[:, 5:6], s[:, 3:4], co.head[:, H + h : H + h + 1], ALU.mult))
                step(dve.tensor_tensor(s[:, 4:5], s[:, 4:5], s[:, 5:6], ALU.add))
                step(dve.tensor_scalar(s[:, 4:5], s[:, 4:5], 1.0e-30, None, ALU.max))
                step(dve.reciprocal(s[:, 6:7], s[:, 4:5]))
                step(dve.tensor_tensor(s[:, 7:8], s[:, 5:6], s[:, 6:7], ALU.mult))
                step(dve.tensor_scalar(w[:], w[:], s[:, 6:7], None, ALU.mult))
                dve.nop().then_inc(weighed, 1)
                dve.wait_ge(turned, h + 1)
                step(dve.tensor_copy(wt[:], ps[1][:, 0:P]))
                dve.nop().then_inc(untangled, 1)
                dve.wait_ge(summed, h + 1)
                step(dve.scalar_tensor_tensor(out[:, h, :], head[:, h, :], s[:, 7:8], ps[2][:, 0:W], ALU.mult, ALU.add))
                dve.nop().then_inc(out_of, 1)


X2 = D + 2
FEAT = (slice(0, D), slice(2, X2))
PAIR = (slice(D, X2), slice(0, 2))
SEEN = (slice(2, 2 + X2), slice(0, X2))


def fold_conv(k, l):
    nc, A = k.nc, k.a
    with ExitStack() as c:
        sb = lambda n, s, d=F32: c.enter_context(nc.sbuf_tensor(k.name(n), s, d))
        sem = lambda n: k.semaphore(n)
        wq = sb("wq", [P, 2, D])
        wk = sb("wk", [P, 2, D])
        wv = sb("wv", [P, 2, D])
        vb = sb("vb", [4, D])
        b3, rest, parts = sb("b3", [3, 2 * X2]), sb("rest", [3, 2 * X2]), sb("parts", [3, 3, 2 * X2])
        bq = sb("bq", [P, 2])
        wqt = sb("wqt", [P, 2, D])
        right = sb("right", [P, 2, X2])
        pt = [c.enter_context(nc.psum_tensor(k.name(f"pt{i}"), [P, 512], F32)) for i in range(2)]
        pm = [c.enter_context(nc.psum_tensor(k.name(f"pm{i}"), [P, 512], F32)) for i in range(2)]
        loaded, turned, copied, folded, done = [sem(n) for n in ("loaded", "turned", "copied", "folded", "done")]
        heads = lambda ap: ap.rearrange("i (h d) -> i h d", h=2)
        cols = lambda ap: ap.rearrange("(h d) -> d h", h=2)
        with nc.Block() as b:

            @b.sync
            def _(sp):
                with nc.allow_non_contiguous_dma(reason="two columns of biases"):
                    sp.dma_start(wq[:], heads(A["L1_gnn_Wq"][l])).then_inc(loaded, 16)
                    sp.dma_start(wk[:], heads(A["L1_gnn_Wk"][l])).then_inc(loaded, 16)
                    sp.dma_start(wv[:], heads(A["L1_gnn_Wv"][l])).then_inc(loaded, 16)
                    sp.dma_start(k.w_skip[:], A["L1_gnn_Wskip"][l]).then_inc(loaded, 16)
                    for h in range(2):
                        hd = slice(h * D, (h + 1) * D)
                        sp.dma_start(right[:, h, PAIR[h].start : PAIR[h].start + 1], A["L1_gnn_bk"][l, hd].unsqueeze(1)).then_inc(loaded, 16)
                        sp.dma_start(right[:, h, PAIR[h].start + 1 : PAIR[h].stop], A["L1_gnn_We"][l, 0, hd].unsqueeze(1)).then_inc(loaded, 16)
                        sp.dma_start(bq[:, h : h + 1], A["L1_gnn_bq"][l, hd].unsqueeze(1)).then_inc(loaded, 16)
                        sp.dma_start(vb[2 * h : 2 * h + 1, :], A["L1_gnn_bv"][l, hd].unsqueeze(0)).then_inc(loaded, 16)
                        sp.dma_start(vb[2 * h + 1 : 2 * h + 2, :], A["L1_gnn_We"][l, 0:1, hd]).then_inc(loaded, 16)
                    sp.dma_start(k.b_skip[0:1, :], A["L1_gnn_bskip"][l].unsqueeze(0)).then_inc(loaded, 16)
                    sp.dma_start(k.ln_g[:], A["L1_gnn_ln_g"][l].partition_broadcast(P)).then_inc(loaded, 16)
                    sp.dma_start(k.ln_b[:], A["L1_gnn_ln_b"][l].partition_broadcast(P)).then_inc(loaded, 16)
                sp.wait_ge(loaded, 16 * 17)

            @b.tensor
            def _(pe):
                pe.wait_ge(loaded, 16 * 17)
                for h in range(2):
                    pe.transpose(pt[0][:, h * D : (h + 1) * D], wq[:, h, :], k.ident[:])
                    pe.transpose(pt[1][:, h * D : (h + 1) * D], wk[:, h, :], k.ident[:]).then_inc(turned, 1)
                pe.wait_ge(copied, 2)
                for h in range(2):
                    pe.matmul(pm[0][:, h * X2 : (h + 1) * X2], wqt[:, h, :], right[:, h, :], start=True, stop=True)
                    pe.matmul(pm[1][0:3, h * X2 : (h + 1) * X2], bq[:, h : h + 1].to_broadcast([P, 3]), right[:, h, :], start=True,
                              stop=True).then_inc(folded, 1)

            @b.vector
            def _(dve):
                step = Chain(dve, done)
                dve.wait_ge(loaded, 16 * 17)
                dve.wait_ge(turned, 2)
                step(dve.tensor_copy(wqt[:], pt[0][:, 0 : 2 * D].rearrange("p (h d) -> p h d", h=2)))
                dve.nop().then_inc(copied, 1)
                for h in range(2):
                    step(dve.tensor_copy(right[:, h, FEAT[h]], pt[1][:, h * D : (h + 1) * D]))
                dve.nop().then_inc(copied, 1)
                step(dve.tensor_scalar(k.w_val[:], wv[:], 0.5, None, ALU.mult))
                step(dve.tensor_scalar(k.b_val[:], vb[:], 0.5, None, ALU.mult))
                dve.wait_ge(folded, 2)
                step(dve.tensor_copy(k.w_qk[:].rearrange("p h d -> p (h d)"), pm[0][:, 0 : 2 * X2]))
                step(dve.tensor_copy(b3[:], pm[1][0:3, 0 : 2 * X2]))
                split_in_three(step, dve, b3, rest, parts, k.b_qk, k.ident)


def conv_edges(k, table):
    nc = k.nc
    H = 2
    with ExitStack() as c:
        sb = lambda n, s, d=F32: c.enter_context(nc.sbuf_tensor(k.name(n), s, d))
        sem = lambda n: k.semaphore(n)
        psum = lambda n: c.enter_context(nc.psum_tensor(k.name(n), [P, 512], F32))
        rec = sb("rec", [P, UB, FIELDS, J], I32)
        xs = sb("xs", [P, UB, J, D + 4])
        xd = sb("xd", [P, UB, J, D])
        xdt = sb("xdt", [P, 2, D])
        junk = sb("junk", [P, 2, H, X2])
        st = sb("st", [P, RING, J, H, X2])
        at = sb("at", [P, 2, H * D])
        bt = sb("bt", [4, 2, P])
        head = sb("head", [P, H, X2])
        fix = sb("fix", [P, H, X2])
        mo = sb("mo", [P, RING, J, D])
        fo = sb("fo", [P, D])
        co = Coef(sb, H)
        p_t = [psum(f"p_t{i}") for i in range(2)]
        p_y = [psum(f"p_y{i}") for i in range(2)]
        p_a = [psum(f"p_a{i}") for i in range(2)]
        p_m = [psum(f"p_m{i}") for i in range(2)]
        rec_in = [sem(f"rec_in{u}") for u in range(UB)]
        got_in = [sem(f"got_in{u}") for u in range(UB)]
        put_out = [sem(f"put_out{u}") for u in range(RING)]
        xd_turned, xd_copied, y_made, scored = [sem(n) for n in ("xd_turned", "xd_copied", "y_made", "scored")]
        exp_in, exped, shares, weighted = [sem(n) for n in ("exp_in", "exped", "shares", "weighted")]
        st_turned, st_copied, m_made, m_out = [sem(n) for n in ("st_turned", "st_copied", "m_made", "m_out")]
        coef_done, state_done, head_done, begun = [sem(n) for n in ("coef_done", "state_done", "head_done", "begun")]
        wgt_done, passed = sem("wgt_done"), sem("passed")
        recf = rec[:].bitcast(F32)
        scale = float(D) ** -0.5

        def value_turn(pe, a, i):
            for h in range(H):
                pe.transpose(p_a[i][:, h * D : (h + 1) * D], a[:, h, FEAT[h]], k.ident[:])
            pair = a.rearrange("p h x -> p (h x)")[:, D : D + 4]
            return pe.transpose(p_a[i][0:4, 2 * D : 3 * D], pair, k.ident[:])

        def value_copy(act, i):
            act.activation(bt[:, i, :], p_a[i][0:4, 2 * D : 3 * D], ACT.Copy)
            return act.activation(at[:, i, :], p_a[i][:, 0 : 2 * D], ACT.Copy)

        def value_product(pe, i):
            pe.matmul(p_m[i][:, 0:D], at[:, i, 0:D], k.w_val[:, 0, :], start=True, stop=False)
            pe.matmul(p_m[i][:, 0:D], at[:, i, D : 2 * D], k.w_val[:, 1, :], start=False, stop=False)
            return pe.matmul(p_m[i][:, 0:D], bt[:, i, :], k.b_val[:], start=False, stop=True)

        chunks = lambda t, u: [Chunk(k, t, u, lag) for lag in (SCORE, SHARE, 0)]
        two = lambda c, j: (c.u * J + j) % 2

        with nc.Block() as b:

            @b.sync
            def _(sp):
                def one(t, u):
                    c = Chunk(k, t, u, EAHEAD)
                    if c.there:
                        wait(sp, head_done, (c.n - UB + 1) * J, passed)
                        load_records(sp, k, c, rec, rec_in)
                    c = Chunk(k, t, u)
                    if c.there:
                        wait(sp, m_out, (c.n + 1) * J, passed)
                        store_chunk(sp, k, c, mo, put_out)

                walk(k, sp, one, EAHEAD, 0)
                for u in range(RING):
                    sp.wait_ge(put_out[u], k.NB // RING * 16)

            @b.gpsimd
            def _(pool):
                def one(t, u):
                    c, i = Chunk(k, t, u), u % UB
                    wait(pool, rec_in[i], (c.use(UB) + 1) * 16, passed)
                    for j in range(J):
                        pool.indirect_dma_start(xs[:, i, j, 2 : 2 + D], None, table,
                                                bass.IndirectOffsetOnAxis(ap=rec[:, i, SRC, j : j + 1], axis=0)).then_inc(got_in[i], 16)
                        pool.indirect_dma_start(xd[:, i, j, :], None, table,
                                                bass.IndirectOffsetOnAxis(ap=rec[:, i, DST, j : j + 1], axis=0)).then_inc(got_in[i], 16)

                walk(k, pool, one, 0, 0)

            @b.tensor
            def _(pe):
                def turn_xd(c, j):
                    if j == 0:
                        pe.wait_ge(got_in[c.slot(UB)], (c.use(UB) + 1) * 32 * J)
                    wait(pe, xd_copied, c.n * J + j - 1)
                    pe.transpose(p_t[two(c, j)][:, 0:D], xd[:, c.slot(UB), j, :], k.ident[:]).then_inc(xd_turned, 1)

                def score_product(c, j):
                    pe.wait_ge(xd_copied, c.n * J + j + 1)
                    wait(pe, scored, c.n * J + j - 1)
                    y = p_y[two(c, j)][:, 0 : H * X2]
                    pe.matmul(y, xdt[:, two(c, j), :], k.w_qk[:].rearrange("p h d -> p (h d)"), start=True, stop=False)
                    pe.matmul(y, k.ones_bf[:], k.b_qk[:], start=False, stop=True).then_inc(y_made, 1)

                def turn_state(c, j):
                    pe.wait_ge(state_done, (c.n * J + j + 1) * H)
                    wait(pe, st_copied, c.n * J + j - 1)
                    value_turn(pe, st[:, c.slot(RING), j], two(c, j)).then_inc(st_turned, 1)

                def value(c, j):
                    pe.wait_ge(st_copied, c.n * J + j + 1)
                    wait(pe, m_out, c.n * J + j - 1)
                    value_product(pe, two(c, j)).then_inc(m_made, 1)

                def one(t, u):
                    for j in range(J):
                        for lag, shift, step in ((SCORE, 1, turn_xd), (SCORE, 0, score_product), (0, -1, turn_state), (0, -2, value)):
                            c, i = column(k, t, u, lag, j + shift)
                            if c.there:
                                step(c, i)

                walk(k, pe, one, SCORE + 1, 1)

            @b.scalar
            def _(act):
                def carry_xd(c, j):
                    act.wait_ge(xd_turned, c.n * J + j + 1)
                    wait(act, y_made, c.n * J + j - 1)
                    act.activation(xdt[:, two(c, j), :], p_t[two(c, j)][:, 0:D], ACT.Copy).then_inc(xd_copied, 1)

                def weigh(c, j):
                    if j == 0:
                        act.wait_ge(shares, c.n + 1)
                        wait(act, head_done, (c.n - RING + 1) * J)
                    for h in range(H):
                        ins = act.activation(st[:, c.slot(RING), j, h, :], xs[:, c.slot(UB), j, SEEN[h]], ACT.Copy,
                                             scale=co.b[:, c.slot(2), h, j : j + 1])
                    ins.then_inc(weighted, 1)

                def carry_state(c, j):
                    act.wait_ge(st_turned, c.n * J + j + 1)
                    wait(act, m_made, c.n * J + j - 1)
                    value_copy(act, two(c, j)).then_inc(st_copied, 1)

                def carry_message(c, j):
                    if j == 0:
                        wait(act, put_out[c.slot(RING)], c.use(RING) * 16)
                    act.wait_ge(m_made, c.n * J + j + 1)
                    act.activation(mo[:, c.slot(RING), j, :], p_m[two(c, j)][:, 0:D], ACT.Copy).then_inc(m_out, 1)

                def one(t, u):
                    for j in range(J):
                        mid = Chunk(k, t, u, SHARE)
                        if j == co.EXP and mid.there:
                            act.wait_ge(exp_in, mid.n + 1)
                            act.activation(co.ex[:], co.ex[:], ACT.Exp).then_inc(exped, 1)
                        for lag, shift, step in ((SCORE, 1, carry_xd), (0, -1, carry_state), (0, -2, carry_message), (0, 1, weigh)):
                            c, i = column(k, t, u, lag, j + shift)
                            if c.there:
                                step(c, i)

                walk(k, act, one, SCORE + 1, 1)

            @b.vector
            def _(dve):
                begin = Chain(dve, begun)
                co.begin(begin, dve)
                begin(dve.memset(head[:], 0.0))
                begin(dve.memset(st[:, RING - 1, J - 1], 0.0))
                for at_ in (0, D + 2):
                    begin(dve.memset(xs[:, :, :, at_ : at_ + 1], 1.0))
                coef, state, heads, wgt = Steps(dve, coef_done), Steps(dve, state_done), Steps(dve, head_done), Steps(dve, wgt_done)
                field = lambda c, f: recf[:, c.slot(UB), f, :]

                def score(c, j):
                    dve.wait_ge(y_made, c.n * J + j + 1)
                    wait(dve, scored, c.n * J + j - 1)
                    for h in range(H):
                        ins = dve.tensor_tensor_reduce(junk[:, two(c, j), h], p_y[two(c, j)][:, h * X2 : (h + 1) * X2],
                                                       xs[:, c.slot(UB), j, SEEN[h]], scale, 0.0, ALU.mult, ALU.add,
                                                       co.A[:, c.slot(2), h, 1 + j : 2 + j])
                    ins.then_inc(scored, 1)

                def add_state(c, j):
                    dve.wait_ge(weighted, c.n * J + j + 1)
                    state.land()
                    i = c.slot(RING)
                    prev = st[:, i, j - 1] if j else st[:, (i - 1) % RING, J - 1]
                    state.put(*[dve.scalar_tensor_tensor(st[:, i, j, h, :], prev[:, h, :], co.g[:, c.slot(2), h, j : j + 1],
                                                         st[:, i, j, h, :], ALU.mult, ALU.add) for h in range(H)])

                def add_head(c, j):
                    heads.land()
                    heads.put(dve.scalar_tensor_tensor(head[:], st[:, c.slot(RING), j], field(c, END)[:, j : j + 1], head[:],
                                                       ALU.mult, ALU.add))

                def one(t, u):
                    ahead, mid, c = chunks(t, u)
                    if ahead.there:
                        i = ahead.slot(UB)
                        wgt.at(ahead)
                        dve.wait_ge(got_in[i], (ahead.use(UB) + 1) * 32 * J)
                        wait(dve, weighted, (ahead.n - UB + 1) * J)
                        wgt(*[dve.tensor_copy(xs[:, i, :, at_ : at_ + 1], field(ahead, WGT).unsqueeze(2)) for at_ in (1, D + 3)])
                        wgt.end()
                    if mid.there:
                        coef.at(mid)
                        dve.wait_ge(scored, (mid.n + 1) * J)
                    if c.there:
                        state.at(c)
                        heads.at(c)

                    def coefficients(n):
                        if mid.there and n is not None:
                            co.level(n, coef, dve, mid.slot(2), field(mid, SAME), field(mid, END))

                    for j in range(J):
                        if mid.there and j == co.EXP:
                            coef.land()
                            dve.nop().then_inc(exp_in, 1)
                        if mid.there and j == 4:
                            dve.wait_ge(exped, mid.n + 1)
                        coefficients(co.EARLY.get(j))
                        if mid.there and j == 6:
                            dve.nop().then_inc(shares, 1)
                        if c.there:
                            add_state(c, j)
                        if ahead.there:
                            score(ahead, j)
                        coefficients(co.MIDDLE.get(j))
                        if c.there and j:
                            add_head(c, j - 1)
                    if mid.there:
                        coef.land()
                        coef.end()
                    if c.there:
                        state.land()
                        add_head(c, J - 1)
                        heads.land()
                        state.end()
                        heads.end()

                walk(k, dve, one, SCORE, 0)

        merge_softmax(k, sb, sem, [p_t[0], p_t[1], p_y[0]], co, st[:, RING - 1, J - 1], head, fix, X2)
        f_turned, f_copied, f_made, f_out, f_put = [sem(n) for n in ("f_turned", "f_copied", "f_made", "f_out", "f_put")]
        with nc.Block() as b:

            @b.tensor
            def _(pe):
                value_turn(pe, fix[:], 0).then_inc(f_turned, 1)
                pe.wait_ge(f_copied, 1)
                value_product(pe, 0).then_inc(f_made, 1)

            @b.scalar
            def _(act):
                act.wait_ge(f_turned, 1)
                value_copy(act, 0).then_inc(f_copied, 1)
                act.wait_ge(f_made, 1)
                act.activation(fo[:], p_m[0][:, 0:D], ACT.Copy).then_inc(f_out, 1)

            @b.gpsimd
            def _(pool):
                pool.wait_ge(f_out, 1)
                pool.indirect_dma_start(k.msg, bass.IndirectOffsetOnAxis(ap=k.join_row[:], axis=0), fo[:], None,
                                        bounds_check=k.NR - 1, oob_is_err=False).then_inc(f_put, 16)
                pool.wait_ge(f_put, 16)


def angle_edges(k, table):
    nc, A = k.nc, k.a
    H, W = 8, 16
    with ExitStack() as c:
        sb = lambda n, s, d=F32: c.enter_context(nc.sbuf_tensor(k.name(n), s, d))
        sem = lambda n: k.semaphore(n)
        psum = lambda n: c.enter_context(nc.psum_tensor(k.name(n), [P, 512], F32))
        rec = sb("rec", [P, UB, FIELDS, J], I32)
        x3 = sb("x3", [P, 3, UB, J, D])
        x3t = sb("x3t", [P, 2, 3 * D])
        q = sb("q", [P, 4, D])
        prod = sb("prod", [P, 2, D])
        st = sb("st", [P, RING, J, D])
        kept = sb("kept", [P, D])
        head = sb("head", [P, H, W])
        fix = sb("fix", [P, H, W])
        w_kv = sb("w_kv", [P, 2, D])
        w_q = sb("w_q", [P, D])
        w_ee = sb("w_ee", [P, D])
        b3, rest, parts = sb("b3", [3, 3 * D]), sb("rest", [3, 3 * D]), sb("parts", [3, 3, 3 * D])
        b_qkv = sb("b_qkv", [3, 3 * D], BF16)
        co = Coef(sb, H)
        p_t = [psum(f"p_t{i}") for i in range(2)]
        p_q = [psum(f"p_q{i}") for i in range(4)]
        p_v = [psum(f"p_v{i}") for i in range(2)]
        rec_in = [sem(f"rec_in{u}") for u in range(UB)]
        edge_in = [sem(f"edge_in{u}") for u in range(UB)]
        got_in = [sem(f"got_in{u}") for u in range(UB)]
        put_out = [sem(f"put_out{u}") for u in range(RING)]
        w_in, b_split, turned, copied, made, v_out = [sem(n) for n in ("w_in", "b_split", "turned", "copied", "made", "v_out")]
        exp_in, exped, scored, q_out, f_put = [sem(n) for n in ("exp_in", "exped", "scored", "q_out", "f_put")]
        coef_done, state_done, head_done, begun = [sem(n) for n in ("coef_done", "state_done", "head_done", "begun")]
        reduced, share_done, passed = sem("reduced"), sem("share_done"), sem("passed")
        recf = rec[:].bitcast(F32)
        scale = float(W) ** -0.5
        edge = rows(A["edge"], J)
        heads = lambda ap: ap.rearrange("p (h w) -> p h w", h=H)
        chunks = lambda t, u: [Chunk(k, t, u, lag) for lag in (SCORE, SHARE, 0)]
        two, four = lambda c, j: (c.u * J + j) % 2, lambda c, j: (c.u * J + j) % 4
        with nc.Block() as b:

            @b.sync
            def _(sp):
                sp.dma_start(w_kv[:, 0, :], A["L3_gnn_Wk"]).then_inc(w_in, 16)
                sp.dma_start(w_kv[:, 1, :], A["L3_gnn_Wv"]).then_inc(w_in, 16)
                sp.dma_start(w_q[:], A["L3_gnn_Wq"]).then_inc(w_in, 16)
                sp.dma_start(w_ee[:], A["L3_gnn_We"]).then_inc(w_in, 16)
                for i, name in enumerate(("L3_gnn_bq", "L3_gnn_bk", "L3_gnn_bv")):
                    sp.dma_start(b3[:, i * D : (i + 1) * D], A[name].partition_broadcast(3)).then_inc(w_in, 16)

                def one(t, u):
                    c = Chunk(k, t, u, EAHEAD)
                    if c.there:
                        wait(sp, head_done, (c.n - UB + 1) * J, passed)
                        load_records(sp, k, c, rec, rec_in)
                        sp.dma_start(x3[:, 2, c.slot(UB)].rearrange("p j d -> p (j d)"), edge[:, c.n, :]).then_inc(edge_in[c.slot(UB)], 16)
                    c = Chunk(k, t, u)
                    if c.there:
                        wait(sp, state_done, (c.n + 1) * J * 2, passed)
                        store_chunk(sp, k, c, st, put_out)

                walk(k, sp, one, EAHEAD, 0)
                for u in range(RING):
                    sp.wait_ge(put_out[u], k.NB // RING * 16)

            @b.gpsimd
            def _(pool):
                def one(t, u):
                    c, i = Chunk(k, t, u), u % UB
                    wait(pool, rec_in[i], (c.use(UB) + 1) * 16, passed)
                    for j in range(J):
                        for s, f in ((0, SRC), (1, DST)):
                            pool.indirect_dma_start(x3[:, s, i, j, :], None, table,
                                                    bass.IndirectOffsetOnAxis(ap=rec[:, i, f, j : j + 1], axis=0)).then_inc(got_in[i], 16)

                walk(k, pool, one, 0, 0)

            @b.tensor
            def _(pe):
                pe.wait_ge(w_in, 16 * 7)
                pe.wait_ge(b_split, 1)

                def turn(c, j):
                    if j == 0:
                        pe.wait_ge(got_in[c.slot(UB)], (c.use(UB) + 1) * 32 * J)
                        pe.wait_ge(edge_in[c.slot(UB)], (c.use(UB) + 1) * 16)
                    wait(pe, copied, c.n * J + j - 1)
                    for s in range(3):
                        ins = pe.transpose(p_t[two(c, j)][:, s * D : (s + 1) * D], x3[:, s, c.slot(UB), j, :], k.ident[:])
                    ins.then_inc(turned, 1)

                def product(c, j):
                    i, n_q = two(c, j), four(c, j)
                    pe.wait_ge(copied, c.n * J + j + 1)
                    wait(pe, v_out, c.n * J + j - 1)
                    wait(pe, scored, c.n * J + j - 3)
                    tj = x3t[:, i, :]
                    src, dst_, own = tj[:, 0:D], tj[:, D : 2 * D], tj[:, 2 * D : 3 * D]
                    for o, terms, at_ in ((p_q[n_q][:, 0:D], [(dst_, w_q[:])], 0),
                                          (p_q[n_q][:, D : 2 * D], [(src, w_kv[:, 0, :]), (own, w_ee[:])], 1),
                                          (p_v[i][:, 0:D], [(src, w_kv[:, 1, :]), (own, w_ee[:])], 2)):
                        for n, (rows_, w) in enumerate(terms):
                            pe.matmul(o, rows_, w, start=n == 0, stop=False)
                        ins = pe.matmul(o, k.ones_bf[:], b_qkv[:, at_ * D : (at_ + 1) * D], start=False, stop=True)
                    ins.then_inc(made, 1)

                def one(t, u):
                    for j in range(J):
                        for shift, step in ((1, turn), (0, product)):
                            c, i = column(k, t, u, SCORE, j + shift)
                            if c.there:
                                step(c, i)

                walk(k, pe, one, SCORE + 1, 0)

            @b.scalar
            def _(act):
                def carry(c, j):
                    act.wait_ge(turned, c.n * J + j + 1)
                    wait(act, made, c.n * J + j - 1)
                    act.activation(x3t[:, two(c, j), :], p_t[two(c, j)][:, 0 : 3 * D], ACT.Copy).then_inc(copied, 1)

                def values(c, j):
                    if j == 0:
                        wait(act, head_done, (c.n - RING + 1) * J)
                        wait(act, put_out[c.slot(RING)], c.use(RING) * 16)
                    act.wait_ge(made, c.n * J + j + 1)
                    act.activation(q[:, four(c, j), :], p_q[four(c, j)][:, 0:D], ACT.Copy, scale=scale).then_inc(q_out, 1)
                    act.activation(st[:, c.slot(RING), j, :], p_v[two(c, j)][:, 0:D], ACT.Copy).then_inc(v_out, 1)

                def one(t, u):
                    mid = Chunk(k, t, u, SHARE)
                    for j in range(J):
                        if j == co.EXP and mid.there:
                            act.wait_ge(exp_in, mid.n + 1)
                            act.activation(co.ex[:], co.ex[:], ACT.Exp).then_inc(exped, 1)
                        for shift, step in ((1, carry), (0, values)):
                            c, i = column(k, t, u, SCORE, j + shift)
                            if c.there:
                                step(c, i)

                walk(k, act, one, SCORE + 1, 0)

            @b.vector
            def _(dve):
                begin = Chain(dve, begun)
                co.begin(begin, dve)
                begin(dve.memset(head[:], 0.0))
                begin(dve.memset(st[:, RING - 1, J - 1], 0.0))
                dve.wait_ge(w_in, 16 * 7)
                split_in_three(begin, dve, b3, rest, parts, b_qkv, k.ident)
                dve.nop().then_inc(b_split, 1)
                coef, state, heads_, sums, share = [Steps(dve, x) for x in (coef_done, state_done, head_done, reduced, share_done)]
                field = lambda c, f: recf[:, c.slot(UB), f, :]

                def products(c, j):
                    i = four(c, j)
                    dve.wait_ge(q_out, c.n * J + j + 1)
                    sums.land()
                    dve.tensor_tensor(prod[:, two(c, j), :], q[:, i, :], p_q[i][:, D : 2 * D], ALU.mult).then_inc(scored, 1)

                def reduce(c, j):
                    dve.wait_ge(scored, c.n * J + j + 1)
                    sums.put(dve.tensor_reduce(co.A[:, c.slot(2), :, 1 + j : 2 + j], heads(prod[:, two(c, j), :]), AX.X, ALU.add))

                def keep(c, j):
                    i = c.slot(RING)
                    prev = st[:, i, j - 1, :] if j else st[:, (i - 1) % RING, J - 1, :]
                    state.land()
                    state.put(dve.tensor_tensor(heads(kept[:]), heads(prev), co.g[:, c.slot(2), :, j : j + 1].to_broadcast([P, H, W]), ALU.mult))

                def add_state(c, j):
                    v = st[:, c.slot(RING), j, :]
                    state.land()
                    state.put(dve.tensor_tensor(v, v, kept[:], ALU.add))

                def add_head(c, j):
                    flat = head[:].rearrange("p h w -> p (h w)")
                    heads_.land()
                    heads_.put(dve.scalar_tensor_tensor(flat, st[:, c.slot(RING), j, :], field(c, END)[:, j : j + 1], flat, ALU.mult, ALU.add))

                def one(t, u):
                    ahead, mid, c = chunks(t, u)
                    if mid.there:
                        coef.at(mid)
                        share.at(mid)
                        dve.wait_ge(reduced, (mid.n + 1) * J)
                    if ahead.there:
                        sums.at(ahead)
                        dve.wait_ge(rec_in[ahead.slot(UB)], (ahead.use(UB) + 1) * 16)
                    if c.there:
                        state.at(c)
                        heads_.at(c)

                    def coefficients(n):
                        if mid.there and n is not None:
                            co.level(n, coef, dve, mid.slot(2), field(mid, SAME), field(mid, END))

                    for j in range(J):
                        if mid.there and j == co.EXP:
                            coef.land()
                            dve.nop().then_inc(exp_in, 1)
                        if mid.there and j == 4:
                            dve.wait_ge(exped, mid.n + 1)
                        coefficients(co.EARLY.get(j))
                        if c.there:
                            keep(c, j)
                        if ahead.there:
                            products(ahead, j)
                        if c.there:
                            add_state(c, j)
                        if ahead.there:
                            reduce(ahead, j)
                        coefficients(co.MIDDLE.get(j))
                        if c.there and j:
                            add_head(c, j - 1)
                    if mid.there:
                        coef.land()
                        dve.wait_ge(v_out, (mid.n + 1) * J)
                        v = st[:, mid.slot(RING)].rearrange("p j (h w) -> p j h w", h=H)
                        share.put(dve.tensor_tensor(v, v, co.b[:, mid.slot(2)].rearrange("p h j -> p j h").unsqueeze(3).to_broadcast([P, J, H, W]), ALU.mult))
                    if c.there:
                        state.land()
                        add_head(c, J - 1)
                        heads_.land()
                        state.end()
                        heads_.end()
                    if ahead.there:
                        sums.end()
                    if mid.there:
                        share.land()
                        coef.end()
                        share.end()

                walk(k, dve, one, SCORE, 0)

        merge_softmax(k, sb, sem, [p_t[0], p_t[1], p_q[0]], co, heads(st[:, RING - 1, J - 1, :]), head, fix, W)
        with nc.Block() as b:

            @b.gpsimd
            def _(pool):
                pool.indirect_dma_start(k.msg, bass.IndirectOffsetOnAxis(ap=k.join_row[:], axis=0),
                                        fix[:].rearrange("p h w -> p (h w)"), None,
                                        bounds_check=k.NR - 1, oob_is_err=False).then_inc(f_put, 16)
                pool.wait_ge(f_put, 16)


class Norm:

    def __init__(self, k, c, i):
        sb = lambda n, s, d=F32: c.enter_context(k.nc.sbuf_tensor(k.name(n), s, d))
        self.k = k
        self.keep = None
        self.raw = sb(f"raw{i}", [P, JN, 6])
        self.mv = sb(f"mv{i}", [P, JN, 2])
        self.s = sb(f"norm{i}", [P, RING, 3, JN])
        self.passed = k.semaphore(f"passed{i}")
        self.radicand, self.powed = k.semaphore(f"radicand{i}"), k.semaphore(f"powed{i}")
        self.rooted, self.applied = k.semaphore(f"rooted{i}"), k.semaphore(f"applied{i}")

    def stats(self, dve, step, c, v):
        s = self.s[:, c.slot(RING)]
        step(*[dve.bn_stats(out=self.raw[:, r, :], in_=v[:, r, :]) for r in range(JN)])
        step.before_form_without_wait(self.passed)
        step(*[dve.bn_aggr(out=self.mv[:, r, :], in_=self.raw[:, r, :]) for r in range(JN)])
        wait(dve, self.applied, c.n - RING + 1)
        step(dve.tensor_scalar(s[:, 0, :], self.mv[:, :, 0], -1.0, None, ALU.mult),
             dve.tensor_scalar(s[:, 1, :], self.mv[:, :, 1], EPS, None, ALU.add),
             *([] if self.keep is None else [dve.tensor_copy(self.keep, self.mv[:, :, 1])]))
        dve.nop().then_inc(self.radicand, 1)

    def root(self, pool, c):
        s = self.s[:, c.slot(RING)]
        pool.wait_ge(self.radicand, c.n + 1)
        pool.tensor_tensor(s[:, 1, :], s[:, 1, :], wide(self.k.root[:], JN), ALU.pow).then_inc(self.powed, 1)
        pool.wait_ge(self.powed, c.n + 1)
        pool.tensor_tensor(s[:, 2, :], s[:, 0, :], s[:, 1, :], ALU.mult).then_inc(self.rooted, 1)

    def apply(self, act, c, v, o):
        s = self.s[:, c.slot(RING)]
        act.wait_ge(self.rooted, c.n + 1)
        for r in range(JN):
            ins = act.activation(o[:, r, :], v[:, r, :], ACT.Identity, bias=s[:, 2, r : r + 1], scale=s[:, 1, r : r + 1])
        ins.then_inc(self.applied, 1)


class NormTwice(Norm):

    STEPS = 5

    def __init__(self, k, c, i):
        super().__init__(k, c, i)
        self.var = c.enter_context(k.nc.sbuf_tensor(k.name("var"), [P, RING, JN], F32))
        self.s2 = c.enter_context(k.nc.sbuf_tensor(k.name("norm_twice"), [P, RING, 2, JN], F32))
        self.stepped, self.rooted2, self.applied2 = [k.semaphore(n) for n in ("stepped", "rooted2", "applied2")]

    def stats(self, dve, step, c, v):
        wait(dve, self.applied2, c.n - RING + 1)
        self.keep = self.var[:, c.slot(RING)]
        super().stats(dve, step, c, v)

    def root(self, pool, c):
        super().root(pool, c)
        i = c.slot(RING)
        neg_mean, inv = self.s[:, i, 0, :], self.s[:, i, 1, :]
        var, scale, shift = self.var[:, i], self.s2[:, i, 0, :], self.s2[:, i, 1, :]
        eps = wide(self.k.eps[:], JN)
        steps = [(scale, var, inv, ALU.mult), (scale, scale, inv, ALU.mult), (scale, scale, eps, ALU.add),
                 (scale, scale, wide(self.k.root[:], JN), ALU.pow), (scale, scale, inv, ALU.mult)]
        for n, (o, a, b, op) in enumerate(steps):
            pool.tensor_tensor(o, a, b, op).then_inc(self.stepped, 1)
            pool.wait_ge(self.stepped, c.n * self.STEPS + n + 1)
        pool.tensor_tensor(shift, neg_mean, scale, ALU.mult).then_inc(self.rooted2, 1)

    def apply_twice(self, act, c, v, o):
        act.wait_ge(self.rooted2, c.n + 1)
        for r in range(JN):
            ins = act.activation(o[:, r, :], v[:, r, :], ACT.Identity, bias=self.s2[:, c.slot(RING), 1, r : r + 1],
                                 scale=self.s2[:, c.slot(RING), 0, r : r + 1])
        ins.then_inc(self.applied2, 1)


class Nodes:

    def __init__(self, k, c, n_in, n_out, n_src, message=1):
        nc = self.nc = k.nc
        self.k, self.c = k, c
        sem = lambda n: k.semaphore(n)
        psum = lambda n: c.enter_context(nc.psum_tensor(k.name(n), [P, 512], F32))
        self.x = [self.ring(f"in{i}", UB) for i in range(n_in)]
        self.o = [self.ring(f"out{i}", RING) for i in range(n_out)]
        self.n_in, self.n_out, self.n_src = n_in - message, n_out, n_src
        if n_src:
            self.z = self.ring("z", RING)
            self.xt = c.enter_context(nc.sbuf_tensor(k.name("xt"), [P, 2, n_src, 4 * D], F32))
            self.p_t = [[psum(f"p_t{i}{s}") for s in range(n_src)] for i in range(2)]
            self.p_m = [psum(f"p_m{i}") for i in range(2)]
        self.loaded = [sem(f"loaded{u}") for u in range(UB)]
        self.stored = [sem(f"stored{u}") for u in range(RING)]
        self.prepped, self.turned, self.copied = sem("prepped"), sem("turned"), sem("copied")
        self.made, self.z_in, self.passed = sem("made"), sem("z_in"), sem("passed")
        self.finished, self.idx_in = sem("finished"), sem("idx_in")
        self.got = [sem(f"got{u}") for u in range(UB)]
        self.idx = c.enter_context(nc.sbuf_tensor(k.name("idx"), [P, UB, JN], I32))
        self.z_free = None

    def ring(self, name, n, d=D):
        return self.c.enter_context(self.nc.sbuf_tensor(self.k.name(name), [P, n, JN, d], F32))

    def wait_loaded(self, eng, c):
        eng.wait_ge(self.loaded[c.slot(UB)], (c.use(UB) + 1) * 16 * self.n_in)

    def wait_message(self, eng, c):
        eng.wait_ge(self.got[c.slot(UB)], (c.use(UB) + 1) * 16 * JN)

    def wait_stored(self, eng, c):
        wait(eng, self.stored[c.slot(RING)], c.use(RING) * 16 * self.n_out)

    def run(self, ins, outs, srcs, weights, bias, dve_stages, act_stages, pool_stages, prep=False, pe_stages=(), begin=None, with_row=None):
        k, nc, n_src = self.k, self.nc, self.n_src
        chunk = lambda t, u, lag=0: Chunk(k, t, u, lag)

        def run_stages(eng, stages, t, u):
            for lag, stage in stages:
                c = chunk(t, u, lag)
                if c.there:
                    stage(eng, c)

        with nc.Block() as b:

            @b.sync
            def _(sp):
                def one(t, u):
                    c = chunk(t, u, AHEAD)
                    if c.there:
                        wait(sp, self.finished, c.n - UB + 1, self.passed)
                        for i, table in enumerate(ins):
                            if table is k.msg:
                                continue
                            sp.dma_start(self.x[i][:, c.slot(UB)].rearrange("p j d -> p (j d)"),
                                         rows(table)[:, c.n, :]).then_inc(self.loaded[c.slot(UB)], 16)
                    c = chunk(t, u, -DRAIN)
                    if c.there:
                        wait(sp, self.finished, c.n + 1, self.passed)
                        for i, table in enumerate(outs):
                            sp.dma_start(rows(table)[:, c.n, :],
                                         self.o[i][:, c.slot(RING)].rearrange("p j d -> p (j d)")).then_inc(self.stored[c.slot(RING)], 16)

                walk(k, sp, one, LEAD, DRAIN)
                for u in range(RING):
                    sp.wait_ge(self.stored[u], k.NB // RING * 16 * len(outs))

            @b.tensor
            def _(pe):
                def turn(c, g):
                    a, z = GROUPS[g]
                    if g == 0:
                        self.wait_loaded(pe, c)
                        if prep:
                            pe.wait_ge(self.prepped, c.n + 1)
                    wait(pe, self.copied, c.n * NG + g - 1)
                    for s, x in enumerate(srcs(c)):
                        for r in range(a, z):
                            ins_ = pe.transpose(self.p_t[g % 2][s][:, (r - a) * D : (r - a + 1) * D], x[:, r, :], k.ident[:])
                    ins_.then_inc(self.turned, 1)

                def product(c, g):
                    a, z = GROUPS[g]
                    pe.wait_ge(self.copied, c.n * NG + g + 1)
                    wait(pe, self.z_in, c.n * NG + g - 1)
                    for r in range(z - a):
                        o = self.p_m[g % 2][:, r * D : (r + 1) * D]
                        for s in range(n_src):
                            pe.matmul(o, self.xt[:, g % 2, s, r * D : (r + 1) * D], weights[s][:], start=s == 0, stop=False)
                        if with_row:
                            with_row(pe, c, a + r, self.xt[:, g % 2, 0, r * D : (r + 1) * D])
                        ins_ = pe.matmul(o, k.ones[0:1, :], bias[0:1, :], start=False, stop=True)
                    ins_.then_inc(self.made, 1)

                def one(t, u):
                    if n_src:
                        for g in range(NG):
                            nxt = chunk(t, u, 1 + (g + 1) // NG)
                            if nxt.there:
                                turn(nxt, (g + 1) % NG)
                            c = chunk(t, u, 1)
                            if c.there:
                                product(c, g)
                    run_stages(pe, pe_stages, t, u)

                walk(k, pe, one, LEAD, DRAIN)

            @b.scalar
            def _(act):
                def carry_turned(c, g):
                    a, z = GROUPS[g]
                    act.wait_ge(self.turned, c.n * NG + g + 1)
                    wait(act, self.made, c.n * NG + g - 1)
                    for s in range(n_src):
                        ins_ = act.activation(self.xt[:, g % 2, s, 0 : (z - a) * D], self.p_t[g % 2][s][:, 0 : (z - a) * D], ACT.Copy)
                    ins_.then_inc(self.copied, 1)

                def carry_product(c, g):
                    a, z = GROUPS[g]
                    act.wait_ge(self.made, c.n * NG + g + 1)
                    if g == 0 and self.z_free is not None:
                        wait(act, self.z_free, c.n - RING + 1)
                    act.activation(self.z[:, c.slot(RING), a:z, :].rearrange("p j d -> p (j d)"),
                                   self.p_m[g % 2][:, 0 : (z - a) * D], ACT.Copy).then_inc(self.z_in, 1)

                def one(t, u):
                    half = len(act_stages) // 2
                    for g in range(NG):
                        if n_src:
                            nxt = chunk(t, u, 1 + (g + 1) // NG)
                            if nxt.there:
                                carry_turned(nxt, (g + 1) % NG)
                        run_stages(act, act_stages[:half] if g == 0 else act_stages[half:], t, u)
                        if n_src:
                            c = chunk(t, u, 1)
                            if c.there:
                                carry_product(c, g)

                walk(k, act, one, LEAD, DRAIN)

            @b.gpsimd
            def _(pool):
                def gather(c, js):
                    for j in js:
                        pool.indirect_dma_start(x[:, c.slot(UB), j, :], None, k.msg,
                                                bass.IndirectOffsetOnAxis(ap=self.idx[:, c.slot(UB), j : j + 1], axis=0)).then_inc(self.got[c.slot(UB)], 16)

                def begin_message(pool, c):
                    wait(pool, self.finished, c.n - UB + 1, self.passed)
                    pool.tensor_copy(self.idx[:, c.slot(UB), :], k.last[:, c.n, :]).then_inc(self.idx_in, 1)
                    wait(pool, self.idx_in, c.n + 1, self.passed)
                    gather(c, range(0, JN // 2))

                def end_message(pool, c):
                    gather(c, range(JN // 2, JN))

                stages = list(pool_stages)
                if any(table is k.msg for table in ins):
                    x = self.x[[table is k.msg for table in ins].index(True)]
                    half = (len(stages) + 1) // 2
                    stages = [(AHEAD, begin_message)] + stages[:half] + [(AHEAD, end_message)] + stages[half:]
                walk(k, pool, lambda t, u: run_stages(pool, stages, t, u), LEAD, DRAIN)

            @b.vector
            def _(dve):
                if begin:
                    begin(dve)
                steps = [Steps(dve, k.semaphore(f"done{i}")) for i in range(len(dve_stages))]

                def one(t, u):
                    for step, (lag, stage) in zip(steps, dve_stages):
                        c = chunk(t, u, lag)
                        if c.there:
                            step.at(c)
                            stage(dve, step, c)
                            step.end()

                walk(k, dve, one, LEAD, DRAIN)

    def wait_z(self, dve, c):
        dve.wait_ge(self.z_in, (c.n + 1) * NG)


def load_rows(k, pairs):
    nc = k.nc
    with ExitStack() as c:
        loaded = k.semaphore("loaded")
        with nc.Block() as b:

            @b.sync
            def _(sp):
                for tile, ap in pairs:
                    sp.dma_start(tile, ap).then_inc(loaded, 16)
                sp.wait_ge(loaded, 16 * len(pairs))


def gcn_nodes(k):
    nc, A = k.nc, k.a
    bc = lambda n: A[n].partition_broadcast(P)
    with ExitStack() as c:
        sb = lambda n, s: c.enter_context(nc.sbuf_tensor(k.name(n), s, F32))
        g2, b2 = sb("g2", [P, D]), sb("b2", [P, D])
        load_rows(k, [(k.w_skip[:], A["L0_gnn_W"]), (k.b_skip[0:1, :], A["L0_gnn_b"].unsqueeze(0)),
                      (k.ln_g[:], bc("L0_gnn_ln_gamma")), (k.ln_b[:], bc("L0_gnn_ln_beta")),
                      (g2[:], bc("L1_gnn_ln_in_g")), (b2[:], bc("L1_gnn_ln_in_b"))])
        n = Nodes(k, c, 3, 2, 1)
        first, second = Norm(k, c, 0), NormTwice(k, c, 1)
        summed, y = n.ring("summed", 4), n.ring("y", RING)
        dinv = k.dinv[:].rearrange("p (b j) -> p b j", j=JN)
        R = lambda t, c: t[:, c.slot(RING)]
        every = lambda g: g[:].unsqueeze(1).to_broadcast([P, JN, D])

        def prep(dve, step, c):
            n.wait_loaded(dve, c)
            n.wait_message(dve, c)
            i, o = c.slot(UB), summed[:, c.slot(4)]
            wait(dve, n.turned, (c.n - 3) * NG)
            step(dve.tensor_tensor(o, n.x[0][:, i], n.x[1][:, i], ALU.add))
            step(dve.tensor_tensor(o, o, dinv[:, c.n, :].unsqueeze(2).to_broadcast([P, JN, D]), ALU.mult))
            dve.nop().then_inc(n.prepped, 1)

        def gcn(dve, step, c):
            n.wait_z(dve, c)
            first.stats(dve, step, c, R(n.z, c))

        def residual(dve, step, c):
            v = R(y, c)
            dve.wait_ge(first.applied, c.n + 1)
            step(dve.tensor_tensor(v, v, every(k.ln_g), ALU.mult))
            step(dve.tensor_tensor(v, v, every(k.ln_b), ALU.add))
            step(dve.scalar_tensor_tensor(v, v, 0.0, n.x[2][:, c.slot(UB)], ALU.max, ALU.add))
            second.stats(dve, step, c, v)

        def finish(dve, step, c):
            o = R(n.o[1], c)
            dve.wait_ge(second.applied2, c.n + 1)
            step(dve.tensor_tensor(o, o, every(g2), ALU.mult))
            step(dve.tensor_tensor(o, o, every(b2), ALU.add))
            dve.nop().then_inc(n.finished, 1)

        def apply_second(act, c):
            n.wait_stored(act, c)
            second.apply(act, c, R(y, c), R(n.o[0], c))
            second.apply_twice(act, c, R(y, c), R(n.o[1], c))

        n.z_free = first.applied
        n.run([k.msg, k.tab[0], A["x"]], [k.res, k.tab[1]], lambda c: [summed[:, c.slot(4)]], [k.w_skip], k.b_skip,
              [(2, prep), (0, gcn), (-1, residual), (-2, finish)],
              [(-2, apply_second), (0, lambda act, c: first.apply(act, c, R(n.z, c), R(y, c)))],
              [(0, first.root), (-1, second.root)], prep=True)


def conv_nodes(k, src, dst, last):
    nc = k.nc
    with ExitStack() as c:
        n = Nodes(k, c, 3 if last else 2, 1, 1)
        e, y = n.ring("e", RING), n.ring("y", RING)
        norms = [Norm(k, c, i) for i in range(2 if last else 1)]
        e_in, e_out = k.semaphore("e_in"), k.semaphore("e_out")
        R = lambda t, c: t[:, c.slot(RING)]
        every = lambda g: g[:].unsqueeze(1).to_broadcast([P, JN, D])

        def message(dve, step, c):
            z = R(n.z, c)
            n.wait_z(dve, c)
            n.wait_message(dve, c)
            step(dve.tensor_tensor(z, z, n.x[1][:, c.slot(UB)], ALU.add))
            step(dve.tensor_scalar(R(e, c), z, 0.0, None, ALU.min))
            dve.nop().then_inc(e_in, 1)

        def exponential(act, c):
            act.wait_ge(e_in, c.n + 1)
            act.activation(R(e, c), R(e, c), ACT.Exp).then_inc(e_out, 1)

        def residual(dve, step, c):
            z, v = R(n.z, c), R(y, c)
            dve.wait_ge(e_out, c.n + 1)
            wait(dve, norms[-1].applied, c.n - RING + 1)
            step(dve.scalar_tensor_tensor(v, z, 0.0, R(e, c), ALU.max, ALU.add))
            step(dve.scalar_tensor_tensor(v, v, -1.0, n.x[0][:, c.slot(UB)], ALU.add, ALU.add))
            norms[0].stats(dve, step, c, v)

        def affine(dve, step, c):
            v = R(y if last else n.o[0], c)
            dve.wait_ge(norms[0].applied, c.n + 1)
            step(dve.tensor_tensor(v, v, every(k.ln_g), ALU.mult))
            step(dve.tensor_tensor(v, v, every(k.ln_b), ALU.add))
            if last:
                step(dve.tensor_tensor(v, v, n.x[2][:, c.slot(UB)], ALU.add))
                norms[1].stats(dve, step, c, v)
            else:
                dve.nop().then_inc(n.finished, 1)

        def apply_first(act, c):
            if not last:
                n.wait_stored(act, c)
            norms[0].apply(act, c, R(y, c), R(y if last else n.o[0], c))

        def apply_last(act, c):
            n.wait_stored(act, c)
            norms[1].apply(act, c, R(y, c), R(n.o[0], c))

        n.z_free = norms[0].radicand
        if last:
            n.finished = norms[1].applied
        n.run([src, k.msg] + ([k.res] if last else []), [dst], lambda c: [n.x[0][:, c.slot(UB)]], [k.w_skip], k.b_skip,
              [(0, message), (-1, residual), (-2, affine)],
              [(-2, apply_first)] + ([(-3, apply_last)] if last else []) + [(0, exponential)],
              [(-1, norms[0].root)] + ([(-2, norms[1].root)] if last else []))


def sage_nodes(k):
    nc, A = k.nc, k.a
    with ExitStack() as c:
        sb = lambda n, s, d=F32: c.enter_context(nc.sbuf_tensor(k.name(n), s, d))
        sem = lambda n: k.semaphore(n)
        w = sb("w", [P, 2, D])
        wt = sb("wt", [P, 2, D])
        gb = sb("gb", [1, 2, D])
        real_i = sb("real_i", [P, k.COLS], I32)
        real = sb("real", [P, k.COLS])
        load_rows(k, [(w[:, 0, :], A["L2_gnn_W_l"]), (w[:, 1, :], A["L2_gnn_W_r"]), (k.b_skip[0:1, :], A["L2_gnn_b_l"].unsqueeze(0)),
                      (gb[:, 0, :], A["L2_gnn_gamma"].unsqueeze(0)), (gb[:, 1, :], A["L2_gnn_beta"].unsqueeze(0))])
        with ExitStack() as c2:
            turned, row_no, done = [k.semaphore(s) for s in ("turned", "row_no", "done")]
            pw = c2.enter_context(nc.psum_tensor(k.name("pw"), [P, 512], F32))
            with nc.Block() as b:

                @b.tensor
                def _(pe):
                    pe.transpose(pw[:, 0:D], w[:, 0, :], k.ident[:])
                    pe.transpose(pw[:, D : 2 * D], w[:, 1, :], k.ident[:]).then_inc(turned, 1)

                @b.gpsimd
                def _(pool):
                    pool.iota(real_i[:], pattern=[[1, k.COLS]], base=0, channel_multiplier=k.COLS).then_inc(row_no, 1)

                @b.vector
                def _(dve):
                    step = Chain(dve, done)
                    dve.wait_ge(turned, 1)
                    step(dve.tensor_copy(wt[:].rearrange("p s d -> p (s d)"), pw[:, 0 : 2 * D]))
                    dve.wait_ge(row_no, 1)
                    step(dve.tensor_copy(real[:], real_i[:]))
                    step(dve.tensor_scalar(real[:], real[:], float(k.N), None, ALU.is_lt))

        n = Nodes(k, c, 2, 1, 2)
        p_s = [c.enter_context(nc.psum_tensor(k.name(f"p_s{i}"), [P, 512], F32)) for i in range(2)]
        row = sb("row", [1, 6, D])
        mean, sq, o2 = n.ring("mean", 4), n.ring("sq", RING), n.ring("o2", RING)
        inv = sb("inv", [P, RING, JN])
        squared, radicand, rooted, scaled, both, counted = [
            sem(x) for x in ("squared", "radicand", "rooted", "scaled", "both", "counted")]
        R = lambda t, c: t[:, c.slot(RING)]
        part = lambda t: t[:].rearrange("p (b j) -> p b j", j=JN)
        wide3 = lambda a: a.unsqueeze(2).to_broadcast([P, JN, D])

        def prep(dve, step, c):
            n.wait_message(dve, c)
            wait(dve, n.turned, (c.n - 3) * NG)
            step(dve.tensor_tensor(mean[:, c.slot(4)], n.x[0][:, c.slot(UB)], wide3(part(k.rcnt)[:, c.n, :]), ALU.mult))
            dve.nop().then_inc(n.prepped, 1)

        def square(act, c):
            act.wait_ge(n.z_in, (c.n + 1) * NG)
            act.activation(R(sq, c), R(n.z, c), ACT.Square).then_inc(squared, 1)

        def length(dve, step, c):
            dve.wait_ge(squared, c.n + 1)
            step(dve.tensor_reduce(R(inv, c), R(sq, c), AX.X, ALU.add))
            step(dve.tensor_scalar(R(inv, c), R(inv, c), 1.0e-24, None, ALU.max))
            dve.nop().then_inc(radicand, 1)

        def root(pool, c):
            pool.wait_ge(radicand, c.n + 1)
            pool.tensor_tensor(R(inv, c), R(inv, c), wide(k.root[:], JN), ALU.pow).then_inc(rooted, 1)

        def scale(dve, step, c):
            dve.wait_ge(rooted, c.n + 1)
            n.wait_stored(dve, c)
            wait(dve, counted, c.n - RING + 1)
            step(dve.tensor_tensor(R(inv, c), R(inv, c), part(real)[:, c.n, :], ALU.mult))
            step(dve.scalar_tensor_tensor(R(n.o[0], c), R(n.z, c), 0.0, wide3(R(inv, c)), ALU.max, ALU.mult))
            dve.nop().then_inc(n.finished, 1)

        def square_scaled(act, c):
            act.wait_ge(n.finished, c.n + 1)
            wait(act, counted, c.n - RING + 1)
            act.activation(R(o2, c), R(n.o[0], c), ACT.Square).then_inc(both, 1)

        def sums(pe, c):
            pe.wait_ge(both, c.n + 1)
            first = isinstance(c.n, int) and c.n == 0
            final = isinstance(c.n, int) and c.n == k.NB - 1
            for a, z in GROUPS:
                for i, src in enumerate((n.o[0], o2)):
                    ins = pe.matmul(p_s[i][0:1, 0 : (z - a) * D], k.ones[:, 0:1], R(src, c)[:, a:z, :].rearrange("p j d -> p (j d)"),
                                    start=first and a == 0, stop=final and z == JN)
            ins.then_inc(counted, 1)

        n.z_free = n.finished
        n.run([k.msg, k.tab[0]], [k.tab[1]], lambda c: [mean[:, c.slot(4)], n.x[1][:, c.slot(UB)]], [wt[:, 0, :], wt[:, 1, :]],
              k.b_skip, [(2, prep), (0, length), (-1, scale)], [(0, square), (-2, square_scaled)], [(0, root)],
              prep=True, pe_stages=[(-2, sums)])
        ready, spread, done, radicand, rooted = [sem(x) for x in ("ready", "spread", "bdone", "bradicand", "brooted")]
        wide_row = sb("wide_row", [1, 2, 4 * D])
        sh = sb("sh", [1, 2 * D])
        with nc.Block() as b:

            @b.gpsimd
            def _(pool):
                pool.wait_ge(radicand, 1)
                pool.tensor_tensor(row[:, 2, :], row[:, 2, :], k.root[0:1, :].to_broadcast([1, D]), ALU.pow).then_inc(rooted, 1)

            @b.vector
            def _(dve):
                step = Chain(dve, done)
                f = lambda i: row[:, i, :]
                for i in range(2):
                    step(dve.tensor_copy(wide_row[:, i, :], p_s[i][0:1, :]))
                    step(dve.tensor_reduce(f(i), wide_row[:, i, :].rearrange("p (r d) -> p d r", d=D), AX.X, ALU.add))
                    step(dve.tensor_scalar(f(i), f(i), 1.0 / k.N, None, ALU.mult))
                step(dve.tensor_tensor(f(2), f(0), f(0), ALU.mult))
                step(dve.tensor_tensor(f(2), f(1), f(2), ALU.subtract))
                step(dve.tensor_scalar(f(2), f(2), 0.0, EPS, ALU.max, ALU.add))
                dve.nop().then_inc(radicand, 1)
                dve.wait_ge(rooted, 1)
                step(dve.tensor_tensor(sh[:, 0:D], f(2), gb[:, 0, :], ALU.mult))
                step(dve.tensor_tensor(f(4), f(0), sh[:, 0:D], ALU.mult))
                step(dve.tensor_tensor(sh[:, D : 2 * D], gb[:, 1, :], f(4), ALU.subtract))
                dve.nop().then_inc(ready, 1)
                dve.wait_ge(spread, 1)
                step(dve.tensor_copy(k.bn[:].rearrange("p s d -> p (s d)"), n.p_m[0][:, 0 : 2 * D]))

            @b.tensor
            def _(pe):
                pe.wait_ge(ready, 1)
                pe.matmul(n.p_m[0][:, 0 : 2 * D], k.ones[0:1, :], sh[:], start=True, stop=True).then_inc(spread, 1)


def batch_norm_nodes(k):
    with ExitStack() as c:
        n = Nodes(k, c, 2, 1, 0, message=0)
        y = n.ring("y", RING)
        norm = Norm(k, c, 0)
        every = lambda i: k.bn[:, i : i + 1, :].to_broadcast([P, JN, D])
        R = lambda t, c: t[:, c.slot(RING)]

        def residual(dve, step, c):
            v, i = R(y, c), c.slot(UB)
            n.wait_loaded(dve, c)
            wait(dve, norm.applied, c.n - RING + 1)
            step(dve.tensor_tensor(v, n.x[0][:, i], every(0), ALU.mult))
            step(dve.tensor_tensor(v, v, every(1), ALU.add))
            step(dve.tensor_tensor(v, v, n.x[1][:, i], ALU.add))
            norm.stats(dve, step, c, v)

        def apply(act, c):
            n.wait_stored(act, c)
            norm.apply(act, c, R(y, c), R(n.o[0], c))

        n.finished = norm.applied
        n.run([k.tab[1], k.tab[0]], [k.res], None, [], None, [(0, residual)], [(-1, apply)], [(0, norm.root)])


def angle_nodes(k):
    nc, A = k.nc, k.a
    with ExitStack() as c:
        sb = lambda n, s, d=F32: c.enter_context(nc.sbuf_tensor(k.name(n), s, d))
        wb = sb("wb", [P, 3, D])
        b_all = sb("b_all", [P, D])
        w_gate, b_gate = sb("w_gate", [P, 1]), sb("b_gate", [P, 1])
        bc = lambda n: A[n].partition_broadcast(P)
        load_rows(k, [(k.w_skip[:], A["L3_gnn_Wskip"]), (k.b_skip[0:1, :], A["L3_gnn_bskip"].unsqueeze(0)),
                      (k.ln_g[:], bc("L3_gnn_ln_gamma")), (k.ln_b[:], bc("L3_gnn_ln_beta")), (b_all[:], bc("L3_gnn_bskip"))]
                  + [(wb[:, i, :], A["L3_gnn_Wbeta"][i * D : (i + 1) * D, :].rearrange("d o -> (d o)").partition_broadcast(P)) for i in range(3)])
        n = Nodes(k, c, 2, 1, 1)
        e, y = n.ring("e", RING), n.ring("y", RING)
        twice = n.ring("twice", RING)
        p_gate = [c.enter_context(nc.psum_tensor(k.name(f"p_gate{i}"), [P, 512], F32)) for i in range(2)]
        gate = sb("gate", [P, RING, 2, JN])
        first, second = [Norm(k, c, i) for i in range(2)]
        begun, gate_in, gate_out, doubled = [k.semaphore(x) for x in ("begun", "gate_in", "gate_out", "doubled")]
        R = lambda t, c: t[:, c.slot(RING)]
        wide_rows = lambda g: g.unsqueeze(2).to_broadcast([P, JN, D])
        weight = lambda i: wb[:, i : i + 1, :].to_broadcast([P, JN, D])
        every = lambda g: g[:].unsqueeze(1).to_broadcast([P, JN, D])

        BEGIN = 6

        def begin(dve):
            step = Chain(dve, begun, BEGIN)
            step(dve.tensor_tensor(wb[:, 0, :], wb[:, 0, :], wb[:, 2, :], ALU.add))
            step(dve.tensor_tensor(wb[:, 1, :], wb[:, 1, :], wb[:, 2, :], ALU.subtract))
            for o, v in ((w_gate, k.w_skip), (b_gate, b_all)):
                step(dve.tensor_tensor(wb[:, 2, :], v[:], wb[:, 1, :], ALU.mult))
                step(dve.tensor_reduce(o[:], wb[:, 2, :], AX.X, ALU.add))

        def gate_row(pe, c, r, turned_row):
            if r == 0:
                wait(pe, begun, BEGIN)
                wait(pe, gate_in, c.n - 1)
            pe.matmul(p_gate[c.slot(2)][:, r : r + 1], turned_row, w_gate[:], start=True, stop=True)

        def logit(dve, step, c):
            m, g = n.x[1][:, c.slot(UB)], R(gate, c)[:, 0, :]
            n.wait_z(dve, c)
            n.wait_message(dve, c)
            wait(dve, second.applied, c.n - RING + 1)
            step(dve.tensor_tensor(R(e, c), m, weight(0), ALU.mult))
            step(dve.tensor_reduce(g, R(e, c), AX.X, ALU.add))
            step(dve.tensor_tensor(g, g, p_gate[c.slot(2)][:, 0:JN], ALU.add))
            step(dve.tensor_scalar(g, g, b_gate[:], -80.0, ALU.add, ALU.max))
            dve.nop().then_inc(gate_in, 1)

        def exponential(act, c):
            act.wait_ge(gate_in, c.n + 1)
            act.activation(R(gate, c)[:, 0, :], R(gate, c)[:, 0, :], ACT.Exp, scale=-1.0).then_inc(gate_out, 1)
            wait(act, n.finished, c.n - RING + 1)
            n.wait_loaded(act, c)
            act.activation(R(twice, c), n.x[0][:, c.slot(UB)], ACT.Copy, scale=2.0).then_inc(doubled, 1)

        def mix(dve, step, c):
            m, z, v, g = n.x[1][:, c.slot(UB)], R(n.z, c), R(y, c), R(gate, c)
            dve.wait_ge(gate_out, c.n + 1)
            step(dve.tensor_scalar(g[:, 0, :], g[:, 0, :], 1.0, None, ALU.add), dve.tensor_tensor(v, z, m, ALU.subtract))
            step(dve.reciprocal(g[:, 1, :], g[:, 0, :]))
            step(dve.tensor_tensor(v, v, wide_rows(g[:, 1, :]), ALU.mult))
            step(dve.tensor_tensor(v, v, m, ALU.add))
            first.stats(dve, step, c, v)

        def residual(dve, step, c):
            v = R(e, c)
            dve.wait_ge(first.applied, c.n + 1)
            step(dve.tensor_tensor(v, v, every(k.ln_g), ALU.mult))
            step(dve.tensor_tensor(v, v, every(k.ln_b), ALU.add))
            dve.wait_ge(doubled, c.n + 1)
            step(dve.scalar_tensor_tensor(v, v, 0.0, R(twice, c), ALU.max, ALU.add))
            second.stats(dve, step, c, v)

        def apply_second(act, c):
            n.wait_stored(act, c)
            second.apply(act, c, R(e, c), R(n.o[0], c))

        n.z_free = first.radicand
        n.finished = second.applied
        n.run([k.res, k.msg], [k.out], lambda c: [n.x[0][:, c.slot(UB)]], [k.w_skip], k.b_skip,
              [(0, logit), (-1, mix), (-2, residual)],
              [(-2, lambda act, c: first.apply(act, c, R(y, c), R(e, c))), (-3, apply_second), (0, exponential)],
              [(-1, first.root), (-2, second.root)], begin=begin, with_row=gate_row)


def build(nc, args, out, n_nodes):
    args["n_nodes"] = n_nodes
    k = Net(nc, args, out)
    k.N = n_nodes
    dram = lambda n, s, d=F32: nc.dram_tensor(n, s, d, kind="Internal").ap()
    k.msg = dram("msg", [k.NR + 1, D])
    k.tab = [dram("tab0", [k.NR, D]), dram("tab1", [k.NR, D])]
    k.res = dram("res", [k.NR, D])
    k.meta = dram("meta", [P, k.NB, FIELDS, J], I32)
    with ExitStack() as c:
        sb = lambda n, s, d=F32: c.enter_context(nc.sbuf_tensor(k.name(n), s, d))
        k.ident, k.ones = sb("ident", [P, P]), sb("ones", [P, P])
        k.dinv, k.rcnt = sb("dinv", [P, k.COLS]), sb("rcnt", [P, k.COLS])
        k.join, k.join_t, k.no_join = sb("join", [P, P]), sb("join_t", [P, P]), sb("no_join", [P, P])
        k.last = sb("last", [P, k.NB, J], I32)
        k.eps = sb("eps", [P, 1])
        k.root = sb("root", [P, 1])
        k.join_row = sb("join_row", [P, 1], I32)
        k.w_skip, k.b_skip = sb("w_skip", [P, D]), sb("b_skip", [1, D])
        k.ln_g, k.ln_b = sb("ln_g", [P, D]), sb("ln_b", [P, D])
        k.w_qk, k.b_qk = sb("w_qk", [P, 2, X2]), sb("b_qk", [3, 2 * X2], BF16)
        k.w_val, k.b_val = sb("w_val", [P, 2, D]), sb("b_val", [4, D])
        k.bn = sb("bn", [P, 2, D])
        k.ones_bf = sb("ones_bf", [3, P], BF16)
        setup(k)
        k.end_phase()
        scale_pass(k)
        k.end_phase()
        sum_edges(k, k.tab[0])
        k.end_phase()
        gcn_nodes(k)
        k.end_phase()
        src, dst = k.tab[1], k.tab[0]
        for l in range(args["L1_gnn_Wq"].shape[0]):
            last = l == args["L1_gnn_Wq"].shape[0] - 1
            fold_conv(k, l)
            k.end_phase()
            conv_edges(k, src)
            k.end_phase()
            conv_nodes(k, src, dst, last)
            k.end_phase()
            src, dst = dst, src
        sum_edges(k, k.tab[0])
        k.end_phase()
        sage_nodes(k)
        k.end_phase()
        batch_norm_nodes(k)
        k.end_phase()
        angle_edges(k, k.res)
        k.end_phase()
        angle_nodes(k)
        k.end_phase()


_ORDER = {"x": "x", "src": "src", "dst": "dst", "edge_attr_128": "edge", "edge_weight1": "weight"}


def kernel(**inputs):
    import concourse.bacc as _bacc
    from concourse.bass_utils import run_bass_kernel_spmd as _run

    nc = _bacc.Bacc("TRN2", target_bir_lowering=False, num_devices=1)
    n = inputs["x"].shape[0]
    nr = padded(n)

    def fill(a, rows_, value):
        return np.concatenate([a, np.full((rows_,) + a.shape[1:], value, a.dtype)])

    arrays, args = {}, {}
    for name, a in inputs.items():
        if name == "L2_gnn_adj_norm_sp":
            continue
        a = np.ascontiguousarray(a)
        if name in ("x", "edge_attr_128", "edge_weight1", "src"):
            a = fill(a, nr - n, 0)
        elif name == "dst":
            a = np.concatenate([np.full((1,), -1, a.dtype), a, np.full((nr - n,), n, a.dtype), np.full((1,), -1, a.dtype)])
        arrays[f"in_{name}"] = a
        args[_ORDER.get(name, name)] = nc.dram_tensor(f"in_{name}", a.shape, mybir.dt.from_np(a.dtype), kind="ExternalInput").ap()
    out = nc.dram_tensor("out_0", (nr, D), F32, kind="ExternalOutput").ap()
    build(nc, args, out, n)
    r = _run(nc, [arrays], core_ids=[0])
    return r.results[0]["out_0"][0:n]
```
